# Optimizing a Trainium2 kernel written in Bass

```python
import numpy as np
import jax
import jax.numpy as jnp

def _softmax(x, axis=-1):
    return jax.nn.softmax(x, axis=axis)

def _gelu(x):
    return jax.nn.gelu(x, approximate=True)

def _silu(x):
    return jax.nn.silu(x)

def _sigmoid(x):
    return jax.nn.sigmoid(x)

def _layernorm(x, axis=-1, eps=1e-05):
    m = jnp.mean(x, axis=axis, keepdims=True)
    v = jnp.var(x, axis=axis, keepdims=True)
    return (x - m) / jnp.sqrt(v + eps)

def _scatter_add(tgt, idx, src, axis=0):
    return tgt.at[idx].add(src)

def _segment_sum(src, seg, n):
    return jax.ops.segment_sum(src, seg, n)
kernel_name = 'mk_macaron_d2_jaxref_r8_167539'

def setup_inputs(seed: int=0):
    np.random.seed(seed)
    _w = jnp.asarray

    def _L0_attn_setup():
        import jax, jax.numpy as jnp
        import numpy as np
        D_MODEL = 128
        NUM_HEADS = 16
        D_HEAD = D_MODEL // NUM_HEADS
        NEG_BIG = 10000000000.0
        key = jax.random.key(seed)
        ks = jax.random.split(key, 9)
        d = D_MODEL
        scale = 1.0 / np.sqrt(d)
        inp = {'x': jax.random.normal(ks[0], (2, 256, d), dtype=jnp.float32), 'W_q': jax.random.normal(ks[1], (d, d), dtype=jnp.float32) * scale, 'b_q': jnp.zeros((d,), dtype=jnp.float32), 'W_k': jax.random.normal(ks[2], (d, d), dtype=jnp.float32) * scale, 'b_k': jnp.zeros((d,), dtype=jnp.float32), 'W_v': jax.random.normal(ks[3], (d, d), dtype=jnp.float32) * scale, 'b_v': jnp.zeros((d,), dtype=jnp.float32), 'W_o': jax.random.normal(ks[4], (d, d), dtype=jnp.float32) * scale, 'b_o': jnp.zeros((d,), dtype=jnp.float32)}
        return inp
    _L0_attn_in = _L0_attn_setup()

    def _L0_ffn_setup():
        import jax, jax.numpy as jnp
        import numpy as np
        B, S, H, NH, E, F = (4, 128, 128, 16, 8, 512)
        D = H // NH
        EPS = 1e-05

        def _layernorm(x, g, b):
            mu = jnp.mean(x, axis=-1, keepdims=True)
            var = jnp.var(x, axis=-1, keepdims=True)
            return (x - mu) * jax.lax.rsqrt(var + EPS) * g + b
        key = jax.random.key(seed)
        ks = jax.random.split(key, 16)
        s = 0.02
        return {'x': jax.random.normal(ks[0], (B, S, H), jnp.float32), 'ln1_g': jnp.ones((H,), jnp.float32), 'ln1_b': jnp.zeros((H,), jnp.float32), 'ln2_g': jnp.ones((H,), jnp.float32), 'ln2_b': jnp.zeros((H,), jnp.float32), 'wq': jax.random.normal(ks[1], (H, H), jnp.float32) * s, 'bq': jnp.zeros((H,), jnp.float32), 'wk': jax.random.normal(ks[2], (H, H), jnp.float32) * s, 'bk': jnp.zeros((H,), jnp.float32), 'wv': jax.random.normal(ks[3], (H, H), jnp.float32) * s, 'bv': jnp.zeros((H,), jnp.float32), 'wo': jax.random.normal(ks[4], (H, H), jnp.float32) * s, 'bo': jnp.zeros((H,), jnp.float32), 'gate_w': jax.random.normal(ks[5], (H, E), jnp.float32) * s, 'gate_b': jnp.zeros((E,), jnp.float32), 'w1': jax.random.normal(ks[6], (E, H, F), jnp.float32) * s, 'b1': jnp.zeros((E, F), jnp.float32), 'w2': jax.random.normal(ks[7], (E, F, H), jnp.float32) * s, 'b2': jnp.zeros((E, H), jnp.float32)}
    _L0_ffn_in = _L0_ffn_setup()

    def _L1_attn_setup():
        import jax, jax.numpy as jnp
        import numpy as np
        B, S, E, H = (2, 256, 128, 16)
        key = jax.random.key(seed)
        k0, k1, k2 = jax.random.split(key, 3)
        x = jax.random.normal(k0, (B, S, E), jnp.float32)
        w_in = jax.random.normal(k1, (3 * E, E), jnp.float32) / np.sqrt(E)
        b_in = jnp.zeros((3 * E,), jnp.float32)
        w_out = jax.random.normal(k2, (E, E), jnp.float32) / np.sqrt(E)
        b_out = jnp.zeros((E,), jnp.float32)
        return {'x': x, 'w_in': w_in, 'b_in': b_in, 'w_out': w_out, 'b_out': b_out}
    _L1_attn_in = _L1_attn_setup()

    def _L1_ffn_setup():
        import jax, jax.numpy as jnp
        import numpy as np
        D_MODEL, D_FF, NUM_EXPERTS, RANK, TOP_K = (128, 512, 8, 16, 2)
        B, S = (8, 256)

        def _expert_ffn(h, wi_w, wo_w, A, Bm):
            inter = jnp.einsum('bsd,fd->bsf', h, wi_w)
            lora = jnp.einsum('bsr,fr->bsf', jnp.einsum('bsd,rd->bsr', h, A), Bm)
            inter = jax.nn.relu(inter + lora)
            return jnp.einsum('bsf,df->bsd', inter, wo_w)
        key = jax.random.key(seed)
        ks = jax.random.split(key, 8)
        hidden_states = jax.random.normal(ks[0], (B, S, D_MODEL), dtype=jnp.float32)
        wi_w = jax.random.normal(ks[1], (D_FF, D_MODEL), dtype=jnp.float32) * (1.0 / np.sqrt(D_MODEL))
        wo_w = jax.random.normal(ks[2], (D_MODEL, D_FF), dtype=jnp.float32) * (1.0 / np.sqrt(D_FF))
        lora_As = jax.random.uniform(ks[3], (NUM_EXPERTS, RANK, D_MODEL), dtype=jnp.float32, minval=-1.0, maxval=1.0) / np.sqrt(D_MODEL)
        lora_Bs = jax.random.normal(ks[4], (NUM_EXPERTS, D_FF, RANK), dtype=jnp.float32) * 0.02
        top_k_indices = jnp.arange(TOP_K, dtype=jnp.int32)
        top_k_values = jax.random.uniform(ks[5], (TOP_K,), dtype=jnp.float32)
        return {'hidden_states': hidden_states, 'wi_w': wi_w, 'wo_w': wo_w, 'lora_As': lora_As, 'lora_Bs': lora_Bs, 'top_k_indices': top_k_indices, 'top_k_values': top_k_values}
    _L1_ffn_in = _L1_ffn_setup()
    _d = {'L0_attn_x': _L0_attn_in['x'], 'L0_attn_W_q': _L0_attn_in['W_q'], 'L0_attn_b_q': _L0_attn_in['b_q'], 'L0_attn_W_k': _L0_attn_in['W_k'], 'L0_attn_b_k': _L0_attn_in['b_k'], 'L0_attn_W_v': _L0_attn_in['W_v'], 'L0_attn_b_v': _L0_attn_in['b_v'], 'L0_attn_W_o': _L0_attn_in['W_o'], 'L0_attn_b_o': _L0_attn_in['b_o'], 'L0_ffn_ln1_g': _L0_ffn_in['ln1_g'], 'L0_ffn_ln1_b': _L0_ffn_in['ln1_b'], 'L0_ffn_ln2_g': _L0_ffn_in['ln2_g'], 'L0_ffn_ln2_b': _L0_ffn_in['ln2_b'], 'L0_ffn_wq': _L0_ffn_in['wq'], 'L0_ffn_bq': _L0_ffn_in['bq'], 'L0_ffn_wk': _L0_ffn_in['wk'], 'L0_ffn_bk': _L0_ffn_in['bk'], 'L0_ffn_wv': _L0_ffn_in['wv'], 'L0_ffn_bv': _L0_ffn_in['bv'], 'L0_ffn_wo': _L0_ffn_in['wo'], 'L0_ffn_bo': _L0_ffn_in['bo'], 'L0_ffn_gate_w': _L0_ffn_in['gate_w'], 'L0_ffn_gate_b': _L0_ffn_in['gate_b'], 'L0_ffn_w1': _L0_ffn_in['w1'], 'L0_ffn_b1': _L0_ffn_in['b1'], 'L0_ffn_w2': _L0_ffn_in['w2'], 'L0_ffn_b2': _L0_ffn_in['b2'], 'L1_attn_w_in': _L1_attn_in['w_in'], 'L1_attn_b_in': _L1_attn_in['b_in'], 'L1_attn_w_out': _L1_attn_in['w_out'], 'L1_attn_b_out': _L1_attn_in['b_out'], 'L1_ffn_wi_w': _L1_ffn_in['wi_w'], 'L1_ffn_wo_w': _L1_ffn_in['wo_w'], 'L1_ffn_lora_As': _L1_ffn_in['lora_As'], 'L1_ffn_lora_Bs': _L1_ffn_in['lora_Bs'], 'L1_ffn_top_k_indices': _L1_ffn_in['top_k_indices'], 'L1_ffn_top_k_values': _L1_ffn_in['top_k_values']}
    _x0 = _d['L0_attn_x']
    _d['L0_attn_x'] = jax.random.normal(jax.random.fold_in(jax.random.key(seed), 1), (4, 512, 128), dtype=_x0.dtype)
    del _x0
    return _d

def reference(L0_attn_x, L0_attn_W_q, L0_attn_b_q, L0_attn_W_k, L0_attn_b_k, L0_attn_W_v, L0_attn_b_v, L0_attn_W_o, L0_attn_b_o, L0_ffn_ln1_g, L0_ffn_ln1_b, L0_ffn_ln2_g, L0_ffn_ln2_b, L0_ffn_wq, L0_ffn_bq, L0_ffn_wk, L0_ffn_bk, L0_ffn_wv, L0_ffn_bv, L0_ffn_wo, L0_ffn_bo, L0_ffn_gate_w, L0_ffn_gate_b, L0_ffn_w1, L0_ffn_b1, L0_ffn_w2, L0_ffn_b2, L1_attn_w_in, L1_attn_b_in, L1_attn_w_out, L1_attn_b_out, L1_ffn_wi_w, L1_ffn_wo_w, L1_ffn_lora_As, L1_ffn_lora_Bs, L1_ffn_top_k_indices, L1_ffn_top_k_values):

    def _L0_attn_ref(x, W_q, b_q, W_k, b_k, W_v, b_v, W_o, b_o):
        import jax, jax.numpy as jnp
        import numpy as np
        D_MODEL = 128
        NUM_HEADS = 16
        D_HEAD = D_MODEL // NUM_HEADS
        NEG_BIG = 10000000000.0
        B, S, d = x.shape
        H, Dh = (NUM_HEADS, D_HEAD)
        Q = x @ W_q + b_q
        K = x @ W_k + b_k
        V = x @ W_v + b_v
        Qh = Q.reshape(B, S, H, Dh).transpose(0, 2, 1, 3)
        Kh = K.reshape(B, S, H, Dh).transpose(0, 2, 1, 3)
        Vh = V.reshape(B, S, H, Dh).transpose(0, 2, 1, 3)
        scores = jnp.einsum('bhid,bhjd->bhij', Qh, Kh) / jnp.sqrt(jnp.asarray(Dh, dtype=x.dtype))
        causal = jnp.tril(jnp.ones((S, S), dtype=x.dtype))
        scores = scores * causal - NEG_BIG * (1.0 - causal)
        attn = jax.nn.softmax(scores, axis=-1)
        vals = jnp.einsum('bhij,bhjd->bhid', attn, Vh)
        vals = vals.transpose(0, 2, 1, 3).reshape(B, S, d)
        return vals @ W_o + b_o

    def _L0_ffn_ref(x, ln1_g, ln1_b, ln2_g, ln2_b, wq, bq, wk, bk, wv, bv, wo, bo, gate_w, gate_b, w1, b1, w2, b2):
        import jax, jax.numpy as jnp
        import numpy as np
        B, S, H, NH, E, F = (4, 128, 128, 16, 8, 512)
        D = H // NH
        EPS = 1e-05

        def _layernorm(x, g, b):
            mu = jnp.mean(x, axis=-1, keepdims=True)
            var = jnp.var(x, axis=-1, keepdims=True)
            return (x - mu) * jax.lax.rsqrt(var + EPS) * g + b
        b, s, h = x.shape
        hn = _layernorm(x, ln1_g, ln1_b)
        q = (hn @ wq + bq).reshape(b, s, NH, D).transpose(0, 2, 1, 3)
        k = (hn @ wk + bk).reshape(b, s, NH, D).transpose(0, 2, 1, 3)
        v = (hn @ wv + bv).reshape(b, s, NH, D).transpose(0, 2, 1, 3)
        scores = jnp.einsum('bhqd,bhkd->bhqk', q, k) / jnp.sqrt(jnp.float32(D))
        attn = jax.nn.softmax(scores, axis=-1)
        o = jnp.einsum('bhqk,bhkd->bhqd', attn, v)
        o = o.transpose(0, 2, 1, 3).reshape(b, s, h)
        x = x + (o @ wo + bo)
        hn2 = _layernorm(x, ln2_g, ln2_b).reshape(-1, h)
        logits = hn2 @ gate_w + gate_b
        idx = jnp.argmax(logits, axis=-1)
        mid = jax.nn.relu(jnp.einsum('th,ehf->etf', hn2, w1) + b1[:, None, :])
        y = jnp.einsum('etf,efh->eth', mid, w2) + b2[:, None, :]
        moe = y[idx, jnp.arange(hn2.shape[0])]
        return x + moe.reshape(b, s, h)

    def _L1_attn_ref(x, w_in, b_in, w_out, b_out):
        import jax, jax.numpy as jnp
        import numpy as np
        B, S, E, H = (2, 256, 128, 16)
        bsz, slen, esz = x.shape
        hsz = esz // H
        qkv = x @ w_in.T + b_in
        q, k, v = jnp.split(qkv, 3, axis=-1)

        def to_heads(t):
            return t.reshape(bsz, slen, H, hsz).transpose(0, 2, 1, 3)
        q, k, v = (to_heads(q), to_heads(k), to_heads(v))
        scale = np.float32(1.0 / np.sqrt(hsz))
        scores = jnp.einsum('bhqd,bhkd->bhqk', q * scale, k)
        causal_bias = jnp.where(jnp.tril(jnp.ones((slen, slen), dtype=bool)), 0.0, -jnp.inf).astype(x.dtype)
        scores = scores + causal_bias
        attn = jax.nn.softmax(scores, axis=-1)
        out = jnp.einsum('bhqk,bhkd->bhqd', attn, v)
        out = out.transpose(0, 2, 1, 3).reshape(bsz, slen, esz)
        out = out @ w_out.T + b_out
        out = jnp.where(jnp.isnan(out), jnp.zeros((), out.dtype), out)
        return out

    def _L1_ffn_ref(hidden_states, wi_w, wo_w, lora_As, lora_Bs, top_k_indices, top_k_values):
        import jax, jax.numpy as jnp
        import numpy as np
        D_MODEL, D_FF, NUM_EXPERTS, RANK, TOP_K = (128, 512, 8, 16, 2)
        B, S = (8, 256)

        def _expert_ffn(h, wi_w, wo_w, A, Bm):
            inter = jnp.einsum('bsd,fd->bsf', h, wi_w)
            lora = jnp.einsum('bsr,fr->bsf', jnp.einsum('bsd,rd->bsr', h, A), Bm)
            inter = jax.nn.relu(inter + lora)
            return jnp.einsum('bsf,df->bsd', inter, wo_w)
        out = jnp.zeros_like(hidden_states)
        for k in range(top_k_values.shape[0]):
            A = jnp.take(lora_As, top_k_indices[k], axis=0)
            Bm = jnp.take(lora_Bs, top_k_indices[k], axis=0)
            out = out + top_k_values[k] * _expert_ffn(hidden_states, wi_w, wo_w, A, Bm)
        return out
    x = L0_attn_x
    x = x + 0.5 * _L0_ffn_ref(_layernorm(x, axis=-1), L0_ffn_ln1_g, L0_ffn_ln1_b, L0_ffn_ln2_g, L0_ffn_ln2_b, L0_ffn_wq, L0_ffn_bq, L0_ffn_wk, L0_ffn_bk, L0_ffn_wv, L0_ffn_bv, L0_ffn_wo, L0_ffn_bo, L0_ffn_gate_w, L0_ffn_gate_b, L0_ffn_w1, L0_ffn_b1, L0_ffn_w2, L0_ffn_b2)
    x = x + _L0_attn_ref(_layernorm(x, axis=-1), L0_attn_W_q, L0_attn_b_q, L0_attn_W_k, L0_attn_b_k, L0_attn_W_v, L0_attn_b_v, L0_attn_W_o, L0_attn_b_o)
    x = x + 0.5 * _L0_ffn_ref(_layernorm(x, axis=-1), L0_ffn_ln1_g, L0_ffn_ln1_b, L0_ffn_ln2_g, L0_ffn_ln2_b, L0_ffn_wq, L0_ffn_bq, L0_ffn_wk, L0_ffn_bk, L0_ffn_wv, L0_ffn_bv, L0_ffn_wo, L0_ffn_bo, L0_ffn_gate_w, L0_ffn_gate_b, L0_ffn_w1, L0_ffn_b1, L0_ffn_w2, L0_ffn_b2)
    x = x + 0.5 * _L1_ffn_ref(_layernorm(x, axis=-1), L1_ffn_wi_w, L1_ffn_wo_w, L1_ffn_lora_As, L1_ffn_lora_Bs, L1_ffn_top_k_indices, L1_ffn_top_k_values)
    x = x + _L1_attn_ref(_layernorm(x, axis=-1), L1_attn_w_in, L1_attn_b_in, L1_attn_w_out, L1_attn_b_out)
    x = x + 0.5 * _L1_ffn_ref(_layernorm(x, axis=-1), L1_ffn_wi_w, L1_ffn_wo_w, L1_ffn_lora_As, L1_ffn_lora_Bs, L1_ffn_top_k_indices, L1_ffn_top_k_values)
    return x

_drawn_inputs = setup_inputs


def setup_inputs(seed=0):
    import zlib

    import numpy as np

    out = dict(_drawn_inputs(seed))
    spreads = {'L0_attn_b_q': (0.0, 0.761),
     'L0_attn_b_k': (0.0, 2.0),
     'L0_attn_b_v': (0.0, 0.1),
     'L0_attn_b_o': (0.0, 0.1),
     'L0_ffn_ln1_g': (1.0, 0.6),
     'L0_ffn_ln1_b': (0.0, 0.8),
     'L0_ffn_ln2_g': (1.0, 0.2),
     'L0_ffn_ln2_b': (0.0, 0.431),
     'L0_ffn_bq': (0.0, 0.8),
     'L0_ffn_bk': (0.0, 2.0),
     'L0_ffn_bv': (0.0, 0.419),
     'L0_ffn_bo': (0.0, 0.1),
     'L0_ffn_gate_b': (0.0, 0.1),
     'L0_ffn_b1': (0.0, 0.445),
     'L0_ffn_b2': (0.0, 0.1),
     'L1_attn_b_in': (0.0, 0.595),
     'L1_attn_b_out': (0.0, 0.604)}
    factors = {'L0_ffn_wq': 8.0,
     'L0_ffn_wk': 8.0,
     'L0_ffn_wv': 7.792,
     'L0_ffn_wo': 2.919,
     'L1_ffn_lora_As': 4.228,
     'L1_ffn_lora_Bs': 4.235,
     'L1_ffn_top_k_values': 8.0}
    for name, (base, spread) in spreads.items():
        noise = np.random.default_rng([zlib.crc32(name.encode()), seed]).standard_normal(out[name].shape)
        drawn = base * np.exp(spread * noise) if base else spread * noise
        out[name] = jnp.asarray(drawn.astype(out[name].dtype))
    for name, factor in factors.items():
        out[name] = (out[name] * factor).astype(out[name].dtype)
    return out
```

```python
from contextlib import ExitStack

import concourse.bass as bass
from concourse import mybir

F32 = mybir.dt.float32
BF16 = mybir.dt.bfloat16
I32 = mybir.dt.int32
ALU = mybir.AluOpType
ACT = mybir.ActivationFunctionType
AX = mybir.AxisListType.X

P = 128
NB, S = 4, 512
TB = S // P
H, DH = 16, 8
E, F = 8, 512
FB = F // P
TOPK = 2
RANK = 16
EPS = 1e-5
SCALE = float(1.0 / DH ** 0.5)
MASKED = -1e30
NPROD = 6
KROWS = NPROD * DH
MROWS = 3
QPART = [0, 0, 0, 1, 1, 2]
KPART = [0, 1, 2, 0, 1, 0]
UNITS = 8
LEAD = 3
STACKED = (2 * 2 * NPROD + 2) * 16
NPT = 8

PLAN = {
    (0, 0): ["stats+"], (0, 3): ["norm+"],
    (1, 0): ["hT+"], (1, 1): ["m1"], (1, 2): ["q+"], (1, 3): ["k+"],
    (2, 0): ["v+"],
    (3, 1): ["m2"], (3, 3): ["o0"],
    (5, 1): ["m3"], (5, 3): ["o1"],
    (7, 1): ["m0+"], (7, 3): ["o2"],
}
LATE = {(2, 1): ["o3-"], (2, 3): ["onT-"], (3, 0): ["out-"]}
PLANS = [PLAN, {at: PLAN.get(at, []) + LATE.get(at, []) for at in set(PLAN) | set(LATE)}]
HEADJOBS = ["stats", "norm", "hT", "q", "k", "v"]
TAIL = ["o3", "onT", "out"]
NOBANK = ("stats", "norm")

PV_AT = [
    {0: [(2, 3)], 1: [(1, 0)], 2: [(1, 1), (1, 2)], 3: [(1, 3)]},
    {1: [(1, 0)], 2: [(1, 1)], 3: [(1, 2)]},
]
PV_LEFT = [(6, 3), (7, 0), (7, 1), (7, 2), (7, 3)]


def bank_jobs():
    order = []
    for par in range(2):
        for u in range(UNITS):
            for k in range(4):
                order += [(par, j) for j in PLANS[par].get((u, k), []) if j.rstrip("+-") not in NOBANK]
    return order + [(1, j) for j in TAIL]


BANK = bank_jobs()
BANKHEAD = ["hT", "q", "k", "v", "m0"]


def program(nc, d):
    with ExitStack() as ctx:
        def sb(name, shape, dt=F32):
            return ctx.enter_context(nc.sbuf_tensor(name, shape, dt))

        def sem(name):
            return ctx.enter_context(nc.semaphore(name))

        ps = ctx.enter_context(nc.psum_tensor("ps", [P, 8, 512], F32))
        SH = 7
        shared = ps[:, SH, :]
        shared_t = shared.rearrange("p (i c) -> p i c", c=P)
        pv_bank = ps[:, 6, :]

        NT = TB * (NB + 1)
        x = sb("x", [P, NT, P])
        res = sb("res", [P, NT, P])
        lnx = sb("lnx", [P, TB, P])
        stats = sb("stats", [P, TB, 6])
        mv = sb("mv", [P, TB, 2])
        rstd = sb("rstd", [P, TB])
        rstd2 = sb("rstd2", [P, TB])
        lntmp = sb("lntmp", [P, TB])
        minus_half = sb("minus_half", [P, TB])
        hT = sb("hT", [P, S])
        q32 = sb("q32", [P, 2, S])
        rem = sb("rem", [P, 2, S])
        parts = sb("parts", [P, 2, 3, S], BF16)
        qs = [sb(f"qs{i}", [P, 2, H // 2, S], BF16) for i in range(2)]
        ks = [sb(f"ks{i}", [P, H // 2, S], BF16) for i in range(2)]
        va = [sb(f"va{i}", [P, TB, H, 32]) for i in range(2)]
        negm = sb("negm", [P, 2, 2, 2, TB])
        mrem = sb("mrem", [P, 2, 2, TB])
        mpart = sb("mpart", [P, 2, 3, 2 * TB], BF16)
        mrow = sb("mrow", [2 * 3 * 2 * TB, P], BF16)
        pt = sb("pt", [P, NPT, 1024])
        ot = sb("ot", [P, S])
        rc = sb("rc", [P, TB, 4])
        on = sb("on", [P, TB, P])
        onT = sb("onT", [P, S])
        upd = sb("upd", [P, TB, P])
        upd2 = sb("upd2", [P, TB, P])
        identf = sb("identf", [P, P])
        identb = sb("identb", [P, P], BF16)
        mask_q = sb("mask_q", [P, P], BF16)
        mask_k = sb("mask_k", [P, P], BF16)
        ones_col = sb("ones_col", [P, 1])
        zero_col = sb("zero_col", [P, 1])
        wraw = sb("wraw", [P, 12, P])
        wT = sb("wT", [P, 4, P])
        wperm = sb("wperm", [P, 6, P])
        bcol = sb("bcol", [P, 6])
        bcols = sb("bcols", [P, 6])
        bvb = sb("bvb", [P, 3, P])
        bob = sb("bob", [P, 3, P])
        gcol = sb("gcol", [P, 4])
        w1 = sb("w1", [P, E, F])
        w2 = sb("w2", [P, E, FB, P])
        b1c = sb("b1c", [P, E, FB])
        b2r = sb("b2r", [E, P])
        gw = sb("gw", [P, E])
        gbb = sb("gbb", [P, E])
        logit = sb("logit", [P, TB, E])
        lmax = sb("lmax", [P, TB])
        pref_i = sb("pref_i", [P, TB, E], I32)
        pref = sb("pref", [P, TB, E])
        score = sb("score", [P, TB, E])
        smax = sb("smax", [P, TB])
        oneh = sb("oneh", [P, TB, E])
        mzero = sb("mzero", [MROWS, S], BF16)
        pick = sb("pick", [E, E, P], BF16)
        ohs = sb("ohs", [E, S])
        relu = pt[:, 0, :].rearrange("p (a c) -> p a c", a=2)
        fold = pt[:, 1, :].rearrange("p (a c) -> p a c", a=2)
        mid = pt[:, 2:4, :].rearrange("p a (b c) -> p (a b) c", b=2)
        hTa = pt[:, 4:6, :].rearrange("p a (b c) -> p (a b) c", b=2)
        ohT = pt[0:E, 6:8, :].rearrange("p a (b c) -> p (a b) c", b=2)
        ohTb = pt[0:E, 1, :].bitcast(BF16).rearrange("p (a c) -> p a c", a=NB)
        wi_raw = pt[:, 4, 0:F].rearrange("p (a c) -> p a c", c=P)
        wo_raw = pt[:, 4, F:2 * F]
        loA = pt[0:RANK, 5, 0:TOPK * P].rearrange("p (a c) -> p a c", a=TOPK)
        loB = pt[:, 5, F:F + TOPK * FB * RANK].rearrange("p (a b c) -> p a b c", a=TOPK, b=FB)
        loBT = pt[0:RANK, 6, :].rearrange("p (a c) -> p a c", a=TOPK)
        wiT = pt[:, 7, 0:F]
        wk = sb("wk", [P, TOPK, F])
        wo2 = sb("wo2", [P, FB, P])
        idx = sb("idx", [1, TOPK], I32)
        tkv = sb("tkv", [P, TOPK])

        x_loaded = sem("x_loaded")
        w_loaded = sem("w_loaded")
        idx_loaded = sem("idx_loaded")
        lora_loaded = sem("lora_loaded")
        const_done = sem("const_done")
        set_dve = sem("set_dve")
        set_pe = sem("set_pe")
        set_free = sem("set_free")
        ln_stat = sem("ln_stat")
        ln_rstd = sem("ln_rstd")
        ln_x = sem("ln_x")
        h_kept = sem("h_kept")
        bank_full = sem("bank_full")
        bank_free = sem("bank_free")
        hi_done = sem("hi_done")
        split_done = sem("split_done")
        qk_loaded = sem("qk_loaded")
        p1_ready = sem("p1_ready")
        max_done = sem("max_done")
        m_parts = sem("m_parts")
        m_loaded = sem("m_loaded")
        p2_ready = sem("p2_ready")
        exp_done = sem("exp_done")
        pv_done = sem("pv_done")
        ot_ready = sem("ot_ready")
        rc_done = sem("rc_done")
        guard_done = sem("guard_done")
        x_done = sem("x_done")
        up_ready = sem("up_ready")
        relu_done = sem("relu_done")
        fold_done = sem("fold_done")
        mask_ready = sem("mask_ready")
        mid_done = sem("mid_done")
        down_done = sem("down_done")
        y_free = sem("y_free")
        half_done = sem("half_done")
        route = sem("route")
        hta_done = sem("hta_done")
        ohT_done = sem("ohT_done")
        ohs_done = sem("ohs_done")
        out_done = sem("out_done")
        stood_apart = sem("stood_apart")

        W = [
            dict(wq=wperm[:, 0, :], wk=wperm[:, 1, :], wv=wraw[:, 2, :], wo=wraw[:, 3, :], n=0,
                 g=gcol[:, 0:1], b=gcol[:, 1:2], causal=False, moe=True, nan_guard=False),
            dict(wq=wperm[:, 2, :], wk=wperm[:, 3, :], wv=wraw[:, 6, :], wo=wraw[:, 7, :], n=1,
                 g=ones_col[:, :], b=zero_col[:, :], causal=True, moe=False, nan_guard=False),
            dict(wq=wperm[:, 4, :], wk=wperm[:, 5, :], wv=wT[:, 2, :], wo=wT[:, 3, :], n=2,
                 g=ones_col[:, :], b=zero_col[:, :], causal=True, moe=False, nan_guard=True),
        ]
        ORDER = [("attn", 0), ("moe", None), ("attn", 1), ("attn", 0), ("moe", None), ("ffn", None),
                 ("attn", 2), ("ffn", None)]
        ATTN_LN, ATTN_BANK = NB + 1, len(BANKHEAD) + NB // 2 * len(BANK)
        ATTN_HALVES, ATTN_QUADS = NB * UNITS + LEAD, NB * 4 + 1

        SETUP_BANK = 3 + 2 * TOPK

        ONE = 1
        credited = [pv_done, exp_done, ot_ready, y_free, mid_done, down_done, relu_done, fold_done, hta_done]

        phases = []
        c = dict(ln=0, bank=SETUP_BANK, half=0, quad=0, attn=0, moe=0, xd=0, prep=0, up=0, mid=ONE, relu=ONE, pick=0,
                 y=ONE, fold=ONE, kept=0)
        for kind, w in ORDER:
            phases.append((kind, w, dict(c)))
            if kind == "attn":
                c["ln"] += ATTN_LN
                c["bank"] += ATTN_BANK
                c["half"] += ATTN_HALVES
                c["quad"] += ATTN_QUADS
                c["prep"] += NB + 1
                c["attn"] += 1
                c["kept"] += (NB + 1) * TB if W[w]["moe"] else 0
            elif kind == "moe":
                c["ln"] += NB
                c["bank"] += 3 * NB
                c["moe"] += 1
                c["up"] += NB * E * FB
                c["relu"] += NB * E * FB
                c["mid"] += NB * E * FB
                c["pick"] += NB * E
                c["y"] += NB
            else:
                c["ln"] += NB
                c["bank"] += NB
                c["fold"] += NB * FB
                c["up"] += NB * FB * TOPK
                c["relu"] += NB * FB
                c["mid"] += NB * FB
                c["y"] += NB
            c["xd"] += NB
        def tiles(t, b):
            return t[:, bass.ds(b * TB, TB), :] if not isinstance(b, int) else t[:, b * TB:(b + 1) * TB, :]

        def tile(t, b, j):
            return t[:, b * TB + j, :]

        def wait(eng, s, n):
            if not isinstance(n, int) or n > 0:
                eng.wait_ge(s, n)

        def apart(eng, s, n):
            wait(eng, s, n)
            if not isinstance(n, int):
                eng.sem_inc(stood_apart, 1)

        block = ctx.enter_context(nc.Block())

        def ln_stats(v, b, n, src, x_ready):
            if x_ready is not None:
                v.wait_ge(x_done, x_ready)
            wait(v, ln_x, n)
            for j in range(TB):
                v.bn_stats(stats[:, j, :], tile(src, b, j)).then_inc(ln_stat, 1)
            apart(v, ln_stat, n * 8 + 4)
            for j in range(TB):
                v.bn_aggr(mv[:, j, :], stats[:, j, :]).then_inc(ln_stat, 1)

        def ln_pool(g, n, twice):
            def step(i):
                return n * 7 + i
            apart(g, ln_stat, n * 8 + 8)
            apart(g, ln_x, n)
            g.tensor_scalar(lntmp[:, :], mv[:, :, 1], EPS, None, ALU.add).then_inc(ln_rstd, 1)
            apart(g, ln_rstd, step(1))
            g.tensor_tensor(rstd[:, :], lntmp[:, :], minus_half[:, :], ALU.pow).then_inc(ln_rstd, 1)
            apart(g, ln_rstd, step(2))
            if not twice:
                g.tensor_copy(rstd2[:, :], rstd[:, :]).then_inc(ln_rstd, 5)
                return
            g.tensor_tensor(lntmp[:, :], rstd[:, :], rstd[:, :], ALU.mult).then_inc(ln_rstd, 1)
            apart(g, ln_rstd, step(3))
            g.tensor_tensor(lntmp[:, :], lntmp[:, :], mv[:, :, 1], ALU.mult).then_inc(ln_rstd, 1)
            apart(g, ln_rstd, step(4))
            g.tensor_scalar(lntmp[:, :], lntmp[:, :], EPS, None, ALU.add).then_inc(ln_rstd, 1)
            apart(g, ln_rstd, step(5))
            g.tensor_tensor(lntmp[:, :], lntmp[:, :], minus_half[:, :], ALU.pow).then_inc(ln_rstd, 1)
            apart(g, ln_rstd, step(6))
            g.tensor_tensor(rstd2[:, :], lntmp[:, :], rstd[:, :], ALU.mult).then_inc(ln_rstd, 1)

        def ln_norm(v, b, n, bank_n, src, keep):
            v.wait_ge(ln_rstd, n * 7 + 7)
            if bank_n is not None:
                wait(v, bank_full, bank_n)
            if keep:
                for j in range(TB):
                    v.tensor_scalar(tile(res, b, j), tile(src, b, j), mv[:, j, 0:1], rstd[:, j:j + 1],
                                    ALU.subtract, ALU.mult).then_inc(h_kept, 1)
            for j in range(TB):
                ins = v.tensor_scalar(lnx[:, j, :], tile(src, b, j), mv[:, j, 0:1], rstd2[:, j:j + 1],
                                      ALU.subtract, ALU.mult)
            ins.then_inc(ln_x, 1)

        def transpose_ln(pe, n, bank_n):
            pe.wait_ge(ln_x, n + 1)
            wait(pe, bank_free, bank_n)
            for j in range(TB):
                ins = pe.transpose(shared_t[:, j, :], lnx[:, j, :], identf[:, :])
            ins.then_inc(bank_full, 1)

        def numbers(cnt, b, par):
            return dict(b=b, par=par, ln=b + cnt["ln"], half=b * UNITS + cnt["half"], quad=b * 4 + cnt["quad"],
                        unit=b * UNITS + cnt["attn"] * NB * UNITS, prep=b + cnt["prep"],
                        x_ready=b + (cnt["xd"] - NB + 1) if cnt["xd"] else None, ot=b * 4 + (cnt["attn"] * NB * 4 + ONE),
                        kept=b * TB + cnt["kept"],
                        xd=b + cnt["xd"])

        def bank_number(cnt, pair, par, job):
            return pair * len(BANK) + (cnt["bank"] + len(BANKHEAD) + BANK.index((par, job)))

        def pass1_tile(pe, w, N, g, hf, r):
            s, i = r // TB, r % TB
            n = (N["half"] + 2 * g + hf) * 8 + r
            t = 2 * g + hf
            q, k = qs[N["par"]], ks[N["par"]]
            width = (i + 1) * P if w["causal"] else S
            wait(pe, max_done, n - 1)
            ins = pe.matmul(ps[:, r % 2, 0:width], q[:, s, t, i * P:(i + 1) * P], k[:, t, 0:width], start=True,
                            stop=not w["causal"])
            if w["causal"]:
                ins = pe.matmul(ps[:, r % 2, i * P:width], identb[:, :], mask_q[:, :], start=False, stop=True)
            ins.then_inc(p1_ready, 1)

        def rowmax_tile(v, w, N, g, hf, r):
            s, i = r // TB, r % TB
            n = (N["half"] + 2 * g + hf) * 8 + r
            width = (i + 1) * P if w["causal"] else S
            v.wait_ge(p1_ready, n + 1)
            v.tensor_reduce(negm[:, g % 2, s, hf, i:i + 1], ps[:, r % 2, 0:width], AX, ALU.max,
                            negate=True).then_inc(max_done, 1)

        def split_max(g_, N, g, bank_n):
            n = (N["quad"] + g) * 4
            apart(g_, max_done, (N["half"] + 2 * g + 2) * 8)
            apart(g_, m_parts, n)
            src = negm[:, g % 2].rearrange("p s t i -> p s (t i)")
            rem_ = mrem[:, :, :, :].rearrange("p s t i -> p s (t i)")
            g_.tensor_copy(mpart[:, :, 0, :], src).then_inc(m_parts, 1)
            apart(g_, m_parts, n + 1)
            g_.tensor_tensor(rem_, src, mpart[:, :, 0, :], ALU.subtract).then_inc(m_parts, 1)
            apart(g_, m_parts, n + 2)
            g_.tensor_copy(mpart[:, :, 1, :], rem_).then_inc(m_parts, 1)
            apart(g_, m_parts, n + 3)
            g_.tensor_tensor(mpart[:, :, 2, :], rem_, mpart[:, :, 1, :], ALU.subtract).then_inc(m_parts, 1)

        def store_max(g_, N, g, bank_n):
            apart(g_, bank_free, bank_n + 1)
            for s in range(2):
                g_.dma_start(qs[N["par"]][64 * s + KROWS:64 * s + KROWS + MROWS, s, 2 * g:2 * g + 2, :],
                             mrow[24 * s:24 * s + 24, :]).then_inc(m_loaded, 16)

        def slot_cols(w, hf, kb):
            q0 = kb * P if w["causal"] else 0
            if w["causal"]:
                at = {0: 0, 1: S, 2: 0, 3: S - 2 * P}[kb]
            else:
                at = (kb % 2) * S
            return at, at + S - q0, q0

        def slot_width(w, hf):
            return slot_cols(w, hf, 2 * hf + 1)[1]

        def pass2_slot(pe, w, N, u, k):
            g, hf = u // 2, u % 2
            t, s = 2 * g + k // 2, k % 2
            n = (N["unit"] + u) * 4 + k
            q, kk = qs[N["par"]], ks[N["par"]]
            flat = ps[:, 2 + 2 * (k % 2):4 + 2 * (k % 2), :].rearrange("p a c -> p (a c)")
            if k == 0 and hf == 0:
                pe.wait_ge(m_loaded, (N["quad"] + g + 1) * 32)
            wait(pe, exp_done, (n - 1 if u or k else n) + ONE)
            for kb in (2 * hf, 2 * hf + 1):
                a, z, q0 = slot_cols(w, hf, kb)
                ins = pe.matmul(flat[:, a:z], kk[:, t, kb * P:(kb + 1) * P], q[:, s, t, q0:S],
                                start=True, stop=not w["causal"])
                if w["causal"]:
                    ins = pe.matmul(flat[:, a:a + P], identb[:, :], mask_k[:, :], start=False, stop=True)
            ins.then_inc(p2_ready, 1)

        def exp_slot(a, w, N, u, k):
            n = (N["unit"] + u) * 4 + k
            flat = ps[:, 2 + 2 * (k % 2):4 + 2 * (k % 2), :].rearrange("p a c -> p (a c)")
            width = slot_width(w, u % 2)
            a.wait_ge(p2_ready, n + 1)
            if k == 0:
                wait(a, pv_done, N["unit"] + (u - 1 if u or N["par"] else 0) + ONE)
            a.activation(pt[:, (u % 2) * 4 + k, 0:width], flat[:, 0:width], ACT.Exp).then_inc(exp_done, 1)

        def pv_piece(pe, w, N, u, piece):
            g, hf = u // 2, u % 2
            kb, half = 2 * hf + piece // 2, piece % 2
            a, _, q0 = slot_cols(w, hf, kb)
            if piece == 0:
                pe.wait_ge(exp_done, (N["unit"] + u + 1) * 4 + ONE)
                if hf == 0:
                    wait(pe, ot_ready, N["ot"] + g)
            lo, hi = max(half * S // 2, q0), (half + 1) * S // 2
            if lo >= hi:
                return
            for j in range(4):
                ins = pe.matmul(pv_bank[32 * j:32 * j + 32, lo:hi], va[N["par"]][:, kb, 4 * g + j, :],
                                pt[:, hf * 4 + j, a + lo - q0:a + hi - q0], start=(kb == 0 and half == 0),
                                stop=(kb == TB - 1), skip_group_check=True)
            if piece == 3:
                ins.then_inc(pv_done, 1)

        def pe_job(pe, w, cnt, N, job, bn):
            if job == "hT":
                transpose_ln(pe, N["ln"], bn)
            elif job in ("q", "k"):
                wait(pe, bank_free, bn)
                pe.matmul(shared, w["wq" if job == "q" else "wk"], hT[:, :], start=True, stop=True).then_inc(bank_full, 1)
            elif job == "v":
                wait(pe, bank_free, bn)
                for i in range(TB):
                    ins = pe.matmul(shared_t[:, i, :], hT[:, i * P:(i + 1) * P], w["wv"], start=True, stop=True)
                ins.then_inc(bank_full, 1)
            elif job[0] == "m":
                g = int(job[1])
                pe.wait_ge(m_parts, (N["quad"] + g) * 4 + 4)
                apart(pe, bank_free, bn)
                pe.transpose(shared[0:48, 0:P // 2].bitcast(BF16), mpart[:, :, :, :].rearrange("p s r c -> p (s r c)"),
                             identb[:, :]).then_inc(bank_full, 1)
            elif job in ("o0", "o1", "o2", "o3"):
                pe.wait_ge(ot_ready, N["ot"] + int(job[1]) + 1)
                wait(pe, bank_free, bn)
                for i in range(TB):
                    ins = pe.transpose(shared_t[:, i, :], ot[:, i * P:(i + 1) * P], identf[:, :])
                ins.then_inc(bank_full, 1)
            elif job == "onT":
                wait(pe, bank_free, bn)
                for i in range(TB):
                    ins = pe.transpose(shared_t[:, i, :], on[:, i, :], identf[:, :])
                ins.then_inc(bank_full, 1)
            elif job == "out":
                wait(pe, bank_free, bn)
                for i in range(TB):
                    ins = pe.matmul(shared_t[:, i, :], onT[:, i * P:(i + 1) * P], w["wo"], start=True, stop=True)
                ins.then_inc(bank_full, 1)

        def act_job(a, w, cnt, N, job, bn):
            if job == "hT":
                a.wait_ge(bank_full, bn + 1)
                a.activation(hT[:, :], shared, ACT.Identity, bias=w["b"], scale=w["g"]).then_inc(bank_free, 1)
            elif job in ("q", "k"):
                c_ = 0 if job == "q" else 1
                col = 2 * w["n"] + c_
                a.wait_ge(bank_full, bn + 1)
                wait(a, split_done, (N["prep"] - 1) * 6 + 3 * c_ + 3)
                a.activation(q32[:, c_, :], shared, ACT.Identity, bias=bcols[:, col:col + 1],
                             scale=SCALE if job == "q" else 1.0).then_inc(bank_free, 1)
                a.wait_ge(bank_free, bn + 1)
                wait(a, qk_loaded, N["prep"] * STACKED)
                a.activation(parts[:, c_, 0, :], q32[:, c_, :], ACT.Copy).then_inc(hi_done, 1)
            elif job[0] == "m":
                a.wait_ge(bank_full, bn + 1)
                wait(a, m_loaded, (N["quad"] + int(job[1])) * 32)
                a.activation(mrow[:, :], shared[0:48, 0:P // 2].bitcast(BF16), ACT.Copy).then_inc(bank_free, 1)
            elif job == "onT":
                a.wait_ge(bank_full, bn + 1)
                a.activation(onT[:, :], shared, ACT.Copy).then_inc(bank_free, 1)

        def ot_copy(a, N, u):
            g = u // 2
            a.wait_ge(pv_done, N["unit"] + u + 1 + ONE)
            a.activation(ot[:, :], pv_bank, ACT.Copy).then_inc(ot_ready, 1)

        def dve_job(v, w, cnt, N, job, bn):
            if job == "stats":
                ln_stats(v, N["b"], N["ln"], x, N["x_ready"])
            elif job == "norm":
                ln_norm(v, N["b"], N["ln"], None, x, w["moe"])
            elif job == "v":
                v.wait_ge(bank_full, bn + 1)
                v.tensor_tensor(va[N["par"]][:, :, :, 0:DH],
                                shared_t.rearrange("p i (h e) -> p i h e", e=DH),
                                bvb[:, w["n"]:w["n"] + 1, :].rearrange("p o (h e) -> p o h e", e=DH)
                                .broadcast_to([P, TB, H, DH]), ALU.add).then_inc(bank_free, 1)
            elif job in ("o0", "o1", "o2", "o3"):
                g = int(job[1])
                v.wait_ge(bank_full, bn + 1)
                o4 = shared_t.rearrange("p i (j e) -> p i j e", e=32)
                v.reciprocal(rc[:, :, :], o4[:, :, :, DH]).then_inc(rc_done, 1)
                v.wait_ge(rc_done, N["ot"] - ONE + g + 1)
                v.tensor_tensor(on[:, :, 32 * g:32 * g + 32].rearrange("p i (j e) -> p i j e", e=DH),
                                o4[:, :, :, 0:DH],
                                rc[:, :, :].rearrange("p i (j o) -> p i j o", o=1).broadcast_to([P, TB, 4, DH]),
                                ALU.mult).then_inc(bank_free, 1)
            elif job == "out":
                bo = bob[:, w["n"]:w["n"] + 1, :].broadcast_to([P, TB, P])
                dst = tiles(res if w["moe"] else x, N["b"])
                v.wait_ge(bank_full, bn + 1)
                v.tensor_tensor(upd[:, :, :], shared_t, bo, ALU.add).then_inc(bank_free, 1)
                v.wait_ge(bank_free, bn + 1)
                if w["moe"]:
                    v.wait_ge(h_kept, N["kept"] + TB)
                if w["nan_guard"]:
                    v.tensor_scalar(upd2[:, :, :], upd[:, :, :], 0.0, None, ALU.max).then_inc(guard_done, 1)
                    v.wait_ge(guard_done, N["b"] * 2 + 1)
                    v.scalar_tensor_tensor(upd[:, :, :], upd[:, :, :], 0.0, upd2[:, :, :], ALU.min,
                                           ALU.add).then_inc(guard_done, 1)
                    v.wait_ge(guard_done, N["b"] * 2 + 2)
                v.tensor_tensor(dst, dst, upd[:, :, :], ALU.add).then_inc(x_done, 1)
                v.wait_ge(x_done, N["xd"] + 1)

        def pool_job(g_, w, cnt, N, job, bn):
            if job == "norm":
                ln_pool(g_, N["ln"], w["moe"])
            elif job in ("q", "k"):
                c_ = 0 if job == "q" else 1
                n = N["prep"] * 6 + 3 * c_
                apart(g_, hi_done, N["prep"] * 2 + c_ + 1)
                g_.tensor_tensor(rem[:, c_, :], q32[:, c_, :], parts[:, c_, 0, :], ALU.subtract).then_inc(split_done, 1)
                apart(g_, split_done, n + 1)
                g_.tensor_copy(parts[:, c_, 1, :], rem[:, c_, :]).then_inc(split_done, 1)
                apart(g_, split_done, n + 2)
                g_.tensor_tensor(parts[:, c_, 2, :], rem[:, c_, :], parts[:, c_, 1, :],
                                 ALU.subtract).then_inc(split_done, 1)
            elif job[0] == "m":
                split_max(g_, N, int(job[1]), bn)
                store_max(g_, N, int(job[1]), bn)

        def walk(eng, w, cnt, pair, par, scores, job_fn, unit_end=None):
            b = pair * 2 + par
            N, after = numbers(cnt, b, par), numbers(cnt, b + 1, 1 - par)
            before = numbers(cnt, pair * 2, 0) if par else None
            for u in range(UNITS):
                for k in range(4):
                    if scores:
                        scores(before, N, after, u, k)
                    for job in PLANS[par].get((u, k), []):
                        name = job.rstrip("+-")
                        at = "hT+" if name in NOBANK else job
                        job_fn(eng, w, cnt, {"+": after, "-": before}.get(job[-1], N), name,
                               bank_number(cnt, pair, par, at))
                if unit_end:
                    unit_end(before, N, u)
            return N

        def head(eng, w, cnt, job_fn):
            N = numbers(cnt, 0, 0)
            for name in HEADJOBS:
                at = "hT" if name in NOBANK else name
                job_fn(eng, w, cnt, N, name, cnt["bank"] + BANKHEAD.index(at))
            return N

        def lead_of(N, M, u):
            h = u + LEAD
            return (N, h // 2, h % 2) if h < UNITS else (M, (h - UNITS) // 2, h % 2)

        def attention_pe(pe, w, cnt):
            wait(pe, y_free, cnt["y"])
            N0 = head(pe, w, cnt, pe_job)
            pe.wait_ge(qk_loaded, (N0["prep"] + 1) * STACKED)
            for h in range(LEAD):
                for r in range(8):
                    if (h, r) == (2, 6):
                        pe_job(pe, w, cnt, N0, "m0", cnt["bank"] + BANKHEAD.index("m0"))
                    pass1_tile(pe, w, N0, h // 2, h % 2, r)

            def scores(before, N, after, u, k):
                L, g, hf = lead_of(N, after, u)
                if k == 0 and hf == 0 and g == 0:
                    pe.wait_ge(qk_loaded, (L["prep"] + 1) * STACKED)
                pass1_tile(pe, w, L, g, hf, 2 * k)
                pass2_slot(pe, w, N, u, k)
                pass1_tile(pe, w, L, g, hf, 2 * k + 1)
                for back, piece in PV_AT[u % 2].get(k, []):
                    if u >= back:
                        pv_piece(pe, w, N, u - back, piece)
                    elif before:
                        pv_piece(pe, w, before, u - back + UNITS, piece)

            with pe.Fori(0, NB // 2) as pair:
                for par in range(2):
                    N = walk(pe, w, cnt, pair, par, scores, pe_job)
                for u, piece in PV_LEFT:
                    pv_piece(pe, w, N, u, piece)
                for job in TAIL:
                    pe_job(pe, w, cnt, N, job, bank_number(cnt, pair, 1, job))

        def attention_dve(v, w, cnt):
            N0 = head(v, w, cnt, dve_job)
            wait(v, m_parts, N0["quad"] * 4)
            for h in range(LEAD):
                for r in range(8):
                    rowmax_tile(v, w, N0, h // 2, h % 2, r)

            def scores(before, N, after, u, k):
                L, g, hf = lead_of(N, after, u)
                for r in (2 * k, 2 * k + 1):
                    if k == 0 and r == 0 and hf == 0:
                        wait(v, m_parts, (L["quad"] + g - 1) * 4)
                    rowmax_tile(v, w, L, g, hf, r)

            with v.Fori(0, NB // 2) as pair:
                for par in range(2):
                    N = walk(v, w, cnt, pair, par, scores, dve_job)
                for job in TAIL:
                    dve_job(v, w, cnt, N, job, bank_number(cnt, pair, 1, job))

        def attention_act(a, w, cnt):
            N0 = head(a, w, cnt, act_job)
            act_job(a, w, cnt, N0, "m0", cnt["bank"] + BANKHEAD.index("m0"))

            def scores(before, N, after, u, k):
                exp_slot(a, w, N, u, k)

            def unit_end(before, N, u):
                if u % 2 == 0 and u > 0:
                    ot_copy(a, N, u - 1)
                elif u == 0 and before:
                    ot_copy(a, before, UNITS - 1)

            with a.Fori(0, NB // 2) as pair:
                for par in range(2):
                    N = walk(a, w, cnt, pair, par, scores, act_job, unit_end)
                ot_copy(a, N, UNITS - 1)
                for job in TAIL:
                    act_job(a, w, cnt, N, job, bank_number(cnt, pair, 1, job))

        def attention_pool(g_, w, cnt):
            N0 = head(g_, w, cnt, pool_job)
            pool_job(g_, w, cnt, N0, "m0", cnt["bank"] + BANKHEAD.index("m0"))
            with g_.Fori(0, NB // 2) as pair:
                for par in range(2):
                    walk(g_, w, cnt, pair, par, None, pool_job)

        def stack(sp, N, par, quads):
            wait(sp, m_loaded, quads * 32)
            for c_, which in ((0, QPART), (1, KPART)):
                sp.wait_ge(split_done, N * 6 + 3 * c_ + 3)
                for s in range(2):
                    if c_ == 0:
                        sp.dma_start(qs[par][64 * s + KROWS:64 * s + KROWS + MROWS, s, :, :],
                                     mzero[:, :].rearrange("p (o c) -> p o c", o=1)
                                     .broadcast_to([MROWS, UNITS, S])).then_inc(qk_loaded, 16)
                    for p_ in range(NPROD):
                        r0 = 64 * s + DH * p_
                        dst = qs[par][r0:r0 + DH, s] if c_ == 0 else ks[par][r0:r0 + DH]
                        sp.dma_start(dst, parts[64 * s:64 * s + 64, c_, which[p_], :]).then_inc(qk_loaded, 16)

        def attention_sync(sp, cnt):
            stack(sp, cnt["prep"], 0, cnt["quad"])
            with sp.Fori(0, NB // 2) as i:
                for par in range(2):
                    stack(sp, i * 2 + par + 1 + cnt["prep"], 1 - par, (i * 2 + par) * 4 + max(cnt["quad"], 1))

        def moe_pe(pe, cnt):
            def one_batch(b):
                bn = b * 3 + cnt["bank"]
                transpose_ln(pe, b + cnt["ln"], bn)
                pe.wait_ge(bank_free, bn + 1)
                for i in range(TB):
                    ins = pe.matmul(shared_t[:, i, 0:E], hT[:, i * P:(i + 1) * P], gw[:, :], start=True, stop=True)
                ins.then_inc(bank_full, 1)
                pe.wait_ge(route, (b + cnt["moe"] * NB) * 6 + 6)
                for i in range(TB):
                    ins = pe.transpose(shared_t[0:E, i, :], oneh[:, i, :], identf[:, :])
                ins.then_inc(bank_full, 1)

            with pe.Fori(0, NB) as b:
                one_batch(b)
            pe.wait_ge(max_done, (cnt["half"]) * 8)
            pe.wait_ge(bank_free, cnt["bank"] + 3 * NB)
            pe.wait_ge(hta_done, (cnt["moe"] + 1) * NB + ONE)
            with pe.Fori(0, NB) as b:
                n0 = b * (E * FB) + cnt["up"]
                m0 = b * (E * FB) + cnt["mid"]
                pe.wait_ge(ohs_done, b + (cnt["moe"] * NB + 1))
                wait(pe, y_free, b + cnt["y"])
                for i in range(TB):
                    pe.matmul(ps[:, 6, i * P:(i + 1) * P], ohs[:, i * P:(i + 1) * P], b2r[:, :],
                              start=(i == 0), stop=False, skip_group_check=True)

                def down(n):
                    e, fb = n // FB, n % FB
                    pe.wait_ge(mid_done, m0 + n + 1)
                    for i in range(TB):
                        ins = pe.matmul(ps[:, 6, i * P:(i + 1) * P], mid[:, n % 4, i * P:(i + 1) * P],
                                        w2[:, e, fb, :], start=False, stop=(n == E * FB - 1), skip_group_check=True)
                    ins.then_inc(down_done, 1)

                for n in range(E * FB):
                    e, fb = n // FB, n % FB
                    if fb == 0:
                        apart(pe, mid_done, m0 + max(n - FB, 0))
                        pe.matmul(ps[:, 4 + e % 2, :], pick[:, e, :], ohTb[:, b, :], start=True,
                                  stop=True).then_inc(mask_ready, 1)
                    if n >= 4:
                        pe.wait_ge(relu_done, b * (E * FB) + (cnt["relu"] + n - 3))
                    pe.matmul(ps[:, n % 4, :], w1[:, e, fb * P:(fb + 1) * P], hTa[:, b, :], start=True,
                              stop=True).then_inc(up_ready, 1)
                    if n >= 2:
                        down(n - 2)
                down(E * FB - 2)
                down(E * FB - 1)

        def moe_act(a, cnt):
            with a.Fori(0, NB) as b:
                bn = b * 3 + cnt["bank"]
                a.wait_ge(bank_full, bn + 1)
                wait(a, hta_done, b + (cnt["moe"] * NB + ONE))
                a.activation(hT[:, :], shared, ACT.Identity, bias=gcol[:, 3:4], scale=gcol[:, 2:3]).then_inc(bank_free, 1)
                a.wait_ge(bank_full, bn + 3)
                a.activation(ohT[:, b, :], shared[0:E, :], ACT.Copy).then_inc(ohT_done, 1)
                a.activation(ohTb[:, b, :], shared[0:E, :], ACT.Copy).then_inc(bank_free, 1)
            with a.Fori(0, NB) as b:
                for n in range(E * FB):
                    e, fb = n // FB, n % FB
                    a.wait_ge(up_ready, b * (E * FB) + (cnt["up"] + n + 1))
                    wait(a, mid_done, b * (E * FB) + (cnt["mid"] + max(n - 1, 0)))
                    a.activation(relu[:, n % 2, :], ps[:, n % 4, :], ACT.Relu, bias=b1c[:, e, fb:fb + 1])\
                        .then_inc(relu_done, 1)

        def moe_dve(v, cnt):
            with v.Fori(0, NB) as b:
                bn = b * 3 + cnt["bank"]
                r = (b + cnt["moe"] * NB) * 6
                ln_stats(v, b, b + cnt["ln"], res, b + (cnt["xd"] - NB + 1))
                ln_norm(v, b, b + cnt["ln"], None, res, False)
                v.wait_ge(bank_full, bn + 2)
                v.tensor_tensor(logit[:, :, :], shared_t[:, :, 0:E],
                                gbb[:, :].rearrange("p (o e) -> p o e", o=1).broadcast_to([P, TB, E]),
                                ALU.add).then_inc(bank_free, 1)
                v.wait_ge(bank_free, bn + 2)
                v.tensor_reduce(lmax[:, :], logit[:, :, :], AX, ALU.max).then_inc(route, 1)

                def spread(t):
                    return t[:, :].rearrange("p (i o) -> p i o", o=1).broadcast_to([P, TB, E])

                v.wait_ge(route, r + 1)
                v.tensor_tensor(score[:, :, :], logit[:, :, :], spread(lmax), ALU.is_equal).then_inc(route, 1)
                v.wait_ge(route, r + 2)
                v.tensor_tensor(score[:, :, :], score[:, :, :], pref[:, :, :], ALU.mult).then_inc(route, 1)
                v.wait_ge(route, r + 3)
                v.tensor_reduce(smax[:, :], score[:, :, :], AX, ALU.max).then_inc(route, 1)
                v.wait_ge(route, r + 4)
                v.tensor_tensor(oneh[:, :, :], score[:, :, :], spread(smax), ALU.is_equal).then_inc(route, 2)
                v.scalar_tensor_tensor(tiles(x, b), tiles(res, b), 0.5, tiles(x, b), ALU.mult,
                                       ALU.add).then_inc(half_done, 1)
            with v.Fori(0, NB) as b:
                for n in range(E * FB):
                    e, fb = n // FB, n % FB
                    if fb == 0:
                        v.wait_ge(mask_ready, b * E + (cnt["pick"] + e + 1))
                    v.wait_ge(relu_done, b * (E * FB) + (cnt["relu"] + n + 1))
                    wait(v, down_done, b * (E * FB) + (cnt["mid"] + max(n - 3, 0)))
                    v.tensor_tensor(mid[:, n % 4, :], relu[:, n % 2, :], ps[:, 4 + e % 2, :],
                                    ALU.mult).then_inc(mid_done, 1)
                v.wait_ge(down_done, b * (E * FB) + (cnt["mid"] + E * FB))
                v.wait_ge(half_done, b + (cnt["moe"] * NB + 1))
                v.scalar_tensor_tensor(tiles(x, b), ps[:, 6, :].rearrange("p (i c) -> p i c", c=P), 0.5, tiles(x, b),
                                       ALU.mult, ALU.add).then_inc(y_free, 1)
                v.wait_ge(y_free, b + (cnt["y"] + 1))
                v.sem_inc(x_done, 1)

        def moe_pool(g_, cnt):
            with g_.Fori(0, NB) as b:
                ln_pool(g_, b + cnt["ln"], False)
                apart(g_, bank_free, b * 3 + (cnt["bank"] + 1))
                g_.tensor_copy(hTa[:, b, :], hT[:, :]).then_inc(hta_done, 1)
            with g_.Fori(0, NB) as b:
                apart(g_, ohT_done, b + (cnt["moe"] * NB + 1))
                apart(g_, down_done, b * (E * FB) + cnt["mid"])
                g_.tensor_copy(ohs[:, :], ohT[:, b, :]).then_inc(ohs_done, 1)

        def ffn_pe(pe, cnt):
            with pe.Fori(0, NB) as b:
                transpose_ln(pe, b + cnt["ln"], b + cnt["bank"])
            pe.wait_ge(max_done, cnt["half"] * 8)
            pe.wait_ge(bank_free, cnt["bank"] + NB)
            with pe.Fori(0, NB) as b:
                m0 = b * FB + cnt["mid"]
                wait(pe, y_free, b + cnt["y"])

                def down(n):
                    pe.wait_ge(mid_done, m0 + n + 1)
                    for i in range(TB):
                        ins = pe.matmul(ps[:, 6, i * P:(i + 1) * P], mid[:, n, i * P:(i + 1) * P], wo2[:, n, :],
                                        start=(n == 0 and i == 0), stop=(n == FB - 1), skip_group_check=True)
                    ins.then_inc(down_done, 1)

                for n in range(FB):
                    for kx in range(TOPK):
                        if kx == 0:
                            wait(pe, relu_done, b * FB + (cnt["relu"] + max(n - 1, 0)))
                        else:
                            wait(pe, fold_done, b * FB + (cnt["fold"] + max(n - 1, 0)))
                        pe.matmul(ps[:, (2 * n + kx) % 4, :], wk[:, kx, n * P:(n + 1) * P], hTa[:, b, :], start=True,
                                  stop=True).then_inc(up_ready, 1)
                    if n >= 1:
                        down(n - 1)
                down(FB - 1)

        def ffn_act(a, cnt):
            with a.Fori(0, NB) as b:
                a.wait_ge(bank_full, b + (cnt["bank"] + 1))
                a.activation(hTa[:, b, :], shared, ACT.Copy).then_inc(bank_free, 1)
            with a.Fori(0, NB) as b:
                for n in range(FB):
                    a.wait_ge(up_ready, b * (FB * TOPK) + (cnt["up"] + 2 * n + 1))
                    wait(a, mid_done, b * FB + (cnt["mid"] + max(n - 1, 0)))
                    a.activation(relu[:, n % 2, :], ps[:, (2 * n) % 4, :], ACT.Relu).then_inc(relu_done, 1)

        def ffn_dve(v, cnt):
            with v.Fori(0, NB) as b:
                ln_stats(v, b, b + cnt["ln"], x, b + (cnt["xd"] - NB + 1))
                ln_norm(v, b, b + cnt["ln"], b + cnt["bank"], x, False)
            with v.Fori(0, NB) as b:
                for n in range(FB):
                    v.wait_ge(up_ready, b * (FB * TOPK) + (cnt["up"] + 2 * n + 2))
                    wait(v, mid_done, b * FB + (cnt["mid"] + max(n - 1, 0)))
                    v.tensor_scalar(fold[:, n % 2, :], ps[:, (2 * n + 1) % 4, :], 0.0, tkv[:, 1:2], ALU.max,
                                    ALU.mult).then_inc(fold_done, 1)
                    v.wait_ge(fold_done, b * FB + (cnt["fold"] + n + 1))
                    v.wait_ge(relu_done, b * FB + (cnt["relu"] + n + 1))
                    wait(v, down_done, b * FB + (cnt["mid"] + max(n - 3, 0)))
                    v.scalar_tensor_tensor(mid[:, n, :], relu[:, n % 2, :], tkv[:, 0:1], fold[:, n % 2, :], ALU.mult,
                                           ALU.add).then_inc(mid_done, 1)
                v.wait_ge(down_done, b * FB + (cnt["mid"] + FB))
                v.scalar_tensor_tensor(tiles(x, b), ps[:, 6, :].rearrange("p (i c) -> p i c", c=P), 0.5, tiles(x, b),
                                       ALU.mult, ALU.add).then_inc(y_free, 1)
                v.wait_ge(y_free, b + (cnt["y"] + 1))
                v.sem_inc(x_done, 1)

        def ffn_pool(g_, cnt):
            with g_.Fori(0, NB) as b:
                ln_pool(g_, b + cnt["ln"], False)

        loads = [(x[:, 0:TB * NB, :], d["L0_attn_x"].rearrange("b (i p) d -> p (b i) d", p=P))]
        wl = []
        for j, n in enumerate(("L0_ffn_wq", "L0_ffn_wk", "L0_ffn_wv", "L0_ffn_wo", "L0_attn_W_q", "L0_attn_W_k",
                               "L0_attn_W_v", "L0_attn_W_o")):
            wl.append((wraw[:, j, :], d[n]))
        wl.append((wraw[:, 8:11, :], d["L1_attn_w_in"].rearrange("(a p) d -> p a d", p=P)))
        wl.append((wraw[:, 11, :], d["L1_attn_w_out"]))
        b_in = d["L1_attn_b_in"]
        for c_, v_ in enumerate((d["L0_ffn_bq"], d["L0_ffn_bk"], d["L0_attn_b_q"], d["L0_attn_b_k"], b_in[0:P],
                                 b_in[P:2 * P])):
            o = v_.rearrange("(t s e) -> s e t", s=2, e=DH)
            for s in range(2):
                wl.append((bcol[64 * s:64 * s + 64, c_:c_ + 1], o[s]))
        for j, v_ in enumerate((d["L0_ffn_bv"], d["L0_attn_b_v"], b_in[2 * P:3 * P])):
            wl.append((bvb[:, j, :], v_.partition_broadcast(P)))
        for j, v_ in enumerate((d["L0_ffn_bo"], d["L0_attn_b_o"], d["L1_attn_b_out"])):
            wl.append((bob[:, j, :], v_.partition_broadcast(P)))
        for j, n in enumerate(("L0_ffn_ln1_g", "L0_ffn_ln1_b", "L0_ffn_ln2_g", "L0_ffn_ln2_b")):
            wl.append((gcol[:, j:j + 1], d[n].rearrange("(p o) -> p o", o=1)))
        wl += [
            (w1[:, :, :], d["L0_ffn_w1"].rearrange("e p f -> p e f")),
            (w2[:, :, :, :].rearrange("p e a h -> p (e a) h"), d["L0_ffn_w2"].rearrange("e (a p) h -> p (e a) h", p=P)),
            (b1c[:, :, :].rearrange("p e a -> p (e a)"), d["L0_ffn_b1"].rearrange("e (a p) -> p (e a)", p=P)),
            (b2r[:, :], d["L0_ffn_b2"]),
            (gw[:, :], d["L0_ffn_gate_w"]),
            (gbb[:, :], d["L0_ffn_gate_b"].partition_broadcast(P)),
            (wi_raw[:, :, :], d["L1_ffn_wi_w"].rearrange("(a p) h -> p a h", p=P)),
            (wo_raw[:, :], d["L1_ffn_wo_w"]),
            (tkv[:, :], d["L1_ffn_top_k_values"].partition_broadcast(P)),
        ]
        NCONST = 26

        @block.sync
        def _(sp):
            sp.dma_start(*loads[0]).then_inc(x_loaded, 16)
            sp.dma_start(idx[:, :], d["L1_ffn_top_k_indices"].rearrange("(o k) -> o k", o=1)).then_inc(idx_loaded, 16)
            for dst, src in wl:
                sp.dma_start(dst, src, allow_slow_non_contiguous=True).then_inc(w_loaded, 16)
            sp.wait_ge(idx_loaded, 16)
            for kx in range(TOPK):
                which = sp.value_load(idx[0:1, kx:kx + 1], min_val=0, max_val=E - 1)
                sp.dma_start(loA[:, kx, :], d["L1_ffn_lora_As"][bass.ds(which, 1), :, :]
                             .rearrange("o r h -> (o r) h")).then_inc(lora_loaded, 16)
                sp.dma_start(loB[:, kx, :, :], d["L1_ffn_lora_Bs"][bass.ds(which, 1), :, :]
                             .rearrange("o (a p) r -> p (o a) r", p=P)).then_inc(lora_loaded, 16)
            sp.wait_ge(const_done, NCONST)
            for kind, w, cnt in phases:
                if kind == "attn":
                    attention_sync(sp, cnt)
            last = phases[-1][2]
            out_t = d["out"].rearrange("b (i p) h -> b p i h", p=P)
            for b in range(NB):
                sp.wait_ge(x_done, last["xd"] + b + 1)
                sp.dma_start(out_t[b], tiles(x, b)).then_inc(out_done, 16)
            sp.wait_ge(out_done, 16 * NB)
            sp.wait_ge(qk_loaded, c["prep"] * STACKED)

        @block.gpsimd
        def _(g_):
            done = [0]

            for s in credited:
                g_.sem_inc(s, ONE)

            def const(ins):
                done[0] += 1
                ins.then_inc(const_done, 1)

            const(g_.memset(identf[:, :], 0.0))
            const(g_.memset(identb[:, :], 0.0))
            const(g_.memset(mask_q[:, :], 0.0))
            const(g_.memset(mask_k[:, :], 0.0))
            const(g_.memset(pick[:, :, :], 0.0))
            for i in range(2):
                const(g_.memset(va[i][:, :, :, :], 0.0))
                const(g_.memset(ks[i][:, :, :], 1.0))
                const(g_.memset(qs[i][:, :, :, :].rearrange("p s t c -> p (s t c)").bitcast(F32), 0.0))
            const(g_.memset(mzero[:, :], 0.0))
            g_.wait_ge(const_done, 12)
            const(g_.affine_select(out=identf[:, :], in_=identf[:, :], compare_op=ALU.not_equal, fill=1.0, base=0,
                                   pattern=[[-1, P]], channel_multiplier=1))
            const(g_.affine_select(out=identb[:, :], in_=identb[:, :], compare_op=ALU.not_equal, fill=1.0, base=0,
                                   pattern=[[-1, P]], channel_multiplier=1))
            const(g_.affine_select(out=mask_q[:, :], in_=mask_q[:, :], compare_op=ALU.is_ge, fill=MASKED, base=0,
                                   pattern=[[-1, P]], channel_multiplier=1))
            const(g_.affine_select(out=mask_k[:, :], in_=mask_k[:, :], compare_op=ALU.is_ge, fill=MASKED, base=0,
                                   pattern=[[1, P]], channel_multiplier=-1))
            const(g_.affine_select(out=pick[:, :, :], in_=pick[:, :, :], compare_op=ALU.not_equal, fill=1.0, base=0,
                                   pattern=[[-1, E], [0, P]], channel_multiplier=1))
            for i in range(2):
                const(g_.memset(va[i][:, :, :, DH:DH + 1], 1.0))
            const(g_.memset(minus_half[:, :], -0.5))
            const(g_.memset(x[:, TB * NB:NT, :], 0.0))
            const(g_.memset(ones_col[:, :], 1.0))
            const(g_.memset(zero_col[:, :], 0.0))
            const(g_.iota(pref_i[:, :, :], pattern=[[0, TB], [-1, E]], base=E, channel_multiplier=0))
            g_.wait_ge(const_done, 24)
            const(g_.tensor_copy(pref[:, :, :], pref_i[:, :, :]))
            g_.wait_ge(const_done, 25)
            const(g_.memset(upd2[:, 0, 0:1], 0.0))
            assert done[0] == NCONST
            g_.wait_ge(const_done, NCONST)
            for kind, w, cnt in phases:
                if kind == "attn":
                    attention_pool(g_, W[w], cnt)
                elif kind == "moe":
                    moe_pool(g_, cnt)
                else:
                    ffn_pool(g_, cnt)
            apart(g_, m_loaded, c["quad"] * 32)

        @block.vector
        def _(v):
            v.wait_ge(const_done, NCONST)
            v.wait_ge(x_loaded, 16)
            v.wait_ge(w_loaded, 16 * len(wl))
            bn = 0

            def leave(dst, src=shared):
                nonlocal bn
                v.wait_ge(bank_full, bn + 1)
                v.tensor_copy(dst, src).then_inc(bank_free, 1)
                bn += 1

            leave(wT[:, :, :].rearrange("p a c -> p (a c)"))
            v.wait_ge(bank_free, 1)
            v.tensor_copy(bcols[:, :], bcol[:, :]).then_inc(set_dve, 1)
            v.wait_ge(set_dve, 1)
            v.tensor_scalar(bcols[:, 0:6:2], bcol[:, 0:6:2], SCALE, None, ALU.mult).then_inc(set_dve, 1)
            for j, src in enumerate((wraw[:, 0, :], wraw[:, 1, :], wraw[:, 4, :], wraw[:, 5, :], wT[:, 0, :],
                                     wT[:, 1, :])):
                v.tensor_copy(wperm[:, j, :].rearrange("p (s e t) -> p s e t", s=2, e=DH),
                              src.rearrange("p (t s e) -> p s e t", s=2, e=DH)).then_inc(set_dve, 1)
            leave(wiT[:, :])
            leave(wo2[:, :, :].rearrange("p a c -> p (a c)"))
            for kx in range(TOPK):
                leave(loBT[:, kx, :], shared[0:RANK, :])
            for kx in range(TOPK):
                v.wait_ge(bank_full, bn + 1)
                v.tensor_tensor(wk[:, kx, :], shared, wiT[:, :], ALU.add).then_inc(bank_free, 1)
                bn += 1
            assert bn == SETUP_BANK
            for kind, w, cnt in phases:
                if kind == "attn":
                    attention_dve(v, W[w], cnt)
                elif kind == "moe":
                    moe_dve(v, cnt)
                else:
                    ffn_dve(v, cnt)

        SET_DVE = 2 + 6

        @block.scalar
        def _(a):
            a.wait_ge(const_done, NCONST)
            a.wait_ge(w_loaded, 16 * len(wl))
            a.wait_ge(set_dve, SET_DVE)
            for kind, w, cnt in phases:
                if kind == "attn":
                    attention_act(a, W[w], cnt)
                elif kind == "moe":
                    moe_act(a, cnt)
                else:
                    ffn_act(a, cnt)

        @block.tensor
        def _(pe):
            pe.wait_ge(const_done, NCONST)
            pe.wait_ge(w_loaded, 16 * len(wl))
            bn = 0

            def flip(pairs):
                nonlocal bn
                wait(pe, bank_free, bn)
                for dst, src in pairs:
                    ins = pe.transpose(dst, src, identf[:, :])
                ins.then_inc(bank_full, 1)
                bn += 1

            flip([(shared_t[:, i, :], wraw[:, 8 + i, :]) for i in range(4)])
            flip([(shared_t[:, i, :], wi_raw[:, i, :]) for i in range(FB)])
            flip([(shared_t[:, i, :], wo_raw[:, i * P:(i + 1) * P]) for i in range(FB)])
            pe.wait_ge(lora_loaded, 16 * 2 * TOPK)
            for kx in range(TOPK):
                flip([(shared_t[0:RANK, i, :], loB[:, kx, i, :]) for i in range(FB)])
            for kx in range(TOPK):
                wait(pe, bank_free, bn)
                pe.matmul(shared, loA[:, kx, :], loBT[:, kx, :], start=True, stop=True).then_inc(bank_full, 1)
                bn += 1
            pe.wait_ge(set_dve, SET_DVE)
            for kind, w, cnt in phases:
                if kind == "attn":
                    attention_pe(pe, W[w], cnt)
                elif kind == "moe":
                    moe_pe(pe, cnt)
                else:
                    ffn_pe(pe, cnt)


NAMES = ["L0_attn_x", "L0_attn_W_q", "L0_attn_b_q", "L0_attn_W_k", "L0_attn_b_k", "L0_attn_W_v", "L0_attn_b_v",
         "L0_attn_W_o", "L0_attn_b_o", "L0_ffn_ln1_g", "L0_ffn_ln1_b", "L0_ffn_ln2_g", "L0_ffn_ln2_b", "L0_ffn_wq",
         "L0_ffn_bq", "L0_ffn_wk", "L0_ffn_bk", "L0_ffn_wv", "L0_ffn_bv", "L0_ffn_wo", "L0_ffn_bo", "L0_ffn_gate_w",
         "L0_ffn_gate_b", "L0_ffn_w1", "L0_ffn_b1", "L0_ffn_w2", "L0_ffn_b2", "L1_attn_w_in", "L1_attn_b_in",
         "L1_attn_w_out", "L1_attn_b_out", "L1_ffn_wi_w", "L1_ffn_wo_w", "L1_ffn_lora_As", "L1_ffn_lora_Bs",
         "L1_ffn_top_k_indices", "L1_ffn_top_k_values"]


def kernel(**inputs):
    import concourse.bacc as bacc
    import numpy as np
    from concourse.bass_utils import run_bass_kernel_spmd

    nc = bacc.Bacc("TRN2", target_bir_lowering=False, num_devices=1)
    arrays, d = {}, {}
    for name in NAMES:
        a = np.ascontiguousarray(inputs[name])
        arrays[f"in_{name}"] = a
        d[name] = nc.dram_tensor(f"in_{name}", a.shape, mybir.dt.from_np(a.dtype), kind="ExternalInput").ap()
    shape = inputs["L0_attn_x"].shape
    d["out"] = nc.dram_tensor("out_dram", shape, F32, kind="ExternalOutput").ap()
    program(nc, d)
    return run_bass_kernel_spmd(nc, [arrays], core_ids=[0]).results[0]["out_dram"]
```

```python
from contextlib import ExitStack

import concourse.bass as bass
from concourse import mybir

F32 = mybir.dt.float32
BF16 = mybir.dt.bfloat16
I32 = mybir.dt.int32
U32 = mybir.dt.uint32
ALU = mybir.AluOpType
ACT = mybir.ActivationFunctionType
AX = mybir.AxisListType.X

P = 128
NB, S = 4, 512
TB = S // P
H, DH = 16, 8
E, F = 8, 512
FB = F // P
TOPK = 2
RANK = 16
EPS = 1e-5
SCALE = float(1.0 / DH ** 0.5)
MASKED = -1e30
NPROD = 6
KROWS = NPROD * DH
MROWS = 3
QPART = [0, 0, 0, 1, 1, 2]
KPART = [0, 1, 2, 0, 1, 0]
UNITS = 8
LEAD = 3
STACKED = (2 * 2 * NPROD + 2) * 16
NPT = 8
TILES = 16
SLOTS = TILES + E - 1
ROW = P + 1
WE = 2 * F + FB + P

PLAN = {
    (0, 0): ["stats+"], (0, 3): ["norm+"],
    (1, 0): ["hT+"], (1, 1): ["m1"], (1, 2): ["q+"], (1, 3): ["k+"],
    (2, 0): ["v+"],
    (3, 1): ["m2"], (3, 3): ["o0"],
    (5, 1): ["m3"], (5, 3): ["o1"],
    (7, 1): ["m0+"], (7, 3): ["o2"],
}
LATE = {(2, 1): ["o3-"], (2, 3): ["onT-"], (3, 0): ["out-"]}
PLANS = [PLAN, {at: PLAN.get(at, []) + LATE.get(at, []) for at in set(PLAN) | set(LATE)}]
HEADJOBS = ["stats", "norm", "hT", "q", "k", "v"]
TAIL = ["o3", "onT", "out"]
NOBANK = ("stats", "norm")

PV_AT = [
    {0: [(2, 3)], 1: [(1, 0)], 2: [(1, 1), (1, 2)], 3: [(1, 3)]},
    {1: [(1, 0)], 2: [(1, 1)], 3: [(1, 2)]},
]
PV_LEFT = [(6, 3), (7, 0), (7, 1), (7, 2), (7, 3)]


def bank_jobs():
    order = []
    for par in range(2):
        for u in range(UNITS):
            for k in range(4):
                order += [(par, j) for j in PLANS[par].get((u, k), []) if j.rstrip("+-") not in NOBANK]
    return order + [(1, j) for j in TAIL]


BANK = bank_jobs()
BANKHEAD = ["hT", "q", "k", "v", "m0"]


def program(nc, d):
    with ExitStack() as ctx:
        def sb(name, shape, dt=F32):
            return ctx.enter_context(nc.sbuf_tensor(name, shape, dt))

        def sem(name):
            return ctx.enter_context(nc.semaphore(name))

        ps = ctx.enter_context(nc.psum_tensor("ps", [P, 8, 512], F32))
        SH = 7
        shared = ps[:, SH, :]
        shared_t = shared.rearrange("p (i c) -> p i c", c=P)
        pv_bank = ps[:, 6, :]

        NT = TB * (NB + 1)
        x = sb("x", [P, NT, P])
        res = sb("res", [P, NT, P])
        lnx = sb("lnx", [P, TB, P])
        stats = sb("stats", [P, TILES, 6])
        mv = sb("mv", [P, TILES, 2])
        rstd = sb("rstd", [P, TILES])
        rstd2 = sb("rstd2", [P, TILES])
        lntmp = sb("lntmp", [P, TILES])
        minus_half = sb("minus_half", [P, TILES])
        hT = sb("hT", [P, S])
        q32 = sb("q32", [P, 2, S])
        rem = sb("rem", [P, 2, S])
        parts = sb("parts", [P, 2, 3, S], BF16)
        qs = [sb(f"qs{i}", [P, 2, H // 2, S], BF16) for i in range(2)]
        ks = [sb(f"ks{i}", [P, H // 2, S], BF16) for i in range(2)]
        va = [sb(f"va{i}", [P, TB, H, 32]) for i in range(2)]
        negm = sb("negm", [P, 2, 2, 2, TB])
        mrem = sb("mrem", [P, 2, 2, TB])
        mpart = sb("mpart", [P, 2, 3, 2 * TB], BF16)
        mrow = sb("mrow", [2 * 3 * 2 * TB, P], BF16)
        pt = sb("pt", [P, NPT, 1024])
        ot = sb("ot", [P, S])
        rc = sb("rc", [P, TB, 4])
        on = sb("on", [P, TB, P])
        onT = sb("onT", [P, S])
        upd = sb("upd", [P, TB, P])
        upd2 = onT[:, :].rearrange("p (i c) -> p i c", i=TB)
        identf = sb("identf", [P, P])
        identb = sb("identb", [P, P], BF16)
        mask_q = sb("mask_q", [P, P], BF16)
        mask_k = sb("mask_k", [P, P], BF16)
        ones_col = sb("ones_col", [P, 1])
        zero_col = sb("zero_col", [P, 1])
        wraw = sb("wraw", [P, 12, P])
        wT = sb("wT", [P, 4, P])
        wperm = sb("wperm", [P, 6, P])
        bcol = sb("bcol", [P, 6])
        bcols = sb("bcols", [P, 6])
        bvb = sb("bvb", [P, 3, P])
        bob = sb("bob", [P, 3, P])
        gcol = sb("gcol", [P, 4])
        experts = sb("experts", [P, E, WE])
        gw = sb("gw", [P, E])
        gbb = sb("gbb", [P, E])
        logit = sb("logit", [P, TILES, E])
        lmax = sb("lmax", [P, TILES])
        pref_i = sb("pref_i", [P, TILES, E], I32)
        pref = sb("pref", [P, TILES, E])
        score = sb("score", [P, TILES, E])
        smax = sb("smax", [P, TILES])
        ohb = sb("ohb", [P, TILES, E], BF16)
        earlier = sb("earlier", [P, P], BF16)
        onesb = sb("onesb", [P, P], BF16)
        count_i = sb("count_i", [P, SLOTS], I32)
        count = sb("count", [P, SLOTS])
        lower_e = sb("lower_e", [P, E, E])
        more = sb("more", [P, E, TILES])
        ntile = sb("ntile", [P, E])
        first = sb("first", [P, E])
        last_e = sb("last_e", [P, E])
        posf = sb("posf", [P, TILES])
        pos = sb("pos", [P, TILES], U32)
        owner_c = sb("owner_c", [1, SLOTS, E - 1])
        ownerf = sb("ownerf", [1, SLOTS])
        owner = sb("owner", [1, SLOTS], I32)
        numbers_y = sb("numbers_y", [P, 2], U32)
        mzero = sb("mzero", [MROWS, S], BF16)
        ptf = pt[:, :, :].rearrange("p a c -> p (a c)")
        lnall = ptf[:, 3072:3072 + TILES * ROW].rearrange("p (a c) -> p a c", c=ROW)
        relu = pt[:, 0, :].rearrange("p (a c) -> p a c", a=2)
        fold = pt[:, 1, :].rearrange("p (a c) -> p a c", a=2)
        mid = pt[:, 2:4, :].rearrange("p a (b c) -> p (a b) c", b=2)
        hTa = pt[:, 6:8, :].rearrange("p a (b c) -> p (a b) c", b=2)
        xs = ptf[:, 0:SLOTS * ROW].rearrange("p (a c) -> p a c", c=ROW)
        yall = ptf[:, 3072:3072 + TILES * P].rearrange("p (a c) -> p a c", c=P)
        we = ptf[:, 5184:5184 + 2 * WE].rearrange("p (a c) -> p a c", c=WE)
        hTm = onT[:, 0:2 * P].rearrange("p (a c) -> p a c", a=2)
        mid_e = q32[:, :, :].rearrange("p a (b c) -> p a b c", c=P)
        ysb = upd[:, 0:2, :]
        xst = lnx[:, 0:2, :]
        hTa_moe = ptf[:, 5184:5184 + NB * S].rearrange("p (a c) -> p a c", a=NB)
        numbers_t = sb("numbers_t", [P, TILES], U32)
        padding = ptf[:, 0:SLOTS * ROW].rearrange("p (a c) -> p a c", c=ROW)
        wi_raw = pt[:, 4, 0:F].rearrange("p (a c) -> p a c", c=P)
        wo_raw = pt[:, 4, F:2 * F]
        loA = pt[0:RANK, 5, 0:TOPK * P].rearrange("p (a c) -> p a c", a=TOPK)
        loB = pt[:, 5, F:F + TOPK * FB * RANK].rearrange("p (a b c) -> p a b c", a=TOPK, b=FB)
        loBT = pt[0:RANK, 6, :].rearrange("p (a c) -> p a c", a=TOPK)
        wiT = pt[:, 7, 0:F]
        wk = sb("wk", [P, TOPK, F])
        wo2 = sb("wo2", [P, FB, P])
        idx = sb("idx", [1, TOPK], I32)
        tkv = sb("tkv", [P, TOPK])

        x_loaded = sem("x_loaded")
        w_loaded = sem("w_loaded")
        idx_loaded = sem("idx_loaded")
        lora_loaded = sem("lora_loaded")
        const_done = sem("const_done")
        set_dve = sem("set_dve")
        set_pe = sem("set_pe")
        set_free = sem("set_free")
        ln_stat = sem("ln_stat")
        ln_rstd = sem("ln_rstd")
        ln_x = sem("ln_x")
        h_kept = sem("h_kept")
        bank_full = sem("bank_full")
        bank_free = sem("bank_free")
        hi_done = sem("hi_done")
        split_done = sem("split_done")
        qk_loaded = sem("qk_loaded")
        p1_ready = sem("p1_ready")
        max_done = sem("max_done")
        m_parts = sem("m_parts")
        m_loaded = sem("m_loaded")
        p2_ready = sem("p2_ready")
        exp_done = sem("exp_done")
        pv_done = sem("pv_done")
        ot_ready = sem("ot_ready")
        rc_done = sem("rc_done")
        guard_done = sem("guard_done")
        x_done = sem("x_done")
        up_ready = sem("up_ready")
        relu_done = sem("relu_done")
        fold_done = sem("fold_done")
        mid_done = sem("mid_done")
        down_done = sem("down_done")
        y_free = sem("y_free")
        ln_turned = sem("ln_turned")
        hta_done = sem("hta_done")
        logits_ready = sem("logits_ready")
        owner_step = sem("owner_step")
        route = sem("route")
        rank_ready = sem("rank_ready")
        prefilled = sem("prefilled")
        numbered = sem("numbered")
        rows_sorted = sem("rows_sorted")
        xs_loaded = sem("xs_loaded")
        tile_copied = sem("tile_copied")
        tile_turned = sem("tile_turned")
        tile_in = sem("tile_in")
        expert_ready = sem("expert_ready")
        tile_down = sem("tile_down")
        y_ready = sem("y_ready")
        y_sent = [sem("y_sent0"), sem("y_sent1")]
        y_loaded = [sem(f"y_loaded{b}") for b in range(NB)]
        out_done = sem("out_done")
        stood_apart = sem("stood_apart")

        W = [
            dict(wq=wperm[:, 0, :], wk=wperm[:, 1, :], wv=wraw[:, 2, :], wo=wraw[:, 3, :], n=0,
                 g=gcol[:, 0:1], b=gcol[:, 1:2], causal=False, moe=True, nan_guard=False),
            dict(wq=wperm[:, 2, :], wk=wperm[:, 3, :], wv=wraw[:, 6, :], wo=wraw[:, 7, :], n=1,
                 g=ones_col[:, :], b=zero_col[:, :], causal=True, moe=False, nan_guard=False),
            dict(wq=wperm[:, 4, :], wk=wperm[:, 5, :], wv=wT[:, 2, :], wo=wT[:, 3, :], n=2,
                 g=ones_col[:, :], b=zero_col[:, :], causal=True, moe=False, nan_guard=True),
        ]
        ORDER = [("attn", 0), ("moe", None), ("attn", 1), ("attn", 0), ("moe", None), ("ffn", None),
                 ("attn", 2), ("ffn", None)]
        ATTN_LN, ATTN_BANK = NB + 1, len(BANKHEAD) + NB // 2 * len(BANK)
        ATTN_HALVES, ATTN_QUADS = NB * UNITS + LEAD, NB * 4 + 1

        SETUP_BANK = 3 + 2 * TOPK

        ONE = 1
        credited = [pv_done, exp_done, ot_ready, y_free, mid_done, down_done, relu_done, fold_done, tile_down, y_ready]

        phases = []
        c = dict(ln=0, bank=SETUP_BANK, half=0, quad=0, attn=0, moe=0, xd=0, prep=0, up=0, mid=ONE, relu=ONE, pick=0,
                 y=ONE, fold=ONE, kept=0, tr=0)
        for kind, w in ORDER:
            phases.append((kind, w, dict(c)))
            if kind == "attn":
                c["ln"] += ATTN_LN
                c["bank"] += ATTN_BANK
                c["half"] += ATTN_HALVES
                c["quad"] += ATTN_QUADS
                c["prep"] += NB + 1
                c["attn"] += 1
                c["kept"] += (NB + 1) * TB if W[w]["moe"] else 0
            elif kind == "moe":
                c["ln"] += NB
                c["tr"] += NB
                c["moe"] += 1
                c["up"] += SLOTS * FB
                c["relu"] += SLOTS * FB
            else:
                c["ln"] += NB
                c["tr"] += NB
                c["fold"] += NB * FB
                c["up"] += NB * FB * TOPK
                c["relu"] += NB * FB
                c["mid"] += NB * FB
                c["y"] += NB
            c["xd"] += NB
        def tiles(t, b):
            return t[:, bass.ds(b * TB, TB), :] if not isinstance(b, int) else t[:, b * TB:(b + 1) * TB, :]

        def tile(t, b, j):
            return t[:, b * TB + j, :]

        def wait(eng, s, n):
            if not isinstance(n, int) or n > 0:
                eng.wait_ge(s, n)

        def apart(eng, s, n):
            wait(eng, s, n)
            if not isinstance(n, int):
                eng.sem_inc(stood_apart, 1)

        block = ctx.enter_context(nc.Block())

        def ln_stats(v, b, n, src, x_ready):
            if x_ready is not None:
                v.wait_ge(x_done, x_ready)
            wait(v, ln_x, n)
            for j in range(TB):
                v.bn_stats(stats[:, j, :], tile(src, b, j)).then_inc(ln_stat, 1)
            apart(v, ln_stat, n * 8 + 4)
            for j in range(TB):
                v.bn_aggr(mv[:, j, :], stats[:, j, :]).then_inc(ln_stat, 1)

        everything = (lntmp[:, :], rstd[:, :], rstd2[:, :], mv[:, :, 1], minus_half[:, :])

        def ln_pool(g, n, twice, batches=1):
            lntmp, rstd, rstd2, var, minus_half = (t[:, 0:TB * batches] for t in everything)
            def step(i):
                return n * 7 + i
            apart(g, ln_stat, n * 8 + 8 * batches)
            apart(g, ln_x, n)
            g.tensor_scalar(lntmp, var, EPS, None, ALU.add).then_inc(ln_rstd, 1)
            apart(g, ln_rstd, step(1))
            g.tensor_tensor(rstd, lntmp, minus_half, ALU.pow).then_inc(ln_rstd, 1)
            apart(g, ln_rstd, step(2))
            if not twice:
                g.tensor_copy(rstd2, rstd).then_inc(ln_rstd, 7 * batches - 2)
                return
            g.tensor_tensor(lntmp, rstd, rstd, ALU.mult).then_inc(ln_rstd, 1)
            apart(g, ln_rstd, step(3))
            g.tensor_tensor(lntmp, lntmp, var, ALU.mult).then_inc(ln_rstd, 1)
            apart(g, ln_rstd, step(4))
            g.tensor_scalar(lntmp, lntmp, EPS, None, ALU.add).then_inc(ln_rstd, 1)
            apart(g, ln_rstd, step(5))
            g.tensor_tensor(lntmp, lntmp, minus_half, ALU.pow).then_inc(ln_rstd, 1)
            apart(g, ln_rstd, step(6))
            g.tensor_tensor(rstd2, lntmp, rstd, ALU.mult).then_inc(ln_rstd, 1)

        def ln_norm(v, b, n, bank_n, src, keep):
            v.wait_ge(ln_rstd, n * 7 + 7)
            if bank_n is not None:
                wait(v, bank_full, bank_n)
            if keep:
                for j in range(TB):
                    v.tensor_scalar(tile(res, b, j), tile(src, b, j), mv[:, j, 0:1], rstd[:, j:j + 1],
                                    ALU.subtract, ALU.mult).then_inc(h_kept, 1)
            for j in range(TB):
                ins = v.tensor_scalar(lnx[:, j, :], tile(src, b, j), mv[:, j, 0:1], rstd2[:, j:j + 1],
                                      ALU.subtract, ALU.mult)
            ins.then_inc(ln_x, 1)

        def ln_everything(v, cnt, src):
            n = cnt["ln"]
            v.wait_ge(ln_x, n)
            for b in range(NB):
                v.wait_ge(x_done, cnt["xd"] - NB + 1 + b)
                for j in range(TB):
                    v.bn_stats(stats[:, b * TB + j, :], tile(src, b, j)).then_inc(ln_stat, 1)
            v.wait_ge(ln_stat, n * 8 + TILES)
            for j in range(TILES):
                v.bn_aggr(mv[:, j, :], stats[:, j, :]).then_inc(ln_stat, 1)
            v.wait_ge(ln_rstd, (n + NB) * 7)
            for j in range(TILES):
                ins = v.tensor_scalar(lnall[:, j, 0:P], src[:, j, :], mv[:, j, 0:1], rstd[:, j:j + 1],
                                      ALU.subtract, ALU.mult)
                if j % TB == TB - 1:
                    ins.then_inc(ln_x, 1)

        def turn_everything(pe, cnt):
            for b in range(NB):
                pe.wait_ge(ln_x, cnt["ln"] + b + 1)
                for j in range(TB):
                    ins = pe.transpose(ps[:, 4 + b, j * P:(j + 1) * P], lnall[:, b * TB + j, 0:P], identf[:, :])
                ins.then_inc(ln_turned, 1)

        def transpose_ln(pe, n, bank_n):
            pe.wait_ge(ln_x, n + 1)
            wait(pe, bank_free, bank_n)
            for j in range(TB):
                ins = pe.transpose(shared_t[:, j, :], lnx[:, j, :], identf[:, :])
            ins.then_inc(bank_full, 1)

        def numbers(cnt, b, par):
            return dict(b=b, par=par, ln=b + cnt["ln"], half=b * UNITS + cnt["half"], quad=b * 4 + cnt["quad"],
                        unit=b * UNITS + cnt["attn"] * NB * UNITS, prep=b + cnt["prep"],
                        x_ready=b + (cnt["xd"] - NB + 1) if cnt["xd"] else None, ot=b * 4 + (cnt["attn"] * NB * 4 + ONE),
                        kept=b * TB + cnt["kept"],
                        xd=b + cnt["xd"])

        def bank_number(cnt, pair, par, job):
            return pair * len(BANK) + (cnt["bank"] + len(BANKHEAD) + BANK.index((par, job)))

        def pass1_tile(pe, w, N, g, hf, r):
            s, i = r // TB, r % TB
            n = (N["half"] + 2 * g + hf) * 8 + r
            t = 2 * g + hf
            q, k = qs[N["par"]], ks[N["par"]]
            width = (i + 1) * P if w["causal"] else S
            wait(pe, max_done, n - 1)
            ins = pe.matmul(ps[:, r % 2, 0:width], q[:, s, t, i * P:(i + 1) * P], k[:, t, 0:width], start=True,
                            stop=not w["causal"])
            if w["causal"]:
                ins = pe.matmul(ps[:, r % 2, i * P:width], identb[:, :], mask_q[:, :], start=False, stop=True)
            ins.then_inc(p1_ready, 1)

        def rowmax_tile(v, w, N, g, hf, r):
            s, i = r // TB, r % TB
            n = (N["half"] + 2 * g + hf) * 8 + r
            width = (i + 1) * P if w["causal"] else S
            v.wait_ge(p1_ready, n + 1)
            v.tensor_reduce(negm[:, g % 2, s, hf, i:i + 1], ps[:, r % 2, 0:width], AX, ALU.max,
                            negate=True).then_inc(max_done, 1)

        def split_max(g_, N, g, bank_n):
            n = (N["quad"] + g) * 4
            apart(g_, max_done, (N["half"] + 2 * g + 2) * 8)
            apart(g_, m_parts, n)
            src = negm[:, g % 2].rearrange("p s t i -> p s (t i)")
            rem_ = mrem[:, :, :, :].rearrange("p s t i -> p s (t i)")
            g_.tensor_copy(mpart[:, :, 0, :], src).then_inc(m_parts, 1)
            apart(g_, m_parts, n + 1)
            g_.tensor_tensor(rem_, src, mpart[:, :, 0, :], ALU.subtract).then_inc(m_parts, 1)
            apart(g_, m_parts, n + 2)
            g_.tensor_copy(mpart[:, :, 1, :], rem_).then_inc(m_parts, 1)
            apart(g_, m_parts, n + 3)
            g_.tensor_tensor(mpart[:, :, 2, :], rem_, mpart[:, :, 1, :], ALU.subtract).then_inc(m_parts, 1)

        def store_max(g_, N, g, bank_n):
            apart(g_, bank_free, bank_n + 1)
            for s in range(2):
                g_.dma_start(qs[N["par"]][64 * s + KROWS:64 * s + KROWS + MROWS, s, 2 * g:2 * g + 2, :],
                             mrow[24 * s:24 * s + 24, :]).then_inc(m_loaded, 16)

        def slot_cols(w, hf, kb):
            q0 = kb * P if w["causal"] else 0
            if w["causal"]:
                at = {0: 0, 1: S, 2: 0, 3: S - 2 * P}[kb]
            else:
                at = (kb % 2) * S
            return at, at + S - q0, q0

        def slot_width(w, hf):
            return slot_cols(w, hf, 2 * hf + 1)[1]

        def pass2_slot(pe, w, N, u, k):
            g, hf = u // 2, u % 2
            t, s = 2 * g + k // 2, k % 2
            n = (N["unit"] + u) * 4 + k
            q, kk = qs[N["par"]], ks[N["par"]]
            flat = ps[:, 2 + 2 * (k % 2):4 + 2 * (k % 2), :].rearrange("p a c -> p (a c)")
            if k == 0 and hf == 0:
                pe.wait_ge(m_loaded, (N["quad"] + g + 1) * 32)
            wait(pe, exp_done, (n - 1 if u or k else n) + ONE)
            for kb in (2 * hf, 2 * hf + 1):
                a, z, q0 = slot_cols(w, hf, kb)
                ins = pe.matmul(flat[:, a:z], kk[:, t, kb * P:(kb + 1) * P], q[:, s, t, q0:S],
                                start=True, stop=not w["causal"])
                if w["causal"]:
                    ins = pe.matmul(flat[:, a:a + P], identb[:, :], mask_k[:, :], start=False, stop=True)
            ins.then_inc(p2_ready, 1)

        def exp_slot(a, w, N, u, k):
            n = (N["unit"] + u) * 4 + k
            flat = ps[:, 2 + 2 * (k % 2):4 + 2 * (k % 2), :].rearrange("p a c -> p (a c)")
            width = slot_width(w, u % 2)
            a.wait_ge(p2_ready, n + 1)
            if k == 0:
                wait(a, pv_done, N["unit"] + (u - 1 if u or N["par"] else 0) + ONE)
            a.activation(pt[:, (u % 2) * 4 + k, 0:width], flat[:, 0:width], ACT.Exp).then_inc(exp_done, 1)

        def pv_piece(pe, w, N, u, piece):
            g, hf = u // 2, u % 2
            kb, half = 2 * hf + piece // 2, piece % 2
            a, _, q0 = slot_cols(w, hf, kb)
            if piece == 0:
                pe.wait_ge(exp_done, (N["unit"] + u + 1) * 4 + ONE)
                if hf == 0:
                    wait(pe, ot_ready, N["ot"] + g)
            lo, hi = max(half * S // 2, q0), (half + 1) * S // 2
            if lo >= hi:
                return
            for j in range(4):
                ins = pe.matmul(pv_bank[32 * j:32 * j + 32, lo:hi], va[N["par"]][:, kb, 4 * g + j, :],
                                pt[:, hf * 4 + j, a + lo - q0:a + hi - q0], start=(kb == 0 and half == 0),
                                stop=(kb == TB - 1), skip_group_check=True)
            if piece == 3:
                ins.then_inc(pv_done, 1)

        def pe_job(pe, w, cnt, N, job, bn):
            if job == "hT":
                transpose_ln(pe, N["ln"], bn)
            elif job in ("q", "k"):
                wait(pe, bank_free, bn)
                pe.matmul(shared, w["wq" if job == "q" else "wk"], hT[:, :], start=True, stop=True).then_inc(bank_full, 1)
            elif job == "v":
                wait(pe, bank_free, bn)
                for i in range(TB):
                    ins = pe.matmul(shared_t[:, i, :], hT[:, i * P:(i + 1) * P], w["wv"], start=True, stop=True)
                ins.then_inc(bank_full, 1)
            elif job[0] == "m":
                g = int(job[1])
                pe.wait_ge(m_parts, (N["quad"] + g) * 4 + 4)
                apart(pe, bank_free, bn)
                pe.transpose(shared[0:48, 0:P // 2].bitcast(BF16), mpart[:, :, :, :].rearrange("p s r c -> p (s r c)"),
                             identb[:, :]).then_inc(bank_full, 1)
            elif job in ("o0", "o1", "o2", "o3"):
                pe.wait_ge(ot_ready, N["ot"] + int(job[1]) + 1)
                wait(pe, bank_free, bn)
                for i in range(TB):
                    ins = pe.transpose(shared_t[:, i, :], ot[:, i * P:(i + 1) * P], identf[:, :])
                ins.then_inc(bank_full, 1)
            elif job == "onT":
                wait(pe, bank_free, bn)
                for i in range(TB):
                    ins = pe.transpose(shared_t[:, i, :], on[:, i, :], identf[:, :])
                ins.then_inc(bank_full, 1)
            elif job == "out":
                wait(pe, bank_free, bn)
                for i in range(TB):
                    ins = pe.matmul(shared_t[:, i, :], onT[:, i * P:(i + 1) * P], w["wo"], start=True, stop=True)
                ins.then_inc(bank_full, 1)

        def act_job(a, w, cnt, N, job, bn):
            if job == "hT":
                a.wait_ge(bank_full, bn + 1)
                a.activation(hT[:, :], shared, ACT.Identity, bias=w["b"], scale=w["g"]).then_inc(bank_free, 1)
            elif job in ("q", "k"):
                c_ = 0 if job == "q" else 1
                col = 2 * w["n"] + c_
                a.wait_ge(bank_full, bn + 1)
                wait(a, split_done, (N["prep"] - 1) * 6 + 3 * c_ + 3)
                a.activation(q32[:, c_, :], shared, ACT.Identity, bias=bcols[:, col:col + 1],
                             scale=SCALE if job == "q" else 1.0).then_inc(bank_free, 1)
                a.wait_ge(bank_free, bn + 1)
                wait(a, qk_loaded, N["prep"] * STACKED)
                a.activation(parts[:, c_, 0, :], q32[:, c_, :], ACT.Copy).then_inc(hi_done, 1)
            elif job[0] == "m":
                a.wait_ge(bank_full, bn + 1)
                wait(a, m_loaded, (N["quad"] + int(job[1])) * 32)
                a.activation(mrow[:, :], shared[0:48, 0:P // 2].bitcast(BF16), ACT.Copy).then_inc(bank_free, 1)
            elif job == "onT":
                a.wait_ge(bank_full, bn + 1)
                a.activation(onT[:, :], shared, ACT.Copy).then_inc(bank_free, 1)

        def ot_copy(a, N, u):
            g = u // 2
            a.wait_ge(pv_done, N["unit"] + u + 1 + ONE)
            a.activation(ot[:, :], pv_bank, ACT.Copy).then_inc(ot_ready, 1)

        def dve_job(v, w, cnt, N, job, bn):
            if job == "stats":
                ln_stats(v, N["b"], N["ln"], x, N["x_ready"])
            elif job == "norm":
                ln_norm(v, N["b"], N["ln"], None, x, w["moe"])
            elif job == "v":
                v.wait_ge(bank_full, bn + 1)
                v.tensor_tensor(va[N["par"]][:, :, :, 0:DH],
                                shared_t.rearrange("p i (h e) -> p i h e", e=DH),
                                bvb[:, w["n"]:w["n"] + 1, :].rearrange("p o (h e) -> p o h e", e=DH)
                                .broadcast_to([P, TB, H, DH]), ALU.add).then_inc(bank_free, 1)
            elif job in ("o0", "o1", "o2", "o3"):
                g = int(job[1])
                v.wait_ge(bank_full, bn + 1)
                o4 = shared_t.rearrange("p i (j e) -> p i j e", e=32)
                v.reciprocal(rc[:, :, :], o4[:, :, :, DH]).then_inc(rc_done, 1)
                v.wait_ge(rc_done, N["ot"] - ONE + g + 1)
                v.tensor_tensor(on[:, :, 32 * g:32 * g + 32].rearrange("p i (j e) -> p i j e", e=DH),
                                o4[:, :, :, 0:DH],
                                rc[:, :, :].rearrange("p i (j o) -> p i j o", o=1).broadcast_to([P, TB, 4, DH]),
                                ALU.mult).then_inc(bank_free, 1)
            elif job == "out":
                bo = bob[:, w["n"]:w["n"] + 1, :].broadcast_to([P, TB, P])
                dst = tiles(res if w["moe"] else x, N["b"])
                v.wait_ge(bank_full, bn + 1)
                v.tensor_tensor(upd[:, :, :], shared_t, bo, ALU.add).then_inc(bank_free, 1)
                v.wait_ge(bank_free, bn + 1)
                if w["moe"]:
                    v.wait_ge(h_kept, N["kept"] + TB)
                if w["nan_guard"]:
                    v.tensor_scalar(upd2[:, :, :], upd[:, :, :], 0.0, None, ALU.max).then_inc(guard_done, 1)
                    v.wait_ge(guard_done, N["b"] * 2 + 1)
                    v.scalar_tensor_tensor(upd[:, :, :], upd[:, :, :], 0.0, upd2[:, :, :], ALU.min,
                                           ALU.add).then_inc(guard_done, 1)
                    v.wait_ge(guard_done, N["b"] * 2 + 2)
                v.tensor_tensor(dst, dst, upd[:, :, :], ALU.add).then_inc(x_done, 1)
                v.wait_ge(x_done, N["xd"] + 1)

        def pool_job(g_, w, cnt, N, job, bn):
            if job == "norm":
                ln_pool(g_, N["ln"], w["moe"])
            elif job in ("q", "k"):
                c_ = 0 if job == "q" else 1
                n = N["prep"] * 6 + 3 * c_
                apart(g_, hi_done, N["prep"] * 2 + c_ + 1)
                g_.tensor_tensor(rem[:, c_, :], q32[:, c_, :], parts[:, c_, 0, :], ALU.subtract).then_inc(split_done, 1)
                apart(g_, split_done, n + 1)
                g_.tensor_copy(parts[:, c_, 1, :], rem[:, c_, :]).then_inc(split_done, 1)
                apart(g_, split_done, n + 2)
                g_.tensor_tensor(parts[:, c_, 2, :], rem[:, c_, :], parts[:, c_, 1, :],
                                 ALU.subtract).then_inc(split_done, 1)
            elif job[0] == "m":
                split_max(g_, N, int(job[1]), bn)
                store_max(g_, N, int(job[1]), bn)

        def walk(eng, w, cnt, pair, par, scores, job_fn, unit_end=None):
            b = pair * 2 + par
            N, after = numbers(cnt, b, par), numbers(cnt, b + 1, 1 - par)
            before = numbers(cnt, pair * 2, 0) if par else None
            for u in range(UNITS):
                for k in range(4):
                    if scores:
                        scores(before, N, after, u, k)
                    for job in PLANS[par].get((u, k), []):
                        name = job.rstrip("+-")
                        at = "hT+" if name in NOBANK else job
                        job_fn(eng, w, cnt, {"+": after, "-": before}.get(job[-1], N), name,
                               bank_number(cnt, pair, par, at))
                if unit_end:
                    unit_end(before, N, u)
            return N

        def head(eng, w, cnt, job_fn):
            N = numbers(cnt, 0, 0)
            for name in HEADJOBS:
                at = "hT" if name in NOBANK else name
                job_fn(eng, w, cnt, N, name, cnt["bank"] + BANKHEAD.index(at))
            return N

        def lead_of(N, M, u):
            h = u + LEAD
            return (N, h // 2, h % 2) if h < UNITS else (M, (h - UNITS) // 2, h % 2)

        def attention_pe(pe, w, cnt):
            wait(pe, y_free, cnt["y"])
            N0 = head(pe, w, cnt, pe_job)
            pe.wait_ge(qk_loaded, (N0["prep"] + 1) * STACKED)
            for h in range(LEAD):
                for r in range(8):
                    if (h, r) == (2, 6):
                        pe_job(pe, w, cnt, N0, "m0", cnt["bank"] + BANKHEAD.index("m0"))
                    pass1_tile(pe, w, N0, h // 2, h % 2, r)

            def scores(before, N, after, u, k):
                L, g, hf = lead_of(N, after, u)
                if k == 0 and hf == 0 and g == 0:
                    pe.wait_ge(qk_loaded, (L["prep"] + 1) * STACKED)
                pass1_tile(pe, w, L, g, hf, 2 * k)
                pass2_slot(pe, w, N, u, k)
                pass1_tile(pe, w, L, g, hf, 2 * k + 1)
                for back, piece in PV_AT[u % 2].get(k, []):
                    if u >= back:
                        pv_piece(pe, w, N, u - back, piece)
                    elif before:
                        pv_piece(pe, w, before, u - back + UNITS, piece)

            with pe.Fori(0, NB // 2) as pair:
                for par in range(2):
                    N = walk(pe, w, cnt, pair, par, scores, pe_job)
                for u, piece in PV_LEFT:
                    pv_piece(pe, w, N, u, piece)
                for job in TAIL:
                    pe_job(pe, w, cnt, N, job, bank_number(cnt, pair, 1, job))

        def attention_dve(v, w, cnt):
            N0 = head(v, w, cnt, dve_job)
            wait(v, m_parts, N0["quad"] * 4)
            for h in range(LEAD):
                for r in range(8):
                    rowmax_tile(v, w, N0, h // 2, h % 2, r)

            def scores(before, N, after, u, k):
                L, g, hf = lead_of(N, after, u)
                for r in (2 * k, 2 * k + 1):
                    if k == 0 and r == 0 and hf == 0:
                        wait(v, m_parts, (L["quad"] + g - 1) * 4)
                    rowmax_tile(v, w, L, g, hf, r)

            with v.Fori(0, NB // 2) as pair:
                for par in range(2):
                    N = walk(v, w, cnt, pair, par, scores, dve_job)
                for job in TAIL:
                    dve_job(v, w, cnt, N, job, bank_number(cnt, pair, 1, job))

        def attention_act(a, w, cnt):
            N0 = head(a, w, cnt, act_job)
            act_job(a, w, cnt, N0, "m0", cnt["bank"] + BANKHEAD.index("m0"))

            def scores(before, N, after, u, k):
                exp_slot(a, w, N, u, k)

            def unit_end(before, N, u):
                if u % 2 == 0 and u > 0:
                    ot_copy(a, N, u - 1)
                elif u == 0 and before:
                    ot_copy(a, before, UNITS - 1)

            with a.Fori(0, NB // 2) as pair:
                for par in range(2):
                    N = walk(a, w, cnt, pair, par, scores, act_job, unit_end)
                ot_copy(a, N, UNITS - 1)
                for job in TAIL:
                    act_job(a, w, cnt, N, job, bank_number(cnt, pair, 1, job))

        def attention_pool(g_, w, cnt):
            N0 = head(g_, w, cnt, pool_job)
            pool_job(g_, w, cnt, N0, "m0", cnt["bank"] + BANKHEAD.index("m0"))
            with g_.Fori(0, NB // 2) as pair:
                for par in range(2):
                    walk(g_, w, cnt, pair, par, None, pool_job)

        def stack(sp, N, par, quads):
            wait(sp, m_loaded, quads * 32)
            for c_, which in ((0, QPART), (1, KPART)):
                sp.wait_ge(split_done, N * 6 + 3 * c_ + 3)
                for s in range(2):
                    if c_ == 0:
                        sp.dma_start(qs[par][64 * s + KROWS:64 * s + KROWS + MROWS, s, :, :],
                                     mzero[:, :].rearrange("p (o c) -> p o c", o=1)
                                     .broadcast_to([MROWS, UNITS, S])).then_inc(qk_loaded, 16)
                    for p_ in range(NPROD):
                        r0 = 64 * s + DH * p_
                        dst = qs[par][r0:r0 + DH, s] if c_ == 0 else ks[par][r0:r0 + DH]
                        sp.dma_start(dst, parts[64 * s:64 * s + 64, c_, which[p_], :]).then_inc(qk_loaded, 16)

        def attention_sync(sp, cnt):
            stack(sp, cnt["prep"], 0, cnt["quad"])
            with sp.Fori(0, NB // 2) as i:
                for par in range(2):
                    stack(sp, i * 2 + par + 1 + cnt["prep"], 1 - par, (i * 2 + par) * 4 + max(cnt["quad"], 1))

        def over_tiles(eng, tile_fn):
            for t in range(3):
                tile_fn(t, t % 2, t // 2)
            with eng.Fori(0, (SLOTS - 3) // 2) as i:
                tile_fn(i * 2 + 3, 1, i + 1)
                tile_fn(i * 2 + 4, 0, i + 2)

        def moe_pe(pe, cnt):
            m = cnt["moe"]
            turn_everything(pe, cnt)
            for b in range(NB):
                pe.wait_ge(hta_done, cnt["tr"] + b + 1)
                for i in range(TB):
                    j = b * TB + i
                    ins = pe.matmul(ps[:, 0, j * E:(j + 1) * E], hTa_moe[:, b, i * P:(i + 1) * P], gw[:, :],
                                    start=True, stop=True)
            ins.then_inc(logits_ready, 1)
            pe.wait_ge(route, m * ROUTE + 6)
            pe.matmul(ps[:, 1, 0:TILES * E], earlier[:, :], ohb[:, :, :], start=True, stop=False, skip_group_check=True)
            for j in range(TILES):
                ins = pe.matmul(ps[:, 1, (j + 1) * E:(TILES + 1) * E], onesb[:, :],
                                ohb[:, j:j + 1, :].broadcast_to([P, TILES - j, E]), start=False,
                                stop=(j == TILES - 1), skip_group_check=True)
            ins.then_inc(rank_ready, 1)
            pe.wait_ge(xs_loaded, 16 * (m + 1))

            def one_tile(t, par, _):
                wait(pe, tile_in, t + m * SLOTS)
                pe.wait_ge(tile_copied, t + (m * (SLOTS + 1) + 1))
                pe.transpose(ps[:, 6, 0:P], xst[:, par, :], identf[:, :]).then_inc(tile_turned, 1)
                if not isinstance(t, int) or t > 0:
                    down_before(t, 1 - par)
                pe.wait_ge(tile_in, t + (m * SLOTS + 1))
                pe.wait_ge(expert_ready, t + (m * SLOTS + 1))
                for a in range(FB):
                    pe.matmul(ps[:, a, 0:P], we[:, par, a * P:(a + 1) * P], hTm[:, par, :], start=True,
                              stop=True).then_inc(up_ready, 1)

            def down_before(t, par):
                wait(pe, y_ready, t + (m * SLOTS - 2 + ONE))
                for a in range(FB):
                    pe.wait_ge(relu_done, t * FB + (cnt["relu"] + a + 1 - FB))
                    ins = pe.matmul(ps[:, 4 + par, 0:P], mid_e[:, par, a, :],
                                    we[:, par, F + a * P:F + (a + 1) * P], start=(a == 0), stop=(a == FB - 1))
                ins.then_inc(tile_down, 1)

            over_tiles(pe, one_tile)
            down_before(SLOTS, (SLOTS - 1) % 2)

        def moe_act(a, cnt):
            m = cnt["moe"]
            for b in range(NB):
                a.wait_ge(ln_turned, cnt["tr"] + b + 1)
                a.activation(hTa_moe[:, b, :], ps[:, 4 + b, :], ACT.Identity, bias=gcol[:, 3:4],
                             scale=gcol[:, 2:3]).then_inc(hta_done, 1)

            def copy_tile(t, par):
                a.activation(xst[:, par, :], ptf[:, bass.ds(t * ROW, P)], ACT.Copy).then_inc(tile_copied, 1)

            a.wait_ge(xs_loaded, 16 * (m + 1))
            copy_tile(0, 0)

            def one_tile(t, par, _):
                a.wait_ge(tile_turned, t + (m * SLOTS + 1))
                a.activation(hTm[:, par, :], ps[:, 6, 0:P], ACT.Identity, bias=gcol[:, 3:4],
                             scale=gcol[:, 2:3]).then_inc(tile_in, 1)
                copy_tile(t + 1, 1 - par)
                for fb in range(FB):
                    a.wait_ge(up_ready, t * FB + (cnt["up"] + fb + 1))
                    a.activation(mid_e[:, par, fb, :], ps[:, fb, 0:P], ACT.Relu,
                                 bias=we[:, par, 2 * F + fb:2 * F + fb + 1]).then_inc(relu_done, 1)

            over_tiles(a, one_tile)

        ROUTE = 16

        def moe_dve(v, cnt):
            m = cnt["moe"]
            steps = [m * ROUTE]

            def step(ins):
                ins.then_inc(route, 1)
                steps[0] += 1
                v.wait_ge(route, steps[0])

            def over_e(t):
                return t[:, :].rearrange("p (i o) -> p i o", o=1).broadcast_to([P, TILES, E])

            ln_everything(v, cnt, res)
            v.wait_ge(logits_ready, m + 1)
            step(v.tensor_tensor(logit[:, :, :], ps[:, 0, 0:TILES * E].rearrange("p (i e) -> p i e", e=E),
                                 gbb[:, :].rearrange("p (o e) -> p o e", o=1).broadcast_to([P, TILES, E]), ALU.add))
            step(v.tensor_reduce(lmax[:, :], logit[:, :, :], AX, ALU.max))
            step(v.tensor_tensor(score[:, :, :], logit[:, :, :], over_e(lmax), ALU.is_equal))
            step(v.tensor_tensor(score[:, :, :], score[:, :, :], pref[:, :, :], ALU.mult))
            step(v.tensor_reduce(smax[:, :], score[:, :, :], AX, ALU.max))
            step(v.tensor_tensor(ohb[:, :, :], score[:, :, :], over_e(smax), ALU.is_equal))
            assert steps[0] == m * ROUTE + 6
            v.wait_ge(rank_ready, m + 1)
            total = ps[:, 1, TILES * E:(TILES + 1) * E]
            step(v.scalar_tensor_tensor(more[:, :, :],
                                        total.rearrange("p (e o) -> p e o", o=1).broadcast_to([P, E, TILES]), 1.0 / P,
                                        count[:, 0:TILES].rearrange("p (o k) -> p o k", o=1)
                                        .broadcast_to([P, E, TILES]), ALU.mult, ALU.is_gt))
            step(v.tensor_reduce(ntile[:, :], more[:, :, :], AX, ALU.add))
            step(v.tensor_tensor(more[:, :, 0:E], lower_e[:, :, :],
                                 ntile[:, :].rearrange("p (o e) -> p o e", o=1).broadcast_to([P, E, E]), ALU.mult))
            step(v.tensor_reduce(first[:, :], more[:, :, 0:E], AX, ALU.add))
            step(v.scalar_tensor_tensor(score[:, :, :],
                                        first[:, :].rearrange("p (o e) -> p o e", o=1).broadcast_to([P, TILES, E]),
                                        float(P), ps[:, 1, 0:TILES * E].rearrange("p (i e) -> p i e", e=E),
                                        ALU.mult, ALU.add))
            step(v.tensor_tensor(logit[:, :, :], score[:, :, :], ohb[:, :, :], ALU.mult))
            step(v.tensor_reduce(posf[:, :], logit[:, :, :], AX, ALU.add))
            step(v.tensor_copy(pos[:, :], posf[:, :]))
            v.tensor_tensor(last_e[:, :], first[:, :], ntile[:, :], ALU.add).then_inc(route, 1)
            v.wait_ge(route, m * ROUTE + 15)
            v.tensor_tensor(owner_c[:, :, :], count[0:1, :].rearrange("p (t o) -> p t o", o=1)
                            .broadcast_to([1, SLOTS, E - 1]),
                            last_e[0:1, 0:E - 1].rearrange("p (o e) -> p o e", o=1).broadcast_to([1, SLOTS, E - 1]),
                            ALU.is_ge).then_inc(owner_step, 1)
            v.wait_ge(owner_step, m * 3 + 1)
            v.tensor_reduce(ownerf[:, :], owner_c[:, :, :], AX, ALU.add).then_inc(owner_step, 1)
            v.wait_ge(owner_step, m * 3 + 2)
            v.tensor_copy(owner[:, :], ownerf[:, :]).then_inc(owner_step, 1)
            v.scalar_tensor_tensor(x[:, 0:TILES, :], res[:, 0:TILES, :], 0.5, x[:, 0:TILES, :], ALU.mult,
                                   ALU.add).then_inc(route, 1)
            v.wait_ge(owner_step, m * 3 + 3)

            def output_before(t, par, half):
                v.wait_ge(tile_down, t + (m * SLOTS + ONE))
                wait(v, y_sent[par], half * 16 + (m * ((SLOTS + 1 - par) // 2) * 16))
                v.tensor_copy(numbers_y[:, par:par + 1],
                              xs[:, bass.ds(t - 1, 1), P:ROW].bitcast(U32).rearrange("p o c -> p (o c)"))
                v.tensor_tensor(ysb[:, par, :], ps[:, 4 + par, 0:P], we[:, par, 2 * F + FB:WE],
                                ALU.add).then_inc(y_ready, 1)

            def one_tile(t, par, half):
                e = v.value_load(owner[0:1, bass.ds(t, 1)], min_val=0, max_val=E - 1)
                wait(v, y_ready, t + (m * SLOTS - 1 + ONE))
                v.tensor_copy(we[:, par, :], experts[:, bass.ds(e, 1), :]
                              .rearrange("p o c -> p (o c)")).then_inc(expert_ready, 1)
                if not isinstance(t, int) or t > 0:
                    output_before(t, 1 - par, half - 1 + par)

            v.wait_ge(xs_loaded, 16 * (m + 1))
            over_tiles(v, one_tile)
            output_before(SLOTS, (SLOTS - 1) % 2, (SLOTS - 1) // 2)
            v.wait_ge(route, (m + 1) * ROUTE)
            for b in range(NB):
                v.wait_ge(y_loaded[b], 16 * (m + 1))
                v.scalar_tensor_tensor(tiles(x, b), tiles(yall, b), 0.5, tiles(x, b), ALU.mult,
                                       ALU.add).then_inc(x_done, 1)
            v.wait_ge(x_done, cnt["xd"] + NB)

        def moe_pool(g_, cnt):
            m = cnt["moe"]
            ln_pool(g_, cnt["ln"], False, NB)
            g_.tensor_copy(lnall[:, :, P:ROW].bitcast(U32).rearrange("p a o -> p (a o)"),
                           numbers_t[:, :]).then_inc(numbered, 1)
            g_.wait_ge(numbered, m + 1)
            g_.wait_ge(route, m * ROUTE + 14)
            g_.wait_ge(prefilled, 32)
            for j in range(TILES):
                g_.indirect_dma_start(d["sorted"][m], bass.IndirectOffsetOnAxis(pos[:, j:j + 1], 0), lnall[:, j, :],
                                      None).then_inc(rows_sorted, 16)

            def one_tile(t, par, _):
                apart(g_, y_ready, t + (m * SLOTS + 1 + ONE))
                g_.indirect_dma_start(d["y_rows"][m], bass.IndirectOffsetOnAxis(numbers_y[:, par:par + 1], 0),
                                      ysb[:, par, :], None).then_inc(y_sent[par], 16)

            over_tiles(g_, one_tile)

        def moe_sync(sp, cnt):
            m = cnt["moe"]
            sp.wait_ge(rows_sorted, (m + 1) * TILES * 16)
            sp.dma_start(xs[:, :, :], d["sorted"][m].rearrange("(t p) c -> p t c", p=P)).then_inc(xs_loaded, 16)
            for par in range(2):
                sp.wait_ge(y_sent[par], (m + 1) * ((SLOTS + 1 - par) // 2) * 16)
            for b in range(NB):
                sp.dma_start(tiles(yall, b), d["y_rows"][m][b * S:(b + 1) * S, :]
                             .rearrange("(t p) c -> p t c", p=P)).then_inc(y_loaded[b], 16)

        def ffn_pe(pe, cnt):
            turn_everything(pe, cnt)
            pe.wait_ge(hta_done, cnt["tr"] + NB)
            with pe.Fori(0, NB) as b:
                m0 = b * FB + cnt["mid"]
                wait(pe, y_free, b + cnt["y"])

                def down(n):
                    pe.wait_ge(mid_done, m0 + n + 1)
                    for i in range(TB):
                        ins = pe.matmul(ps[:, 6, i * P:(i + 1) * P], mid[:, n, i * P:(i + 1) * P], wo2[:, n, :],
                                        start=(n == 0 and i == 0), stop=(n == FB - 1), skip_group_check=True)
                    ins.then_inc(down_done, 1)

                for n in range(FB):
                    for kx in range(TOPK):
                        if kx == 0:
                            wait(pe, relu_done, b * FB + (cnt["relu"] + max(n - 1, 0)))
                        else:
                            wait(pe, fold_done, b * FB + (cnt["fold"] + max(n - 1, 0)))
                        pe.matmul(ps[:, (2 * n + kx) % 4, :], wk[:, kx, n * P:(n + 1) * P], hTa[:, b, :], start=True,
                                  stop=True).then_inc(up_ready, 1)
                    if n >= 1:
                        down(n - 1)
                down(FB - 1)

        def ffn_act(a, cnt):
            for b in range(NB):
                a.wait_ge(ln_turned, cnt["tr"] + b + 1)
                a.activation(hTa[:, b, :], ps[:, 4 + b, :], ACT.Copy).then_inc(hta_done, 1)
            with a.Fori(0, NB) as b:
                for n in range(FB):
                    a.wait_ge(up_ready, b * (FB * TOPK) + (cnt["up"] + 2 * n + 1))
                    wait(a, mid_done, b * FB + (cnt["mid"] + max(n - 1, 0)))
                    a.activation(relu[:, n % 2, :], ps[:, (2 * n) % 4, :], ACT.Relu).then_inc(relu_done, 1)

        def ffn_dve(v, cnt):
            ln_everything(v, cnt, x)
            with v.Fori(0, NB) as b:
                for n in range(FB):
                    v.wait_ge(up_ready, b * (FB * TOPK) + (cnt["up"] + 2 * n + 2))
                    wait(v, mid_done, b * FB + (cnt["mid"] + max(n - 1, 0)))
                    v.tensor_scalar(fold[:, n % 2, :], ps[:, (2 * n + 1) % 4, :], 0.0, tkv[:, 1:2], ALU.max,
                                    ALU.mult).then_inc(fold_done, 1)
                    v.wait_ge(fold_done, b * FB + (cnt["fold"] + n + 1))
                    v.wait_ge(relu_done, b * FB + (cnt["relu"] + n + 1))
                    wait(v, down_done, b * FB + (cnt["mid"] + max(n - 3, 0)))
                    v.scalar_tensor_tensor(mid[:, n, :], relu[:, n % 2, :], tkv[:, 0:1], fold[:, n % 2, :], ALU.mult,
                                           ALU.add).then_inc(mid_done, 1)
                v.wait_ge(down_done, b * FB + (cnt["mid"] + FB))
                v.scalar_tensor_tensor(tiles(x, b), ps[:, 6, :].rearrange("p (i c) -> p i c", c=P), 0.5, tiles(x, b),
                                       ALU.mult, ALU.add).then_inc(y_free, 1)
                v.wait_ge(y_free, b + (cnt["y"] + 1))
                v.sem_inc(x_done, 1)

        def ffn_pool(g_, cnt):
            ln_pool(g_, cnt["ln"], False, NB)

        loads = [(x[:, 0:TB * NB, :], d["L0_attn_x"].rearrange("b (i p) d -> p (b i) d", p=P))]
        wl = []
        for j, n in enumerate(("L0_ffn_wq", "L0_ffn_wk", "L0_ffn_wv", "L0_ffn_wo", "L0_attn_W_q", "L0_attn_W_k",
                               "L0_attn_W_v", "L0_attn_W_o")):
            wl.append((wraw[:, j, :], d[n]))
        wl.append((wraw[:, 8:11, :], d["L1_attn_w_in"].rearrange("(a p) d -> p a d", p=P)))
        wl.append((wraw[:, 11, :], d["L1_attn_w_out"]))
        b_in = d["L1_attn_b_in"]
        for c_, v_ in enumerate((d["L0_ffn_bq"], d["L0_ffn_bk"], d["L0_attn_b_q"], d["L0_attn_b_k"], b_in[0:P],
                                 b_in[P:2 * P])):
            o = v_.rearrange("(t s e) -> s e t", s=2, e=DH)
            for s in range(2):
                wl.append((bcol[64 * s:64 * s + 64, c_:c_ + 1], o[s]))
        for j, v_ in enumerate((d["L0_ffn_bv"], d["L0_attn_b_v"], b_in[2 * P:3 * P])):
            wl.append((bvb[:, j, :], v_.partition_broadcast(P)))
        for j, v_ in enumerate((d["L0_ffn_bo"], d["L0_attn_b_o"], d["L1_attn_b_out"])):
            wl.append((bob[:, j, :], v_.partition_broadcast(P)))
        for j, n in enumerate(("L0_ffn_ln1_g", "L0_ffn_ln1_b", "L0_ffn_ln2_g", "L0_ffn_ln2_b")):
            wl.append((gcol[:, j:j + 1], d[n].rearrange("(p o) -> p o", o=1)))
        wl += [
            (experts[:, :, 0:F], d["L0_ffn_w1"].rearrange("e p f -> p e f")),
            *[(experts[:, :, F + a * P:F + (a + 1) * P], d["L0_ffn_w2"][:, a * P:(a + 1) * P, :].rearrange("e p h -> p e h"))
              for a in range(FB)],
            *[(experts[:, :, 2 * F + a:2 * F + a + 1], d["L0_ffn_b1"][:, a * P:(a + 1) * P].rearrange("e (p o) -> p e o", o=1))
              for a in range(FB)],
            (experts[:, :, 2 * F + FB:WE], d["L0_ffn_b2"].partition_broadcast(P)),
            (gw[:, :], d["L0_ffn_gate_w"]),
            (gbb[:, :], d["L0_ffn_gate_b"].partition_broadcast(P)),
            (wi_raw[:, :, :], d["L1_ffn_wi_w"].rearrange("(a p) h -> p a h", p=P)),
            (wo_raw[:, :], d["L1_ffn_wo_w"]),
            (tkv[:, :], d["L1_ffn_top_k_values"].partition_broadcast(P)),
        ]
        NCONST = 33

        @block.sync
        def _(sp):
            sp.dma_start(*loads[0]).then_inc(x_loaded, 16)
            sp.dma_start(idx[:, :], d["L1_ffn_top_k_indices"].rearrange("(o k) -> o k", o=1)).then_inc(idx_loaded, 16)
            for dst, src in wl:
                sp.dma_start(dst, src, allow_slow_non_contiguous=True).then_inc(w_loaded, 16)
            sp.wait_ge(idx_loaded, 16)
            for kx in range(TOPK):
                which = sp.value_load(idx[0:1, kx:kx + 1], min_val=0, max_val=E - 1)
                sp.dma_start(loA[:, kx, :], d["L1_ffn_lora_As"][bass.ds(which, 1), :, :]
                             .rearrange("o r h -> (o r) h")).then_inc(lora_loaded, 16)
                sp.dma_start(loB[:, kx, :, :], d["L1_ffn_lora_Bs"][bass.ds(which, 1), :, :]
                             .rearrange("o (a p) r -> p (o a) r", p=P)).then_inc(lora_loaded, 16)
            sp.wait_ge(const_done, NCONST)
            for m in range(2):
                sp.dma_start(d["sorted"][m].rearrange("(t p) c -> p t c", p=P), padding).then_inc(prefilled, 16)
            for kind, w, cnt in phases:
                if kind == "attn":
                    attention_sync(sp, cnt)
                elif kind == "moe":
                    moe_sync(sp, cnt)
            last = phases[-1][2]
            out_t = d["out"].rearrange("b (i p) h -> b p i h", p=P)
            for b in range(NB):
                sp.wait_ge(x_done, last["xd"] + b + 1)
                sp.dma_start(out_t[b], tiles(x, b)).then_inc(out_done, 16)
            sp.wait_ge(out_done, 16 * NB)
            sp.wait_ge(qk_loaded, c["prep"] * STACKED)

        @block.gpsimd
        def _(g_):
            done = [0]

            for s in credited:
                g_.sem_inc(s, ONE)

            def const(ins):
                done[0] += 1
                ins.then_inc(const_done, 1)

            const(g_.memset(identf[:, :], 0.0))
            const(g_.memset(identb[:, :], 0.0))
            const(g_.memset(mask_q[:, :], 0.0))
            const(g_.memset(mask_k[:, :], 0.0))
            const(g_.memset(padding, 0.0))
            const(g_.memset(earlier[:, :], 0.0))
            const(g_.memset(lower_e[:, :, :], 0.0))
            for i in range(2):
                const(g_.memset(va[i][:, :, :, :], 0.0))
                const(g_.memset(ks[i][:, :, :], 1.0))
                const(g_.memset(qs[i][:, :, :, :].rearrange("p s t c -> p (s t c)").bitcast(F32), 0.0))
            const(g_.memset(mzero[:, :], 0.0))
            g_.wait_ge(const_done, 14)
            const(g_.affine_select(out=identf[:, :], in_=identf[:, :], compare_op=ALU.not_equal, fill=1.0, base=0,
                                   pattern=[[-1, P]], channel_multiplier=1))
            const(g_.affine_select(out=identb[:, :], in_=identb[:, :], compare_op=ALU.not_equal, fill=1.0, base=0,
                                   pattern=[[-1, P]], channel_multiplier=1))
            const(g_.affine_select(out=mask_q[:, :], in_=mask_q[:, :], compare_op=ALU.is_ge, fill=MASKED, base=0,
                                   pattern=[[-1, P]], channel_multiplier=1))
            const(g_.affine_select(out=mask_k[:, :], in_=mask_k[:, :], compare_op=ALU.is_ge, fill=MASKED, base=0,
                                   pattern=[[1, P]], channel_multiplier=-1))
            const(g_.affine_select(out=earlier[:, :], in_=earlier[:, :], compare_op=ALU.is_ge, fill=1.0, base=0,
                                   pattern=[[-1, P]], channel_multiplier=1))
            const(g_.affine_select(out=lower_e[:, :, :], in_=lower_e[:, :, :], compare_op=ALU.is_ge, fill=1.0, base=0,
                                   pattern=[[-1, E], [1, E]], channel_multiplier=0))
            const(g_.iota(padding[:, :, P:ROW].bitcast(U32).rearrange("p a o -> p (a o)"), pattern=[[P, SLOTS]],
                          base=TILES * P, channel_multiplier=1))
            const(g_.iota(numbers_t[:, :], pattern=[[P, TILES]], base=0, channel_multiplier=1))
            const(g_.memset(onesb[:, :], 1.0))
            const(g_.iota(count_i[:, :], pattern=[[1, SLOTS]], base=0, channel_multiplier=0))
            for i in range(2):
                const(g_.memset(va[i][:, :, :, DH:DH + 1], 1.0))
            const(g_.memset(minus_half[:, :], -0.5))
            const(g_.memset(x[:, TB * NB:NT, :], 0.0))
            const(g_.memset(ones_col[:, :], 1.0))
            const(g_.memset(zero_col[:, :], 0.0))
            const(g_.iota(pref_i[:, :, :], pattern=[[0, TILES], [-1, E]], base=E, channel_multiplier=0))
            g_.wait_ge(const_done, done[0])
            const(g_.tensor_copy(pref[:, :, :], pref_i[:, :, :]))
            const(g_.tensor_copy(count[:, :], count_i[:, :]))
            assert done[0] == NCONST
            g_.wait_ge(const_done, NCONST)
            for kind, w, cnt in phases:
                if kind == "attn":
                    attention_pool(g_, W[w], cnt)
                elif kind == "moe":
                    moe_pool(g_, cnt)
                else:
                    ffn_pool(g_, cnt)
            apart(g_, m_loaded, c["quad"] * 32)

        @block.vector
        def _(v):
            v.wait_ge(const_done, NCONST)
            v.wait_ge(x_loaded, 16)
            v.wait_ge(w_loaded, 16 * len(wl))
            bn = 0

            def leave(dst, src=shared):
                nonlocal bn
                v.wait_ge(bank_full, bn + 1)
                v.tensor_copy(dst, src).then_inc(bank_free, 1)
                bn += 1

            leave(wT[:, :, :].rearrange("p a c -> p (a c)"))
            v.wait_ge(bank_free, 1)
            v.tensor_copy(bcols[:, :], bcol[:, :]).then_inc(set_dve, 1)
            v.wait_ge(set_dve, 1)
            v.tensor_scalar(bcols[:, 0:6:2], bcol[:, 0:6:2], SCALE, None, ALU.mult).then_inc(set_dve, 1)
            for j, src in enumerate((wraw[:, 0, :], wraw[:, 1, :], wraw[:, 4, :], wraw[:, 5, :], wT[:, 0, :],
                                     wT[:, 1, :])):
                v.tensor_copy(wperm[:, j, :].rearrange("p (s e t) -> p s e t", s=2, e=DH),
                              src.rearrange("p (t s e) -> p s e t", s=2, e=DH)).then_inc(set_dve, 1)
            leave(wiT[:, :])
            leave(wo2[:, :, :].rearrange("p a c -> p (a c)"))
            for kx in range(TOPK):
                leave(loBT[:, kx, :], shared[0:RANK, :])
            for kx in range(TOPK):
                v.wait_ge(bank_full, bn + 1)
                v.tensor_tensor(wk[:, kx, :], shared, wiT[:, :], ALU.add).then_inc(bank_free, 1)
                bn += 1
            assert bn == SETUP_BANK
            for kind, w, cnt in phases:
                if kind == "attn":
                    attention_dve(v, W[w], cnt)
                elif kind == "moe":
                    moe_dve(v, cnt)
                else:
                    ffn_dve(v, cnt)

        SET_DVE = 2 + 6

        @block.scalar
        def _(a):
            a.wait_ge(const_done, NCONST)
            a.wait_ge(w_loaded, 16 * len(wl))
            a.wait_ge(set_dve, SET_DVE)
            a.wait_ge(prefilled, 32)
            for kind, w, cnt in phases:
                if kind == "attn":
                    attention_act(a, W[w], cnt)
                elif kind == "moe":
                    moe_act(a, cnt)
                else:
                    ffn_act(a, cnt)

        @block.tensor
        def _(pe):
            pe.wait_ge(const_done, NCONST)
            pe.wait_ge(w_loaded, 16 * len(wl))
            bn = 0

            def flip(pairs):
                nonlocal bn
                wait(pe, bank_free, bn)
                for dst, src in pairs:
                    ins = pe.transpose(dst, src, identf[:, :])
                ins.then_inc(bank_full, 1)
                bn += 1

            flip([(shared_t[:, i, :], wraw[:, 8 + i, :]) for i in range(4)])
            flip([(shared_t[:, i, :], wi_raw[:, i, :]) for i in range(FB)])
            flip([(shared_t[:, i, :], wo_raw[:, i * P:(i + 1) * P]) for i in range(FB)])
            pe.wait_ge(lora_loaded, 16 * 2 * TOPK)
            for kx in range(TOPK):
                flip([(shared_t[0:RANK, i, :], loB[:, kx, i, :]) for i in range(FB)])
            for kx in range(TOPK):
                wait(pe, bank_free, bn)
                pe.matmul(shared, loA[:, kx, :], loBT[:, kx, :], start=True, stop=True).then_inc(bank_full, 1)
                bn += 1
            pe.wait_ge(set_dve, SET_DVE)
            for kind, w, cnt in phases:
                if kind == "attn":
                    attention_pe(pe, W[w], cnt)
                elif kind == "moe":
                    moe_pe(pe, cnt)
                else:
                    ffn_pe(pe, cnt)


NAMES = ["L0_attn_x", "L0_attn_W_q", "L0_attn_b_q", "L0_attn_W_k", "L0_attn_b_k", "L0_attn_W_v", "L0_attn_b_v",
         "L0_attn_W_o", "L0_attn_b_o", "L0_ffn_ln1_g", "L0_ffn_ln1_b", "L0_ffn_ln2_g", "L0_ffn_ln2_b", "L0_ffn_wq",
         "L0_ffn_bq", "L0_ffn_wk", "L0_ffn_bk", "L0_ffn_wv", "L0_ffn_bv", "L0_ffn_wo", "L0_ffn_bo", "L0_ffn_gate_w",
         "L0_ffn_gate_b", "L0_ffn_w1", "L0_ffn_b1", "L0_ffn_w2", "L0_ffn_b2", "L1_attn_w_in", "L1_attn_b_in",
         "L1_attn_w_out", "L1_attn_b_out", "L1_ffn_wi_w", "L1_ffn_wo_w", "L1_ffn_lora_As", "L1_ffn_lora_Bs",
         "L1_ffn_top_k_indices", "L1_ffn_top_k_values"]


def kernel(**inputs):
    import concourse.bacc as bacc
    import numpy as np
    from concourse.bass_utils import run_bass_kernel_spmd

    nc = bacc.Bacc("TRN2", target_bir_lowering=False, num_devices=1)
    arrays, d = {}, {}
    for name in NAMES:
        a = np.ascontiguousarray(inputs[name])
        arrays[f"in_{name}"] = a
        d[name] = nc.dram_tensor(f"in_{name}", a.shape, mybir.dt.from_np(a.dtype), kind="ExternalInput").ap()
    shape = inputs["L0_attn_x"].shape
    for name, rows, cols in (("sorted", SLOTS * P, ROW), ("y_rows", (TILES + SLOTS) * P, P)):
        d[name] = [nc.dram_tensor(f"{name}{m}", (rows, cols), F32, kind="Internal").ap() for m in range(2)]
    d["out"] = nc.dram_tensor("out_dram", shape, F32, kind="ExternalOutput").ap()
    program(nc, d)
    return run_bass_kernel_spmd(nc, [arrays], core_ids=[0]).results[0]["out_dram"]
```

```python
from contextlib import ExitStack

import concourse.bass as bass
from concourse import mybir

F32 = mybir.dt.float32
BF16 = mybir.dt.bfloat16
I32 = mybir.dt.int32
U32 = mybir.dt.uint32
ALU = mybir.AluOpType
ACT = mybir.ActivationFunctionType
AX = mybir.AxisListType.X

P = 128
NB, S = 4, 512
TB = S // P
H, DH = 16, 8
E, F = 8, 512
FB = F // P
TOPK = 2
RANK = 16
EPS = 1e-5
SCALE = float(1.0 / DH ** 0.5)
MASKED = -1e30
NPROD = 6
KROWS = 2 * NPROD * DH
MROWS = 3
QPART = [0, 0, 0, 1, 1, 2]
KPART = [0, 1, 2, 0, 1, 0]
UNITS = 8
STACKED = 3 * NPROD * 16
NPT = 8
TILES = 16
SLOTS = TILES + E - 1
AHEAD = 2
PAD_TILES = 6
PAD_AT = range(0, SLOTS, PAD_TILES)
ROW = P + 1
WE = 2 * F + FB + P

PLAN = {
    False: [(0, "stats+"), (4, "norm+"), (4, "m1"), (5, "hT+"), (7, "q+"), (8, "k+"), (8, "qmid+"),
            (9, "kmid+"), (10, "v+"), (10, "o3-"), (11, "onT-"), (12, "out-"), (13, "m2"), (14, "o0"),
            (21, "m3"), (22, "o1"), (29, "m0+"), (30, "o2")],
    True: [(0, "stats+"), (2, "norm+"), (4, "hT+"), (5, "m1"), (6, "q+"), (7, "k+"), (7, "qmid+"), (8, "v+"),
           (9, "kmid+"), (9, "o3-"), (11, "onT-"), (12, "out-"), (12, "m2"), (14, "o0"), (20, "m3"),
           (21, "o1"), (29, "m0+"), (30, "o2")],
}
LATER = {False: 0, True: 0}
LEAD = {False: 12, True: 14}
QUERIES = [3, 0, 1, 2]
M0_AT = 20
HEADJOBS = ["stats", "norm", "hT", "q", "k", "qmid", "kmid", "v"]
TAIL = ["o3", "onT", "out"]
NOBANK = ("stats", "norm", "qmid", "kmid")

PV_AT = [
    {0: [(2, 3)], 1: [(1, 0)], 2: [(1, 1), (1, 2)], 3: [(1, 3)]},
    {1: [(1, 0)], 2: [(1, 1)], 3: [(1, 2)]},
]
PV_LEFT = [(6, 3), (7, 0), (7, 1), (7, 2), (7, 3)]


def plan_of(causal, par, later=0):
    plan = [[] for _ in range(4 * UNITS)]
    for at, job in PLAN[causal]:
        if par or not job.endswith("-"):
            plan[at + (later if job.rstrip("+-") not in NOBANK else 0)].append(job)
    return plan


def bank_jobs(causal):
    order = [(par, j) for par in range(2) for jobs in plan_of(causal, par) for j in jobs
             if j.rstrip("+-") not in NOBANK]
    return order + [(1, j) for j in TAIL]


BANK = {causal: bank_jobs(causal) for causal in (False, True)}
BANKHEAD = ["hT", "q", "k", "v", "m0"]


def program(nc, d):
    with ExitStack() as ctx:
        def sb(name, shape, dt=F32):
            return ctx.enter_context(nc.sbuf_tensor(name, shape, dt))

        def sem(name):
            return ctx.enter_context(nc.semaphore(name))

        ps = ctx.enter_context(nc.psum_tensor("ps", [P, 8, 512], F32))
        SH = 7
        shared = ps[:, SH, :]
        shared_t = shared.rearrange("p (i c) -> p i c", c=P)
        pv_bank = ps[:, 6, :]

        NT = TB * (NB + 1)
        x = sb("x", [P, NT, P])
        res = sb("res", [P, NT, P])
        lnx = sb("lnx", [P, TB, P])
        stats = sb("stats", [P, TILES, 6])
        mv = sb("mv", [P, TILES, 2])
        rstd = sb("rstd", [P, TILES])
        rstd2 = sb("rstd2", [P, TILES])
        lntmp = sb("lntmp", [P, TILES])
        minus_half = sb("minus_half", [P, TILES])
        hT = sb("hT", [P, S])
        q32 = sb("q32", [P, 2, S])
        rem = sb("rem", [P, 2, S])
        parts = sb("parts", [P, 2, 3, S], BF16)
        qs = [sb(f"qs{i}", [P, 2, H // 2, S], BF16) for i in range(2)]
        ks = [sb(f"ks{i}", [P, H // 2, S], BF16) for i in range(2)]
        va = [sb(f"va{i}", [P, TB, H, 32]) for i in range(2)]
        negm = sb("negm", [P, 2, 2, 2, TB])
        mrem = sb("mrem", [P, 2, 2, TB])
        mpart = sb("mpart", [P, 2, 3, 2 * TB], BF16)
        mrow = sb("mrow", [2 * 3 * 2 * TB, P], BF16)
        pt = sb("pt", [P, NPT, 1024])
        ot = sb("ot", [P, S])
        rc = sb("rc", [P, TB, 4])
        on = sb("on", [P, TB, P])
        onT = sb("onT", [P, S])
        upd = sb("upd", [P, TB, P])
        upd2 = onT[:, :].rearrange("p (i c) -> p i c", i=TB)
        identf = sb("identf", [P, P])
        identb = sb("identb", [P, P], BF16)
        mask_q = sb("mask_q", [P, P], BF16)
        mask_k = sb("mask_k", [P, P], BF16)
        ones_col = sb("ones_col", [P, 1])
        zero_col = sb("zero_col", [P, 1])
        wraw = sb("wraw", [P, 12, P])
        wT = sb("wT", [P, 4, P])
        wperm = sb("wperm", [P, 6, P])
        bcol = sb("bcol", [P, 6])
        bcols = sb("bcols", [P, 6])
        bvb = sb("bvb", [P, 3, P])
        bob = sb("bob", [P, 3, P])
        gcol = sb("gcol", [P, 4])
        experts = sb("experts", [P, E, WE])
        gw = sb("gw", [P, E])
        gbb = sb("gbb", [P, E])
        logit = sb("logit", [P, TILES, E])
        lmax = sb("lmax", [P, TILES])
        pref_i = sb("pref_i", [P, TILES, E], I32)
        pref = sb("pref", [P, TILES, E])
        score = sb("score", [P, TILES, E])
        smax = sb("smax", [P, TILES])
        ohb = sb("ohb", [P, TILES, E], BF16)
        earlier = sb("earlier", [P, P], BF16)
        onesb = sb("onesb", [P, P], BF16)
        count_i = sb("count_i", [P, SLOTS + AHEAD], I32)
        count = sb("count", [P, SLOTS + AHEAD])
        lower_e = sb("lower_e", [P, E, E])
        more = sb("more", [P, E, TILES])
        ntile = sb("ntile", [P, E])
        first = sb("first", [P, E])
        last_e = sb("last_e", [P, E])
        posf = sb("posf", [P, TILES])
        pos = sb("pos", [P, TILES], U32)
        owner_c = sb("owner_c", [1, SLOTS + AHEAD, E - 1])
        ownerf = sb("ownerf", [1, SLOTS + AHEAD])
        owner = sb("owner", [1, SLOTS + AHEAD], I32)
        numbers_y = sb("numbers_y", [P, 2], U32)
        ptf = pt[:, :, :].rearrange("p a c -> p (a c)")
        WE_AT = NPT * 1024 - 4 * WE
        lnall = ptf[:, WE_AT:WE_AT + TILES * ROW].rearrange("p (a c) -> p a c", c=ROW)
        relu = pt[:, 0, :].rearrange("p (a c) -> p a c", a=2)
        fold = pt[:, 1, :].rearrange("p (a c) -> p a c", a=2)
        mid = pt[:, 2:4, :].rearrange("p a (b c) -> p (a b) c", b=2)
        hTa = pt[:, 6:8, :].rearrange("p a (b c) -> p (a b) c", b=2)
        xs = ptf[:, 0:SLOTS * ROW].rearrange("p (a c) -> p a c", c=ROW)
        yall = ptf[:, 0:TILES * P].rearrange("p (a c) -> p a c", c=P)
        we = ptf[:, WE_AT:].rearrange("p (a c) -> p a c", c=WE)
        hTm = onT[:, 0:2 * P].rearrange("p (a c) -> p a c", a=2)
        mid_e = q32[:, :, :].rearrange("p a (b c) -> p a b c", c=P)
        ysb = upd[:, 0:2, :]
        xst = lnx[:, 0:2, :]
        hTa_moe = ptf[:, WE_AT + TILES * ROW:WE_AT + TILES * ROW + NB * S]\
            .rearrange("p (a c) -> p a c", a=NB)
        numbers_t = sb("numbers_t", [P, TILES], U32)
        pad_row = sb("pad_row", [P, P])
        pad_number = sb("pad_number", [P, SLOTS], U32)
        late = ptf[:, WE_AT + TILES * ROW:]
        wi_raw = late[:, 0:F].rearrange("p (a c) -> p a c", c=P)
        wo_raw = late[:, F:2 * F]
        loA = late[0:RANK, 2 * F:2 * F + TOPK * P].rearrange("p (a c) -> p a c", a=TOPK)
        loB = late[:, 1280:1280 + TOPK * FB * RANK].rearrange("p (a b c) -> p a b c", a=TOPK, b=FB)
        loBT = late[0:RANK, 1408:1408 + TOPK * F].rearrange("p (a c) -> p a c", a=TOPK)
        wiT = hT[:, :]
        wk = sb("wk", [P, TOPK, F])
        wo2 = sb("wo2", [P, FB, P])
        idx = sb("idx", [1, TOPK], I32)
        tkv = sb("tkv", [P, TOPK])

        x_loaded = sem("x_loaded")
        w_loaded = sem("w_loaded")
        w_rest = sem("w_rest")
        ffn_loaded = sem("ffn_loaded")
        idx_loaded = sem("idx_loaded")
        lora_loaded = sem("lora_loaded")
        const_first = sem("const_first")
        const_done = sem("const_done")
        cleared = sem("cleared")
        x_rest = sem("x_rest")
        set_dve = sem("set_dve")
        set_pe = sem("set_pe")
        set_free = sem("set_free")
        ln_stat = sem("ln_stat")
        ln_rstd = sem("ln_rstd")
        ln_x = sem("ln_x")
        h_kept = sem("h_kept")
        bank_full = sem("bank_full")
        bank_free = sem("bank_free")
        hi_done = sem("hi_done")
        split_done = [sem("q_split_done"), sem("k_split_done")]
        qk_loaded = sem("qk_loaded")
        p1_ready = sem("p1_ready")
        max_done = sem("max_done")
        m_parts = sem("m_parts")
        m_loaded = sem("m_loaded")
        p2_ready = sem("p2_ready")
        exp_done = sem("exp_done")
        pv_done = sem("pv_done")
        ot_ready = sem("ot_ready")
        rc_done = sem("rc_done")
        guard_done = sem("guard_done")
        x_done = sem("x_done")
        up_ready = sem("up_ready")
        relu_done = sem("relu_done")
        fold_done = sem("fold_done")
        mid_done = sem("mid_done")
        down_done = sem("down_done")
        y_free = sem("y_free")
        ln_turned = sem("ln_turned")
        hta_done = sem("hta_done")
        logits_ready = sem("logits_ready")
        owner_step = sem("owner_step")
        route = sem("route")
        rank_ready = sem("rank_ready")
        prefilled = sem("prefilled")
        numbered = sem("numbered")
        rows_sorted = sem("rows_sorted")
        xs_loaded = [sem("xs_loaded0"), sem("xs_loaded1")]
        tile_copied = sem("tile_copied")
        tile_turned = sem("tile_turned")
        tile_in = sem("tile_in")
        expert_ready = sem("expert_ready")
        tile_down = sem("tile_down")
        y_ready = sem("y_ready")
        y_sent = [sem("y_sent0"), sem("y_sent1")]
        y_loaded = [sem(f"y_loaded{b}") for b in range(NB)]
        out_done = sem("out_done")
        stood_apart = sem("stood_apart")

        NCONST = 16

        W = [
            dict(wq=wperm[:, 0, :], wk=wperm[:, 1, :], wv=wraw[:, 2, :], wo=wraw[:, 3, :], n=0,
                 g=gcol[:, 0:1], b=gcol[:, 1:2], causal=False, moe=True, nan_guard=False),
            dict(wq=wperm[:, 2, :], wk=wperm[:, 3, :], wv=wraw[:, 6, :], wo=wraw[:, 7, :], n=1,
                 g=ones_col[:, :], b=zero_col[:, :], causal=True, moe=False, nan_guard=False),
            dict(wq=wperm[:, 4, :], wk=wperm[:, 5, :], wv=wT[:, 2, :], wo=wT[:, 3, :], n=2,
                 g=ones_col[:, :], b=zero_col[:, :], causal=True, moe=False, nan_guard=True),
        ]
        ORDER = [("attn", 0), ("moe", None), ("attn", 1), ("attn", 0), ("moe", None), ("ffn", None),
                 ("attn", 2), ("ffn", None)]
        ATTN_LN, ATTN_BANK = NB + 1, len(BANKHEAD) + NB // 2 * len(BANK[False])
        ATTN_TILES, ATTN_QUADS = NB * UNITS * 8, NB * 4 + 1

        SETUP_BANK = 3 + 2 * TOPK

        ONE = 1
        credited = [pv_done, exp_done, ot_ready, y_free, mid_done, down_done, relu_done, fold_done, tile_down, y_ready]

        phases = []
        c = dict(ln=0, bank=0, ptile=0, quad=0, attn=0, moe=0, xd=0, prep=0, up=0, mid=ONE, relu=ONE,
                 y=ONE, fold=ONE, kept=0, tr=0)
        for kind, w in ORDER:
            phases.append((kind, w, dict(c)))
            if kind == "attn":
                c["ln"] += ATTN_LN
                c["bank"] += ATTN_BANK
                c["ptile"] += ATTN_TILES + 2 * LEAD[W[w]["causal"]]
                c["quad"] += ATTN_QUADS
                c["prep"] += NB + 1
                c["attn"] += 1
                c["kept"] += (NB + 1) * TB if W[w]["moe"] else 0
            elif kind == "moe":
                c["ln"] += NB
                c["bank"] += SETUP_BANK if c["moe"] == 0 else 0
                c["tr"] += NB
                c["moe"] += 1
                c["up"] += SLOTS * FB
                c["relu"] += SLOTS * FB
            else:
                c["ln"] += NB
                c["tr"] += NB
                c["fold"] += NB * FB
                c["up"] += NB * FB * TOPK
                c["relu"] += NB * FB
                c["mid"] += NB * FB
                c["y"] += NB
            c["xd"] += NB
        def tiles(t, b):
            return t[:, bass.ds(b * TB, TB), :] if not isinstance(b, int) else t[:, b * TB:(b + 1) * TB, :]

        def tile(t, b, j):
            return t[:, b * TB + j, :]

        def wait(eng, s, n):
            if not isinstance(n, int) or n > 0:
                eng.wait_ge(s, n)

        def apart(eng, s, n):
            wait(eng, s, n)
            if not isinstance(n, int):
                eng.sem_inc(stood_apart, 1)

        block = ctx.enter_context(nc.Block())

        def ln_stats(v, b, n, src, x_ready):
            if x_ready is not None:
                v.wait_ge(x_done, x_ready)
            wait(v, ln_x, n)
            for j in range(TB):
                v.bn_stats(stats[:, j, :], tile(src, b, j)).then_inc(ln_stat, 1)
            apart(v, ln_stat, n * 8 + 4)
            for j in range(TB):
                v.bn_aggr(mv[:, j, :], stats[:, j, :]).then_inc(ln_stat, 1)

        everything = (lntmp[:, :], rstd[:, :], rstd2[:, :], mv[:, :, 1], minus_half[:, :])

        def ln_pool(g, n, twice, batches=1, first=0):
            lntmp, rstd, rstd2, var, minus_half = (t[:, TB * first:TB * (first + batches)] for t in everything)
            def step(i):
                return n * 7 + i
            apart(g, ln_stat, n * 8 + 8 * batches)
            apart(g, ln_x, n - first)
            g.tensor_scalar(lntmp, var, EPS, None, ALU.add).then_inc(ln_rstd, 1)
            apart(g, ln_rstd, step(1))
            g.tensor_tensor(rstd, lntmp, minus_half, ALU.pow).then_inc(ln_rstd, 1)
            apart(g, ln_rstd, step(2))
            if not twice:
                g.tensor_copy(rstd2, rstd).then_inc(ln_rstd, 7 * batches - 2)
                return
            g.tensor_tensor(lntmp, rstd, rstd, ALU.mult).then_inc(ln_rstd, 1)
            apart(g, ln_rstd, step(3))
            g.tensor_tensor(lntmp, lntmp, var, ALU.mult).then_inc(ln_rstd, 1)
            apart(g, ln_rstd, step(4))
            g.tensor_scalar(lntmp, lntmp, EPS, None, ALU.add).then_inc(ln_rstd, 1)
            apart(g, ln_rstd, step(5))
            g.tensor_tensor(lntmp, lntmp, minus_half, ALU.pow).then_inc(ln_rstd, 1)
            apart(g, ln_rstd, step(6))
            g.tensor_tensor(rstd2, lntmp, rstd, ALU.mult).then_inc(ln_rstd, 1)

        def ln_norm(v, b, n, bank_n, src, keep):
            v.wait_ge(ln_rstd, n * 7 + 7)
            if bank_n is not None:
                wait(v, bank_full, bank_n)
            if keep:
                for j in range(TB):
                    v.tensor_scalar(tile(res, b, j), tile(src, b, j), mv[:, j, 0:1], rstd[:, j:j + 1],
                                    ALU.subtract, ALU.mult).then_inc(h_kept, 1)
            for j in range(TB):
                ins = v.tensor_scalar(lnx[:, j, :], tile(src, b, j), mv[:, j, 0:1], rstd2[:, j:j + 1],
                                      ALU.subtract, ALU.mult)
            ins.then_inc(ln_x, 1)

        def ln_everything(v, cnt, src):
            n = cnt["ln"]
            v.wait_ge(ln_x, n)
            for half in range(2):
                for b in (2 * half, 2 * half + 1):
                    v.wait_ge(x_done, cnt["xd"] - NB + 1 + b)
                    for j in range(TB):
                        v.bn_stats(stats[:, b * TB + j, :], tile(src, b, j)).then_inc(ln_stat, 1)
                v.wait_ge(ln_stat, n * 8 + (2 * half + 1) * 8)
                for j in range(8 * half, 8 * half + 8):
                    v.bn_aggr(mv[:, j, :], stats[:, j, :]).then_inc(ln_stat, 1)
            for j in range(TILES):
                if j % 8 == 0:
                    v.wait_ge(ln_rstd, n * 7 + 14 * (j // 8 + 1))
                ins = v.tensor_scalar(lnall[:, j, 0:P], src[:, j, :], mv[:, j, 0:1], rstd[:, j:j + 1],
                                      ALU.subtract, ALU.mult)
                if j % TB == TB - 1:
                    ins.then_inc(ln_x, 1)

        def turn_everything(pe, cnt):
            for b in range(NB):
                pe.wait_ge(ln_x, cnt["ln"] + b + 1)
                for j in range(TB):
                    ins = pe.transpose(ps[:, 4 + b, j * P:(j + 1) * P], lnall[:, b * TB + j, 0:P], identf[:, :])
                ins.then_inc(ln_turned, 1)

        def transpose_ln(pe, n, bank_n):
            pe.wait_ge(ln_x, n + 1)
            wait(pe, bank_free, bank_n)
            for j in range(TB):
                ins = pe.transpose(shared_t[:, j, :], lnx[:, j, :], identf[:, :])
            ins.then_inc(bank_full, 1)

        def numbers(cnt, b, par):
            return dict(b=b, par=par, ln=b + cnt["ln"], ptile=b * UNITS * 8 + cnt["ptile"], quad=b * 4 + cnt["quad"],
                        unit=b * UNITS + cnt["attn"] * NB * UNITS, prep=b + cnt["prep"],
                        x_ready=b + (cnt["xd"] - NB + 1) if cnt["xd"] else None,
                        ot=b * 4 + (cnt["attn"] * NB * 4 + ONE),
                        kept=b * TB + cnt["kept"],
                        xd=b + cnt["xd"])

        def bank_number(cnt, causal, pair, par, job):
            return pair * len(BANK[causal]) + (cnt["bank"] + len(BANKHEAD) + BANK[causal].index((par, job)))

        def pass1_tile(pe, w, N, g, hf, r):
            s, i = r // TB, QUERIES[r % TB]
            n = N["ptile"] + (2 * g + hf) * 8 + r
            t = 2 * g + hf
            q, k = qs[N["par"]], ks[N["par"]]
            width = (i + 1) * P if w["causal"] else S
            wait(pe, max_done, n - 1)
            ins = pe.matmul(ps[:, r % 2, 0:width], q[0:KROWS, s, t, i * P:(i + 1) * P], k[0:KROWS, t, 0:width],
                            start=True, stop=not w["causal"])
            if w["causal"]:
                ins = pe.matmul(ps[:, r % 2, i * P:width], identb[:, :], mask_q[:, :], start=False, stop=True)
            ins.then_inc(p1_ready, 1)

        def rowmax_tile(v, w, N, g, hf, r):
            s, i = r // TB, QUERIES[r % TB]
            n = N["ptile"] + (2 * g + hf) * 8 + r
            width = (i + 1) * P if w["causal"] else S
            v.wait_ge(p1_ready, n + 1)
            v.tensor_reduce(negm[:, g % 2, s, hf, i:i + 1], ps[:, r % 2, 0:width], AX, ALU.max,
                            negate=True).then_inc(max_done, 1)

        def split_max(g_, N, g, bank_n):
            n = (N["quad"] + g) * 4
            apart(g_, max_done, N["ptile"] + (g + 1) * 16)
            apart(g_, m_parts, n)
            src = negm[:, g % 2].rearrange("p s t i -> p s (t i)")
            rem_ = mrem[:, :, :, :].rearrange("p s t i -> p s (t i)")
            g_.tensor_copy(mpart[:, :, 0, :], src).then_inc(m_parts, 1)
            apart(g_, m_parts, n + 1)
            g_.tensor_tensor(rem_, src, mpart[:, :, 0, :], ALU.subtract).then_inc(m_parts, 1)
            apart(g_, m_parts, n + 2)
            g_.tensor_copy(mpart[:, :, 1, :], rem_).then_inc(m_parts, 1)
            apart(g_, m_parts, n + 3)
            g_.tensor_tensor(mpart[:, :, 2, :], rem_, mpart[:, :, 1, :], ALU.subtract).then_inc(m_parts, 1)

        def store_max(a, N, g, bank_n):
            a.wait_ge(bank_free, bank_n + 1)
            for s in range(2):
                a.dma_start(qs[N["par"]][KROWS + MROWS * s:KROWS + MROWS * (s + 1), s, 2 * g:2 * g + 2, :],
                            mrow[24 * s:24 * s + 24, :]).then_inc(m_loaded, 16)

        def slot_cols(w, hf, kb):
            q0 = kb * P if w["causal"] else 0
            if w["causal"]:
                at = {0: 0, 1: S, 2: 0, 3: S - 2 * P}[kb]
            else:
                at = (kb % 2) * S
            return at, at + S - q0, q0

        def slot_width(w, hf):
            return slot_cols(w, hf, 2 * hf + 1)[1]

        def pass2_slot(pe, w, N, u, k):
            g, hf = u // 2, u % 2
            t, s = 2 * g + k // 2, k % 2
            n = (N["unit"] + u) * 4 + k
            q, kk = qs[N["par"]], ks[N["par"]]
            flat = ps[:, 2 + 2 * (k % 2):4 + 2 * (k % 2), :].rearrange("p a c -> p (a c)")
            if k == 0 and hf == 0:
                pe.wait_ge(m_loaded, (N["quad"] + g + 1) * 32)
            wait(pe, exp_done, (n - 1 if u or k else n) + ONE)
            for kb in (2 * hf, 2 * hf + 1):
                a, z, q0 = slot_cols(w, hf, kb)
                ins = pe.matmul(flat[:, a:z], kk[:, t, kb * P:(kb + 1) * P], q[:, s, t, q0:S],
                                start=True, stop=not w["causal"])
                if w["causal"]:
                    ins = pe.matmul(flat[:, a:a + P], identb[:, :], mask_k[:, :], start=False, stop=True)
            ins.then_inc(p2_ready, 1)

        def exp_slot(a, w, N, u, k):
            n = (N["unit"] + u) * 4 + k
            flat = ps[:, 2 + 2 * (k % 2):4 + 2 * (k % 2), :].rearrange("p a c -> p (a c)")
            width = slot_width(w, u % 2)
            a.wait_ge(p2_ready, n + 1)
            if k == 0:
                wait(a, pv_done, N["unit"] + (u - 1 if u or N["par"] else 0) + ONE)
            a.activation(pt[:, (u % 2) * 4 + k, 0:width], flat[:, 0:width], ACT.Exp).then_inc(exp_done, 1)

        def pv_piece(pe, w, N, u, piece):
            g, hf = u // 2, u % 2
            kb, half = 2 * hf + piece // 2, piece % 2
            a, _, q0 = slot_cols(w, hf, kb)
            if piece == 0:
                pe.wait_ge(exp_done, (N["unit"] + u + 1) * 4 + ONE)
                if hf == 0:
                    wait(pe, ot_ready, N["ot"] + g)
            lo, hi = max(half * S // 2, q0), (half + 1) * S // 2
            if lo >= hi:
                return
            for j in range(4):
                ins = pe.matmul(pv_bank[32 * j:32 * j + 32, lo:hi], va[N["par"]][:, kb, 4 * g + j, :],
                                pt[:, hf * 4 + j, a + lo - q0:a + hi - q0], start=(kb == 0 and half == 0),
                                stop=(kb == TB - 1), skip_group_check=True)
            if piece == 3:
                ins.then_inc(pv_done, 1)

        def pe_job(pe, w, cnt, N, job, bn):
            if job == "hT":
                transpose_ln(pe, N["ln"], bn)
            elif job in ("q", "k"):
                wait(pe, bank_free, bn)
                weight_ = w["wq" if job == "q" else "wk"]
                pe.matmul(shared, weight_, hT[:, :], start=True, stop=True).then_inc(bank_full, 1)
            elif job == "v":
                wait(pe, bank_free, bn)
                for i in range(TB):
                    ins = pe.matmul(shared_t[:, i, :], hT[:, i * P:(i + 1) * P], w["wv"], start=True, stop=True)
                ins.then_inc(bank_full, 1)
            elif job[0] == "m":
                g = int(job[1])
                pe.wait_ge(m_parts, (N["quad"] + g) * 4 + 4)
                apart(pe, bank_free, bn)
                pe.transpose(shared[0:48, 0:P // 2].bitcast(BF16), mpart[:, :, :, :].rearrange("p s r c -> p (s r c)"),
                             identb[:, :]).then_inc(bank_full, 1)
            elif job in ("o0", "o1", "o2", "o3"):
                pe.wait_ge(ot_ready, N["ot"] + int(job[1]) + 1)
                wait(pe, bank_free, bn)
                for i in range(TB):
                    ins = pe.transpose(shared_t[:, i, :], ot[:, i * P:(i + 1) * P], identf[:, :])
                ins.then_inc(bank_full, 1)
            elif job == "onT":
                wait(pe, bank_free, bn)
                for i in range(TB):
                    ins = pe.transpose(shared_t[:, i, :], on[:, i, :], identf[:, :])
                ins.then_inc(bank_full, 1)
            elif job == "out":
                wait(pe, bank_free, bn)
                for i in range(TB):
                    ins = pe.matmul(shared_t[:, i, :], onT[:, i * P:(i + 1) * P], w["wo"], start=True, stop=True)
                ins.then_inc(bank_full, 1)

        def act_job(a, w, cnt, N, job, bn):
            if job == "hT":
                a.wait_ge(bank_full, bn + 1)
                a.activation(hT[:, :], shared, ACT.Identity, bias=w["b"], scale=w["g"]).then_inc(bank_free, 1)
            elif job in ("q", "k"):
                c_ = 0 if job == "q" else 1
                col = 2 * w["n"] + c_
                a.wait_ge(bank_full, bn + 1)
                wait(a, split_done[c_], N["prep"] * 3)
                a.activation(q32[:, c_, :], shared, ACT.Identity, bias=bcols[:, col:col + 1],
                             scale=SCALE if job == "q" else 1.0).then_inc(bank_free, 1)
                a.wait_ge(bank_free, bn + 1)
                wait(a, qk_loaded, N["prep"] * STACKED)
                a.activation(parts[:, c_, 0, :], q32[:, c_, :], ACT.Copy).then_inc(hi_done, 1)
            elif job in ("qmid", "kmid"):
                c_ = 0 if job == "qmid" else 1
                a.wait_ge(split_done[c_], N["prep"] * 3 + 1)
                a.activation(parts[:, c_, 1, :], rem[:, c_, :], ACT.Copy).then_inc(split_done[c_], 1)
            elif job[0] == "m":
                a.wait_ge(bank_full, bn + 1)
                wait(a, m_loaded, (N["quad"] + int(job[1])) * 32)
                a.activation(mrow[:, :], shared[0:48, 0:P // 2].bitcast(BF16), ACT.Copy).then_inc(bank_free, 1)
                store_max(a, N, int(job[1]), bn)
            elif job == "onT":
                a.wait_ge(bank_full, bn + 1)
                a.activation(onT[:, :], shared, ACT.Copy).then_inc(bank_free, 1)

        def ot_copy(a, N, u):
            g = u // 2
            a.wait_ge(pv_done, N["unit"] + u + 1 + ONE)
            a.activation(ot[:, :], pv_bank, ACT.Copy).then_inc(ot_ready, 1)

        def dve_job(v, w, cnt, N, job, bn):
            if job == "stats":
                ln_stats(v, N["b"], N["ln"], x, N["x_ready"])
            elif job == "norm":
                ln_norm(v, N["b"], N["ln"], None, x, w["moe"])
            elif job == "v":
                v.wait_ge(bank_full, bn + 1)
                v.tensor_tensor(va[N["par"]][:, :, :, 0:DH],
                                shared_t.rearrange("p i (h e) -> p i h e", e=DH),
                                bvb[:, w["n"]:w["n"] + 1, :].rearrange("p o (h e) -> p o h e", e=DH)
                                .broadcast_to([P, TB, H, DH]), ALU.add).then_inc(bank_free, 1)
            elif job in ("o0", "o1", "o2", "o3"):
                g = int(job[1])
                v.wait_ge(bank_full, bn + 1)
                o4 = shared_t.rearrange("p i (j e) -> p i j e", e=32)
                v.reciprocal(rc[:, :, :], o4[:, :, :, DH]).then_inc(rc_done, 1)
                v.wait_ge(rc_done, N["ot"] - ONE + g + 1)
                v.tensor_tensor(on[:, :, 32 * g:32 * g + 32].rearrange("p i (j e) -> p i j e", e=DH),
                                o4[:, :, :, 0:DH],
                                rc[:, :, :].rearrange("p i (j o) -> p i j o", o=1).broadcast_to([P, TB, 4, DH]),
                                ALU.mult).then_inc(bank_free, 1)
            elif job == "out":
                bo = bob[:, w["n"]:w["n"] + 1, :].broadcast_to([P, TB, P])
                dst = tiles(res if w["moe"] else x, N["b"])
                v.wait_ge(bank_full, bn + 1)
                v.tensor_tensor(upd[:, :, :], shared_t, bo, ALU.add).then_inc(bank_free, 1)
                v.wait_ge(bank_free, bn + 1)
                if w["moe"]:
                    v.wait_ge(h_kept, N["kept"] + TB)
                if w["nan_guard"]:
                    v.tensor_scalar(upd2[:, :, :], upd[:, :, :], 0.0, None, ALU.max).then_inc(guard_done, 1)
                    v.wait_ge(guard_done, N["b"] * 2 + 1)
                    v.scalar_tensor_tensor(upd[:, :, :], upd[:, :, :], 0.0, upd2[:, :, :], ALU.min,
                                           ALU.add).then_inc(guard_done, 1)
                    v.wait_ge(guard_done, N["b"] * 2 + 2)
                v.tensor_tensor(dst, dst, upd[:, :, :], ALU.add).then_inc(x_done, 1)
                v.wait_ge(x_done, N["xd"] + 1)

        def pool_job(g_, w, cnt, N, job, bn):
            if job == "norm":
                ln_pool(g_, N["ln"], w["moe"])
            elif job in ("q", "k"):
                c_ = 0 if job == "q" else 1
                done, n = split_done[c_], N["prep"] * 3
                apart(g_, hi_done, N["prep"] * 2 + c_ + 1)
                g_.tensor_tensor(rem[:, c_, :], q32[:, c_, :], parts[:, c_, 0, :], ALU.subtract).then_inc(done, 1)
                apart(g_, done, n + 2)
                g_.tensor_tensor(parts[:, c_, 2, :], rem[:, c_, :], parts[:, c_, 1, :],
                                 ALU.subtract).then_inc(done, 1)
            elif job[0] == "m":
                split_max(g_, N, int(job[1]), bn)

        def walk(eng, w, cnt, pair, par, scores, job_fn, unit_end=None, later=0):
            plan = plan_of(w["causal"], par, later)
            b = pair * 2 + par
            N, after = numbers(cnt, b, par), numbers(cnt, b + 1, 1 - par)
            before = numbers(cnt, pair * 2, 0) if par else None
            for u in range(UNITS):
                for k in range(4):
                    if scores:
                        scores(before, N, after, u, k)
                    for job in plan[4 * u + k]:
                        name = job.rstrip("+-")
                        at = "hT+" if name in NOBANK else job
                        job_fn(eng, w, cnt, {"+": after, "-": before}.get(job[-1], N), name,
                               bank_number(cnt, w["causal"], pair, par, at))
                if unit_end:
                    unit_end(before, N, u)
            return N

        def head(eng, w, cnt, job_fn, after={}):
            N = numbers(cnt, 0, 0)
            for name in HEADJOBS:
                at = "hT" if name in NOBANK else name
                job_fn(eng, w, cnt, N, name, cnt["bank"] + BANKHEAD.index(at))
                if name in after:
                    after[name]()
            return N

        def lead_of(N, after, u, k, lead):
            at = 4 * u + k + lead
            N, at = (N, at) if at < 4 * UNITS else (after, at - 4 * UNITS)
            return N, at // 8, at // 4 % 2, at % 4

        def attention_pe(pe, w, cnt):
            wait(pe, y_free, cnt["y"])
            N0 = head(pe, w, cnt, pe_job)
            pe.wait_ge(qk_loaded, (N0["prep"] + 1) * STACKED)
            for n in range(2 * LEAD[w["causal"]]):
                if n == M0_AT:
                    pe_job(pe, w, cnt, N0, "m0", cnt["bank"] + BANKHEAD.index("m0"))
                pass1_tile(pe, w, N0, n // 16, n // 8 % 2, n % 8)

            def scores(before, N, after, u, k):
                L, g, hf, step = lead_of(N, after, u, k, LEAD[w["causal"]])
                if (g, hf, step) == (0, 0, 0):
                    pe.wait_ge(qk_loaded, (L["prep"] + 1) * STACKED)
                pass1_tile(pe, w, L, g, hf, 2 * step)
                pass2_slot(pe, w, N, u, k)
                pass1_tile(pe, w, L, g, hf, 2 * step + 1)
                for back, piece in PV_AT[u % 2].get(k, []):
                    if u >= back:
                        pv_piece(pe, w, N, u - back, piece)
                    elif before:
                        pv_piece(pe, w, before, u - back + UNITS, piece)

            with pe.Fori(0, NB // 2) as pair:
                for par in range(2):
                    N = walk(pe, w, cnt, pair, par, scores, pe_job)
                for u, piece in PV_LEFT:
                    pv_piece(pe, w, N, u, piece)
                for job in TAIL:
                    pe_job(pe, w, cnt, N, job, bank_number(cnt, w["causal"], pair, 1, job))

        def clear_q(v, par):
            v.memset(qs[par][:, :, :, :].rearrange("p s t c -> p (s t c)").bitcast(F32), 0.0).then_inc(cleared, 1)

        def first_weights(v):
            v.wait_ge(w_loaded, 16 * len(wl))
            scale_biases(v, 0, 2)
            for j in range(2):
                stacking_order(v, j, wraw[:, j, :])

        def attention_dve(v, w, cnt):
            first_one = cnt["attn"] == 0
            N0 = head(v, w, cnt, dve_job, {"norm": lambda: first_weights(v)} if first_one else {})
            if first_one:
                clear_q(v, 1)
                v.wait_ge(x_rest, 16)
                v.wait_ge(const_done, NCONST)
                v.sem_inc(cleared, 1)
            wait(v, m_parts, N0["quad"] * 4)
            for n in range(2 * LEAD[w["causal"]]):
                rowmax_tile(v, w, N0, n // 16, n // 8 % 2, n % 8)

            def scores(before, N, after, u, k):
                L, g, hf, step = lead_of(N, after, u, k, LEAD[w["causal"]])
                for r in (2 * step, 2 * step + 1):
                    if hf == 0 and r == 0:
                        wait(v, m_parts, (L["quad"] + g - 1) * 4)
                    rowmax_tile(v, w, L, g, hf, r)

            with v.Fori(0, NB // 2) as pair:
                for par in range(2):
                    N = walk(v, w, cnt, pair, par, scores, dve_job, later=LATER[w["causal"]])
                for job in TAIL:
                    dve_job(v, w, cnt, N, job, bank_number(cnt, w["causal"], pair, 1, job))

        def attention_act(a, w, cnt):
            N0 = head(a, w, cnt, act_job)
            act_job(a, w, cnt, N0, "m0", cnt["bank"] + BANKHEAD.index("m0"))

            def scores(before, N, after, u, k):
                exp_slot(a, w, N, u, k)

            def unit_end(before, N, u):
                if u % 2 == 0 and u > 0:
                    ot_copy(a, N, u - 1)
                elif u == 0 and before:
                    ot_copy(a, before, UNITS - 1)

            with a.Fori(0, NB // 2) as pair:
                for par in range(2):
                    N = walk(a, w, cnt, pair, par, scores, act_job, unit_end)
                ot_copy(a, N, UNITS - 1)
                for job in TAIL:
                    act_job(a, w, cnt, N, job, bank_number(cnt, w["causal"], pair, 1, job))

        def later_constants(g_):
            done = [0]

            def const(ins):
                done[0] += 1
                ins.then_inc(const_done, 1)

            const(g_.memset(x[:, TB * NB:NT, :], 0.0))
            const(g_.memset(ks[1][:, :, :], 1.0))
            const(g_.memset(va[1][:, :, :, :], 0.0))
            const(g_.memset(earlier[:, :], 0.0))
            const(g_.memset(lower_e[:, :, :], 0.0))
            const(g_.iota(count_i[:, :], pattern=[[1, SLOTS + AHEAD]], base=0, channel_multiplier=0))
            const(g_.iota(pref_i[:, :, :], pattern=[[0, TILES], [-1, E]], base=E, channel_multiplier=0))
            g_.wait_ge(const_done, done[0])
            const(g_.memset(va[1][:, :, :, DH:DH + 1], 1.0))
            const(g_.affine_select(out=earlier[:, :], in_=earlier[:, :], compare_op=ALU.is_ge, fill=1.0, base=0,
                                   pattern=[[-1, P]], channel_multiplier=1))
            const(g_.affine_select(out=lower_e[:, :, :], in_=lower_e[:, :, :], compare_op=ALU.is_ge, fill=1.0, base=0,
                                   pattern=[[-1, E], [1, E]], channel_multiplier=0))
            const(g_.memset(onesb[:, :], 1.0))
            const(g_.memset(pad_row[:, :], 0.0))
            const(g_.iota(pad_number[:, :], pattern=[[P, SLOTS]], base=TILES * P, channel_multiplier=1))
            const(g_.iota(numbers_t[:, :], pattern=[[P, TILES]], base=0, channel_multiplier=1))
            const(g_.tensor_copy(pref[:, :, :], pref_i[:, :, :]))
            const(g_.tensor_copy(count[:, :], count_i[:, :]))
            assert done[0] == NCONST
            g_.wait_ge(const_done, NCONST)

        def attention_pool(g_, w, cnt):
            def ones_k():
                g_.memset(ks[0][:, :, :], 1.0).then_inc(const_first, 1)

            N0 = head(g_, w, cnt, pool_job, {"norm": ones_k} if cnt["attn"] == 0 else {})
            if cnt["attn"] == 0:
                later_constants(g_)
            pool_job(g_, w, cnt, N0, "m0", cnt["bank"] + BANKHEAD.index("m0"))
            with g_.Fori(0, NB // 2) as pair:
                for par in range(2):
                    walk(g_, w, cnt, pair, par, None, pool_job)

        def stack(sp, N, par):
            for part in range(3):
                for c_, which in ((0, QPART), (1, KPART)):
                    if part == 0:
                        sp.wait_ge(hi_done, N * 2 + c_ + 1)
                    else:
                        sp.wait_ge(split_done[c_], N * 3 + part + 1)
                    for p_ in range(NPROD):
                        r0 = 2 * p_ * DH
                        if which[p_] != part:
                            continue
                        if c_ == 1:
                            sp.dma_start(ks[par][r0:r0 + 2 * DH], parts[:, 1, part, :]).then_inc(qk_loaded, 16)
                        else:
                            for s in range(2):
                                sp.dma_start(qs[par][r0 + s * DH:r0 + (s + 1) * DH, s],
                                             parts[64 * s:64 * s + 64, 0, part, :]).then_inc(qk_loaded, 16)

        def attention_sync(sp, cnt, first_one):
            stack(sp, cnt["prep"], 0)
            if first_one:
                sp.wait_ge(const_done, NCONST)
                sp.wait_ge(cleared, 3)
            with sp.Fori(0, NB // 2) as i:
                for par in range(2):
                    stack(sp, i * 2 + par + 1 + cnt["prep"], 1 - par)
            if first_one:
                for dst, src in rest:
                    sp.dma_start(dst, src, allow_slow_non_contiguous=True).then_inc(w_rest, 16)
                sp.dma_start(idx[:, :], d["L1_ffn_top_k_indices"].rearrange("(o k) -> o k", o=1))\
                    .then_inc(idx_loaded, 16)
                for m in range(2):
                    rows = d["sorted"][m].rearrange("(t p) c -> p t c", p=P)
                    for t in PAD_AT:
                        some = rows[:, t:min(t + PAD_TILES, SLOTS), 0:P]
                        sp.dma_start(some, pad_row[:, :].rearrange("p (o c) -> p o c", o=1)
                                     .broadcast_to([P, some.shape[1], P])).then_inc(prefilled, 16)
                    sp.dma_start(rows[:, :, P:ROW].bitcast(U32), pad_number[:, :].rearrange("p (a o) -> p a o", o=1),
                                 allow_slow_non_contiguous=True).then_inc(prefilled, 16)

        def over_tiles(eng, tile_fn, before_loop=None):
            for t in range(3):
                tile_fn(t, t % 4, t // 2)
            if before_loop:
                before_loop()
            with eng.Fori(0, (SLOTS - 3) // 4) as i:
                for r in range(3, 7):
                    tile_fn(i * 4 + r, r % 4, i * 2 + r // 2)

        def moe_pe(pe, cnt):
            m = cnt["moe"]
            turn_everything(pe, cnt)
            if m == 0:
                pe.wait_ge(w_rest, 16 * len(rest))
            for b in range(NB):
                pe.wait_ge(hta_done, cnt["tr"] + b + 1)
                for i in range(TB):
                    j = b * TB + i
                    ins = pe.matmul(ps[:, 0, j * E:(j + 1) * E], hTa_moe[:, b, i * P:(i + 1) * P], gw[:, :],
                                    start=True, stop=True)
            ins.then_inc(logits_ready, 1)
            pe.wait_ge(route, m * ROUTE + 6)
            pe.matmul(ps[:, 1, 0:TILES * E], earlier[:, :], ohb[:, :, :], start=True, stop=False, skip_group_check=True)
            for j in range(TILES):
                ins = pe.matmul(ps[:, 1, (j + 1) * E:(TILES + 1) * E], onesb[:, :],
                                ohb[:, j:j + 1, :].broadcast_to([P, TILES - j, E]), start=False,
                                stop=(j == TILES - 1), skip_group_check=True)
            ins.then_inc(rank_ready, 1)
            if m == 0:
                late_setup_pe(pe, cnt)

            def one_tile(t, r, _):
                par = r % 2
                wait(pe, tile_in, t + m * SLOTS)
                pe.wait_ge(tile_copied, t + (m * (SLOTS + 1) + 1))
                pe.transpose(ps[:, 6, 0:P], xst[:, par, :], identf[:, :]).then_inc(tile_turned, 1)
                if not isinstance(t, int) or t > 0:
                    down_before(t, (r - 1) % 4)
                pe.wait_ge(tile_in, t + (m * SLOTS + 1))
                pe.wait_ge(expert_ready, t + (m * (SLOTS + AHEAD) + 1))
                for a in range(FB):
                    pe.matmul(ps[:, a, 0:P], we[:, r, a * P:(a + 1) * P], hTm[:, par, :], start=True,
                              stop=True).then_inc(up_ready, 1)

            def down_before(t, r):
                par = r % 2
                wait(pe, y_ready, t + (m * SLOTS - 2 + ONE))
                for a in range(FB):
                    pe.wait_ge(relu_done, t * FB + (cnt["relu"] + a + 1 - FB))
                    ins = pe.matmul(ps[:, 4 + par, 0:P], mid_e[:, par, a, :],
                                    we[:, r, F + a * P:F + (a + 1) * P], start=(a == 0), stop=(a == FB - 1))
                ins.then_inc(tile_down, 1)

            over_tiles(pe, one_tile)
            down_before(SLOTS, (SLOTS - 1) % 4)

        def moe_act(a, cnt):
            m = cnt["moe"]
            if m == 0:
                a.wait_ge(w_rest, 16 * len(rest))
            for b in range(NB):
                a.wait_ge(ln_turned, cnt["tr"] + b + 1)
                a.activation(hTa_moe[:, b, :], ps[:, 4 + b, :], ACT.Identity, bias=gcol[:, 3:4],
                             scale=gcol[:, 2:3]).then_inc(hta_done, 1)

            def copy_tile(t, par):
                a.activation(xst[:, par, :], ptf[:, bass.ds(t * ROW, P)], ACT.Copy).then_inc(tile_copied, 1)

            a.wait_ge(xs_loaded[0], 16 * (m + 1))
            copy_tile(0, 0)

            def one_tile(t, r, _):
                par = r % 2
                a.wait_ge(tile_turned, t + (m * SLOTS + 1))
                a.activation(hTm[:, par, :], ps[:, 6, 0:P], ACT.Identity, bias=gcol[:, 3:4],
                             scale=gcol[:, 2:3]).then_inc(tile_in, 1)
                copy_tile(t + 1, 1 - par)
                for fb in range(FB):
                    a.wait_ge(up_ready, t * FB + (cnt["up"] + fb + 1))
                    a.activation(mid_e[:, par, fb, :], ps[:, fb, 0:P], ACT.Relu,
                                 bias=we[:, r, 2 * F + fb:2 * F + fb + 1]).then_inc(relu_done, 1)

            over_tiles(a, one_tile, lambda: a.wait_ge(xs_loaded[1], 16 * (m + 1)))

        ROUTE = 16

        def scale_biases(v, c0, c1):
            v.tensor_copy(bcols[:, c0 + 1:c1:2], bcol[:, c0 + 1:c1:2]).then_inc(set_dve, 1)
            v.tensor_scalar(bcols[:, c0:c1:2], bcol[:, c0:c1:2], SCALE, None, ALU.mult).then_inc(set_dve, 1)

        def stacking_order(v, j, src):
            v.tensor_copy(wperm[:, j, :].rearrange("p (s e t) -> p s e t", s=2, e=DH),
                          src.rearrange("p (t s e) -> p s e t", s=2, e=DH)).then_inc(set_dve, 1)

        def late_setup_dve(v, cnt):
            bn = cnt["bank"]

            def leave(dst, src=shared):
                nonlocal bn
                v.wait_ge(bank_full, bn + 1)
                v.tensor_copy(dst, src).then_inc(bank_free, 1)
                bn += 1

            v.wait_ge(w_rest, 16 * len(rest))
            scale_biases(v, 2, 6)
            leave(wT[:, :, :].rearrange("p a c -> p (a c)"))
            v.wait_ge(bank_free, bn)
            for j, src in enumerate((wraw[:, 4, :], wraw[:, 5, :], wT[:, 0, :], wT[:, 1, :])):
                stacking_order(v, 2 + j, src)
            leave(wiT[:, :])
            leave(wo2[:, :, :].rearrange("p a c -> p (a c)"))
            for kx in range(TOPK):
                leave(loBT[:, kx, :], shared[0:RANK, :])
            for kx in range(TOPK):
                v.wait_ge(bank_full, bn + 1)
                v.tensor_tensor(wk[:, kx, :], shared, wiT[:, :], ALU.add).then_inc(bank_free, 1)
                bn += 1
            v.wait_ge(bank_free, bn)
            assert bn == cnt["bank"] + SETUP_BANK

        def late_setup_pe(pe, cnt):
            bn = cnt["bank"]

            def flip(pairs):
                nonlocal bn
                wait(pe, bank_free, bn)
                for dst, src in pairs:
                    ins = pe.transpose(dst, src, identf[:, :])
                ins.then_inc(bank_full, 1)
                bn += 1

            pe.wait_ge(w_rest, 16 * len(rest))
            flip([(shared_t[:, i, :], wraw[:, 8 + i, :]) for i in range(4)])
            pe.wait_ge(ffn_loaded, 16 * 2)
            flip([(shared_t[:, i, :], wi_raw[:, i, :]) for i in range(FB)])
            flip([(shared_t[:, i, :], wo_raw[:, i * P:(i + 1) * P]) for i in range(FB)])
            pe.wait_ge(lora_loaded, 16 * 2 * TOPK)
            for kx in range(TOPK):
                flip([(shared_t[0:RANK, i, :], loB[:, kx, i, :]) for i in range(FB)])
            for kx in range(TOPK):
                wait(pe, bank_free, bn)
                pe.matmul(shared, loA[:, kx, :], loBT[:, kx, :], start=True, stop=True).then_inc(bank_full, 1)
                bn += 1

        def moe_dve(v, cnt):
            m = cnt["moe"]
            steps = [m * ROUTE]

            def step(ins):
                ins.then_inc(route, 1)
                steps[0] += 1
                v.wait_ge(route, steps[0])

            def over_e(t):
                return t[:, :].rearrange("p (i o) -> p i o", o=1).broadcast_to([P, TILES, E])

            ln_everything(v, cnt, res)
            if m == 0:
                v.wait_ge(w_rest, 16 * len(rest))
            v.wait_ge(logits_ready, m + 1)
            step(v.tensor_tensor(logit[:, :, :], ps[:, 0, 0:TILES * E].rearrange("p (i e) -> p i e", e=E),
                                 gbb[:, :].rearrange("p (o e) -> p o e", o=1).broadcast_to([P, TILES, E]), ALU.add))
            step(v.tensor_reduce(lmax[:, :], logit[:, :, :], AX, ALU.max))
            step(v.tensor_tensor(score[:, :, :], logit[:, :, :], over_e(lmax), ALU.is_equal))
            step(v.tensor_tensor(score[:, :, :], score[:, :, :], pref[:, :, :], ALU.mult))
            step(v.tensor_reduce(smax[:, :], score[:, :, :], AX, ALU.max))
            step(v.tensor_tensor(ohb[:, :, :], score[:, :, :], over_e(smax), ALU.is_equal))
            assert steps[0] == m * ROUTE + 6
            v.wait_ge(rank_ready, m + 1)
            total = ps[:, 1, TILES * E:(TILES + 1) * E]
            step(v.scalar_tensor_tensor(more[:, :, :],
                                        total.rearrange("p (e o) -> p e o", o=1).broadcast_to([P, E, TILES]), 1.0 / P,
                                        count[:, 0:TILES].rearrange("p (o k) -> p o k", o=1)
                                        .broadcast_to([P, E, TILES]), ALU.mult, ALU.is_gt))
            step(v.tensor_reduce(ntile[:, :], more[:, :, :], AX, ALU.add))
            step(v.tensor_tensor(more[:, :, 0:E], lower_e[:, :, :],
                                 ntile[:, :].rearrange("p (o e) -> p o e", o=1).broadcast_to([P, E, E]), ALU.mult))
            step(v.tensor_reduce(first[:, :], more[:, :, 0:E], AX, ALU.add))
            step(v.scalar_tensor_tensor(score[:, :, :],
                                        first[:, :].rearrange("p (o e) -> p o e", o=1).broadcast_to([P, TILES, E]),
                                        float(P), ps[:, 1, 0:TILES * E].rearrange("p (i e) -> p i e", e=E),
                                        ALU.mult, ALU.add))
            step(v.tensor_tensor(logit[:, :, :], score[:, :, :], ohb[:, :, :], ALU.mult))
            step(v.tensor_reduce(posf[:, :], logit[:, :, :], AX, ALU.add))
            step(v.tensor_copy(pos[:, :], posf[:, :]))
            v.tensor_tensor(last_e[:, :], first[:, :], ntile[:, :], ALU.add).then_inc(route, 1)
            v.wait_ge(route, m * ROUTE + 15)
            v.tensor_tensor(owner_c[:, :, :], count[0:1, :].rearrange("p (t o) -> p t o", o=1)
                            .broadcast_to([1, SLOTS + AHEAD, E - 1]),
                            last_e[0:1, 0:E - 1].rearrange("p (o e) -> p o e", o=1)
                            .broadcast_to([1, SLOTS + AHEAD, E - 1]),
                            ALU.is_ge).then_inc(owner_step, 1)
            v.wait_ge(owner_step, m * 3 + 1)
            v.tensor_reduce(ownerf[:, :], owner_c[:, :, :], AX, ALU.add).then_inc(owner_step, 1)
            v.wait_ge(owner_step, m * 3 + 2)
            v.tensor_copy(owner[:, :], ownerf[:, :]).then_inc(owner_step, 1)
            v.scalar_tensor_tensor(x[:, 0:TILES, :], res[:, 0:TILES, :], 0.5, x[:, 0:TILES, :], ALU.mult,
                                   ALU.add).then_inc(route, 1)
            v.wait_ge(owner_step, m * 3 + 3)

            def lay_out(t, r):
                e = v.value_load(owner[0:1, bass.ds(t, 1)], min_val=0, max_val=E - 1)
                v.tensor_copy(we[:, r, :], experts[:, bass.ds(e, 1), :]
                              .rearrange("p o c -> p (o c)")).then_inc(expert_ready, 1)

            def output_before(t, r, half):
                par = r % 2
                v.wait_ge(tile_down, t + (m * SLOTS + ONE))
                wait(v, y_sent[par], half * 16 + (m * ((SLOTS + 1 - par) // 2) * 16))
                v.tensor_copy(numbers_y[:, par:par + 1],
                              xs[:, bass.ds(t - 1, 1), P:ROW].bitcast(U32).rearrange("p o c -> p (o c)"))
                v.tensor_tensor(ysb[:, par, :], ps[:, 4 + par, 0:P], we[:, r, 2 * F + FB:WE],
                                ALU.add).then_inc(y_ready, 1)

            def one_tile(t, r, half):
                wait(v, y_ready, t + (m * SLOTS - 1 + ONE))
                lay_out(t + AHEAD, (r + AHEAD) % 4)
                if not isinstance(t, int) or t > 0:
                    output_before(t, (r - 1) % 4, half - 1 + r % 2)

            if m == 0:
                late_setup_dve(v, cnt)
            v.wait_ge(xs_loaded[0], 16 * (m + 1))
            for t in range(AHEAD):
                lay_out(t, t)
            over_tiles(v, one_tile, lambda: v.wait_ge(xs_loaded[1], 16 * (m + 1)))
            output_before(SLOTS, (SLOTS - 1) % 4, (SLOTS - 1) // 2)
            v.wait_ge(route, (m + 1) * ROUTE)
            for b in range(NB):
                v.wait_ge(y_loaded[b], 16 * (m + 1))
                v.scalar_tensor_tensor(tiles(x, b), tiles(yall, b), 0.5, tiles(x, b), ALU.mult,
                                       ALU.add).then_inc(x_done, 1)
            v.wait_ge(x_done, cnt["xd"] + NB)

        def moe_pool(g_, cnt):
            m = cnt["moe"]
            for half in range(2):
                ln_pool(g_, cnt["ln"] + 2 * half, False, 2, 2 * half)
            g_.tensor_copy(lnall[:, :, P:ROW].bitcast(U32).rearrange("p a o -> p (a o)"),
                           numbers_t[:, :]).then_inc(numbered, 1)
            g_.wait_ge(numbered, m + 1)
            g_.wait_ge(route, m * ROUTE + 14)
            g_.wait_ge(prefilled, 2 * (len(PAD_AT) + 1) * 16)
            for j in range(TILES):
                g_.indirect_dma_start(d["sorted"][m], bass.IndirectOffsetOnAxis(pos[:, j:j + 1], 0), lnall[:, j, :],
                                      None).then_inc(rows_sorted, 16)

            def one_tile(t, r, _):
                par = r % 2
                apart(g_, y_ready, t + (m * SLOTS + 1 + ONE))
                g_.indirect_dma_start(d["y_rows"][m], bass.IndirectOffsetOnAxis(numbers_y[:, par:par + 1], 0),
                                      ysb[:, par, :], None).then_inc(y_sent[par], 16)

            over_tiles(g_, one_tile)

        def moe_sync(sp, cnt):
            m = cnt["moe"]
            if m == 0:
                sp.wait_ge(logits_ready, 1)
                sp.dma_start(wi_raw[:, :, :], d["L1_ffn_wi_w"].rearrange("(a p) h -> p a h", p=P))\
                    .then_inc(ffn_loaded, 16)
                sp.dma_start(wo_raw[:, :], d["L1_ffn_wo_w"]).then_inc(ffn_loaded, 16)
                sp.wait_ge(idx_loaded, 16)
                for kx in range(TOPK):
                    which = sp.value_load(idx[0:1, kx:kx + 1], min_val=0, max_val=E - 1)
                    sp.dma_start(loA[:, kx, :], d["L1_ffn_lora_As"][bass.ds(which, 1), :, :]
                                 .rearrange("o r h -> (o r) h")).then_inc(lora_loaded, 16)
                    sp.dma_start(loB[:, kx, :, :], d["L1_ffn_lora_Bs"][bass.ds(which, 1), :, :]
                                 .rearrange("o (a p) r -> p (o a) r", p=P)).then_inc(lora_loaded, 16)
            sp.wait_ge(rows_sorted, (m + 1) * TILES * 16)
            rows = d["sorted"][m].rearrange("(t p) c -> p t c", p=P)
            sp.dma_start(xs[:, 0:4, :], rows[:, 0:4, :]).then_inc(xs_loaded[0], 16)
            sp.dma_start(xs[:, 4:SLOTS, :], rows[:, 4:SLOTS, :]).then_inc(xs_loaded[1], 16)
            for par in range(2):
                sp.wait_ge(y_sent[par], (m + 1) * ((SLOTS + 1 - par) // 2) * 16)
            for b in range(NB):
                sp.dma_start(tiles(yall, b), d["y_rows"][m][b * S:(b + 1) * S, :]
                             .rearrange("(t p) c -> p t c", p=P)).then_inc(y_loaded[b], 16)

        def ffn_pe(pe, cnt):
            turn_everything(pe, cnt)
            pe.wait_ge(hta_done, cnt["tr"] + NB)

            def down(b, n):
                m0 = b * FB + cnt["mid"]
                if n == 0:
                    wait(pe, y_free, b + cnt["y"])
                pe.wait_ge(mid_done, m0 + n + 1)
                for i in range(TB):
                    ins = pe.matmul(ps[:, 6, i * P:(i + 1) * P], mid[:, n, i * P:(i + 1) * P], wo2[:, n, :],
                                    start=(n == 0 and i == 0), stop=(n == FB - 1), skip_group_check=True)
                ins.then_inc(down_done, 1)

            def one_batch(b, before):
                for n in range(FB):
                    for kx in range(TOPK):
                        if kx == 0:
                            wait(pe, relu_done, b * FB + (cnt["relu"] + n - 1))
                        else:
                            wait(pe, fold_done, b * FB + (cnt["fold"] + n - 1))
                        pe.matmul(ps[:, (2 * n + kx) % 4, :], wk[:, kx, n * P:(n + 1) * P], hTa[:, b, :], start=True,
                                  stop=True).then_inc(up_ready, 1)
                    if n >= 1:
                        down(b, n - 1)
                    elif before is not None:
                        down(before, FB - 1)

            one_batch(0, None)
            with pe.Fori(0, NB - 1) as i:
                one_batch(i + 1, i)
            down(NB - 1, FB - 1)

        def ffn_act(a, cnt):
            for b in range(NB):
                a.wait_ge(ln_turned, cnt["tr"] + b + 1)
                a.activation(hTa[:, b, :], ps[:, 4 + b, :], ACT.Copy).then_inc(hta_done, 1)
            def one_batch(b):
                for n in range(FB):
                    a.wait_ge(up_ready, b * (FB * TOPK) + (cnt["up"] + 2 * n + 1))
                    wait(a, mid_done, b * FB + (cnt["mid"] + n - 1))
                    a.activation(relu[:, n % 2, :], ps[:, (2 * n) % 4, :], ACT.Relu).then_inc(relu_done, 1)

            one_batch(0)
            with a.Fori(0, NB - 1) as i:
                one_batch(i + 1)

        def ffn_dve(v, cnt):
            ln_everything(v, cnt, x)
            def output(b):
                v.wait_ge(down_done, b * FB + (cnt["mid"] + FB))
                v.scalar_tensor_tensor(tiles(x, b), ps[:, 6, :].rearrange("p (i c) -> p i c", c=P), 0.5, tiles(x, b),
                                       ALU.mult, ALU.add).then_inc(y_free, 1)
                v.wait_ge(y_free, b + (cnt["y"] + 1))
                v.sem_inc(x_done, 1)

            def one_batch(b, before):
                for n in range(FB):
                    v.wait_ge(up_ready, b * (FB * TOPK) + (cnt["up"] + 2 * n + 2))
                    wait(v, mid_done, b * FB + (cnt["mid"] + n - 1))
                    v.tensor_scalar(fold[:, n % 2, :], ps[:, (2 * n + 1) % 4, :], 0.0, tkv[:, 1:2], ALU.max,
                                    ALU.mult).then_inc(fold_done, 1)
                    v.wait_ge(fold_done, b * FB + (cnt["fold"] + n + 1))
                    v.wait_ge(relu_done, b * FB + (cnt["relu"] + n + 1))
                    wait(v, down_done, b * FB + (cnt["mid"] + n + 1 - FB))
                    v.scalar_tensor_tensor(mid[:, n, :], relu[:, n % 2, :], tkv[:, 0:1], fold[:, n % 2, :], ALU.mult,
                                           ALU.add).then_inc(mid_done, 1)
                    if n == 0 and before is not None:
                        output(before)

            one_batch(0, None)
            with v.Fori(0, NB - 1) as i:
                one_batch(i + 1, i)
            output(NB - 1)

        def ffn_pool(g_, cnt):
            for half in range(2):
                ln_pool(g_, cnt["ln"] + 2 * half, False, 2, 2 * half)

        wl, rest = [], []
        b_in = d["L1_attn_b_in"]

        def weight(j, n):
            return wraw[:, j, :], d[n]

        def projection_bias(c_, v_):
            o = v_.rearrange("(t s e) -> s e t", s=2, e=DH)
            return [(bcol[64 * s:64 * s + 64, c_:c_ + 1], o[s]) for s in range(2)]

        wl += [weight(0, "L0_ffn_wq")] + projection_bias(0, d["L0_ffn_bq"])
        wl += [weight(1, "L0_ffn_wk")] + projection_bias(1, d["L0_ffn_bk"])
        wl += [weight(2, "L0_ffn_wv"), weight(3, "L0_ffn_wo")]
        for j, n in enumerate(("L0_attn_W_q", "L0_attn_W_k", "L0_attn_W_v", "L0_attn_W_o")):
            rest.append(weight(4 + j, n))
        rest.append((wraw[:, 8:11, :], d["L1_attn_w_in"].rearrange("(a p) d -> p a d", p=P)))
        rest.append((wraw[:, 11, :], d["L1_attn_w_out"]))
        for c_, v_ in enumerate((d["L0_attn_b_q"], d["L0_attn_b_k"], b_in[0:P], b_in[P:2 * P])):
            rest += projection_bias(2 + c_, v_)
        for j, v_ in enumerate((d["L0_ffn_bv"], d["L0_attn_b_v"], b_in[2 * P:3 * P])):
            (rest if j else wl).append((bvb[:, j, :], v_.partition_broadcast(P)))
        for j, v_ in enumerate((d["L0_ffn_bo"], d["L0_attn_b_o"], d["L1_attn_b_out"])):
            (rest if j else wl).append((bob[:, j, :], v_.partition_broadcast(P)))
        for j, n in enumerate(("L0_ffn_ln1_g", "L0_ffn_ln1_b", "L0_ffn_ln2_g", "L0_ffn_ln2_b")):
            (rest if j > 1 else wl).append((gcol[:, j:j + 1], d[n].rearrange("(p o) -> p o", o=1)))
        rest += [
            *[(experts[:, e, 0:F], d["L0_ffn_w1"][e]) for e in range(E)],
            *[(experts[:, e, F:2 * F].rearrange("p (a h) -> p a h", h=P),
               d["L0_ffn_w2"][e].rearrange("(a p) h -> p a h", p=P)) for e in range(E)],
            *[(experts[:, :, 2 * F + a:2 * F + a + 1],
               d["L0_ffn_b1"][:, a * P:(a + 1) * P].rearrange("e (p o) -> p e o", o=1))
              for a in range(FB)],
            (experts[:, :, 2 * F + FB:WE], d["L0_ffn_b2"].partition_broadcast(P)),
            (gw[:, :], d["L0_ffn_gate_w"]),
            (gbb[:, :], d["L0_ffn_gate_b"].partition_broadcast(P)),
            (tkv[:, :], d["L1_ffn_top_k_values"].partition_broadcast(P)),
        ]
        NFIRST = 13

        @block.sync
        def _(sp):
            x_tiles = d["L0_attn_x"].rearrange("b (i p) d -> p (b i) d", p=P)
            sp.dma_start(x[:, 0:TB, :], x_tiles[:, 0:TB, :]).then_inc(x_loaded, 16)
            for dst, src in wl:
                sp.dma_start(dst, src, allow_slow_non_contiguous=True).then_inc(w_loaded, 16)
            sp.dma_start(x[:, TB:TB * NB, :], x_tiles[:, TB:, :]).then_inc(x_rest, 16)
            sp.wait_ge(const_first, NFIRST + 1)
            sp.wait_ge(cleared, 1)
            for kind, w, cnt in phases:
                if kind == "attn":
                    attention_sync(sp, cnt, cnt["attn"] == 0)
                elif kind == "moe":
                    moe_sync(sp, cnt)
            last = phases[-1][2]
            out_t = d["out"].rearrange("b (i p) h -> b p i h", p=P)
            for b in range(NB):
                sp.wait_ge(x_done, last["xd"] + b + 1)
                sp.dma_start(out_t[b], tiles(x, b)).then_inc(out_done, 16)
            sp.wait_ge(out_done, 16 * NB)
            sp.wait_ge(qk_loaded, c["prep"] * STACKED)
            sp.wait_ge(m_loaded, c["quad"] * 32)

        @block.gpsimd
        def _(g_):
            done = [0]

            for s in credited:
                g_.sem_inc(s, ONE)

            def const(ins):
                done[0] += 1
                ins.then_inc(const_first, 1)

            const(g_.memset(minus_half[:, :], -0.5))
            const(g_.memset(identf[:, :], 0.0))
            const(g_.memset(identb[:, :], 0.0))
            const(g_.memset(mask_q[:, :], 0.0))
            const(g_.memset(mask_k[:, :], 0.0))
            const(g_.memset(va[0][:, :, :, :], 0.0))
            g_.wait_ge(const_first, done[0])
            const(g_.affine_select(out=identf[:, :], in_=identf[:, :], compare_op=ALU.not_equal, fill=1.0, base=0,
                                   pattern=[[-1, P]], channel_multiplier=1))
            const(g_.affine_select(out=identb[:, :], in_=identb[:, :], compare_op=ALU.not_equal, fill=1.0, base=0,
                                   pattern=[[-1, P]], channel_multiplier=1))
            const(g_.affine_select(out=mask_q[:, :], in_=mask_q[:, :], compare_op=ALU.is_ge, fill=MASKED, base=0,
                                   pattern=[[-1, P]], channel_multiplier=1))
            const(g_.affine_select(out=mask_k[:, :], in_=mask_k[:, :], compare_op=ALU.is_ge, fill=MASKED, base=0,
                                   pattern=[[1, P]], channel_multiplier=-1))
            const(g_.memset(va[0][:, :, :, DH:DH + 1], 1.0))
            const(g_.memset(ones_col[:, :], 1.0))
            const(g_.memset(zero_col[:, :], 0.0))
            assert done[0] == NFIRST
            g_.wait_ge(const_first, NFIRST)
            for kind, w, cnt in phases:
                if kind == "attn":
                    attention_pool(g_, W[w], cnt)
                elif kind == "moe":
                    moe_pool(g_, cnt)
                else:
                    ffn_pool(g_, cnt)

        @block.vector
        def _(v):
            clear_q(v, 0)
            v.wait_ge(x_loaded, 16)
            for kind, w, cnt in phases:
                if kind == "attn":
                    attention_dve(v, W[w], cnt)
                elif kind == "moe":
                    moe_dve(v, cnt)
                else:
                    ffn_dve(v, cnt)

        SET_DVE = 2 + 2

        @block.scalar
        def _(a):
            a.wait_ge(const_first, NFIRST)
            a.wait_ge(w_loaded, 16 * len(wl))
            a.wait_ge(set_dve, SET_DVE)
            for kind, w, cnt in phases:
                if kind == "attn":
                    attention_act(a, W[w], cnt)
                elif kind == "moe":
                    moe_act(a, cnt)
                else:
                    ffn_act(a, cnt)

        @block.tensor
        def _(pe):
            pe.wait_ge(const_first, NFIRST)
            pe.wait_ge(w_loaded, 16 * len(wl))
            pe.wait_ge(set_dve, SET_DVE)
            for kind, w, cnt in phases:
                if kind == "attn":
                    attention_pe(pe, W[w], cnt)
                elif kind == "moe":
                    moe_pe(pe, cnt)
                else:
                    ffn_pe(pe, cnt)


NAMES = ["L0_attn_x", "L0_attn_W_q", "L0_attn_b_q", "L0_attn_W_k", "L0_attn_b_k", "L0_attn_W_v", "L0_attn_b_v",
         "L0_attn_W_o", "L0_attn_b_o", "L0_ffn_ln1_g", "L0_ffn_ln1_b", "L0_ffn_ln2_g", "L0_ffn_ln2_b", "L0_ffn_wq",
         "L0_ffn_bq", "L0_ffn_wk", "L0_ffn_bk", "L0_ffn_wv", "L0_ffn_bv", "L0_ffn_wo", "L0_ffn_bo", "L0_ffn_gate_w",
         "L0_ffn_gate_b", "L0_ffn_w1", "L0_ffn_b1", "L0_ffn_w2", "L0_ffn_b2", "L1_attn_w_in", "L1_attn_b_in",
         "L1_attn_w_out", "L1_attn_b_out", "L1_ffn_wi_w", "L1_ffn_wo_w", "L1_ffn_lora_As", "L1_ffn_lora_Bs",
         "L1_ffn_top_k_indices", "L1_ffn_top_k_values"]


def kernel(**inputs):
    import concourse.bacc as bacc
    import numpy as np
    from concourse.bass_utils import run_bass_kernel_spmd

    nc = bacc.Bacc("TRN2", target_bir_lowering=False, num_devices=1)
    arrays, d = {}, {}
    for name in NAMES:
        a = np.ascontiguousarray(inputs[name])
        arrays[f"in_{name}"] = a
        d[name] = nc.dram_tensor(f"in_{name}", a.shape, mybir.dt.from_np(a.dtype), kind="ExternalInput").ap()
    shape = inputs["L0_attn_x"].shape
    for name, rows, cols in (("sorted", SLOTS * P, ROW), ("y_rows", (TILES + SLOTS) * P, P)):
        d[name] = [nc.dram_tensor(f"{name}{m}", (rows, cols), F32, kind="Internal").ap() for m in range(2)]
    d["out"] = nc.dram_tensor("out_dram", shape, F32, kind="ExternalOutput").ap()
    program(nc, d)
    return run_bass_kernel_spmd(nc, [arrays], core_ids=[0]).results[0]["out_dram"]
```
